# Optimizing a Trainium2 kernel written in Bass

```python
import numpy as np
import jax
import jax.numpy as jnp

def _softmax(x, axis=-1):
    return jax.nn.softmax(x, axis=axis)

def _gelu(x):
    return jax.nn.gelu(x, approximate=True)

def _silu(x):
    return jax.nn.silu(x)

def _sigmoid(x):
    return jax.nn.sigmoid(x)

def _layernorm(x, axis=-1, eps=1e-05):
    m = jnp.mean(x, axis=axis, keepdims=True)
    v = jnp.var(x, axis=axis, keepdims=True)
    return (x - m) / jnp.sqrt(v + eps)

def _scatter_add(tgt, idx, src, axis=0):
    return tgt.at[idx].add(src)

def _segment_sum(src, seg, n):
    return jax.ops.segment_sum(src, seg, n)
kernel_name = 'mk_recurrent_d2_jaxref_r8_cbe195'

def setup_inputs(seed: int=0):
    np.random.seed(seed)
    _w = jnp.asarray

    def _L0_attn_setup():
        import jax, jax.numpy as jnp
        import numpy as np
        H, P, N, G, K, CS = (64, 64, 128, 8, 4, 32)
        EMB = 256
        INTER = H * P
        CONV_DIM = INTER + 2 * G * N
        PROJ = INTER + CONV_DIM + H
        EPS = 1e-06

        def _segsum(x):
            L = x.shape[-1]
            lo = jnp.tril(jnp.ones((L, L), bool), -1)
            cum = jnp.cumsum(jnp.where(lo, x[..., None], 0.0), axis=-2)
            return jnp.where(jnp.tril(jnp.ones((L, L), bool)), cum, -jnp.inf)

        def _ssd(input_states, in_proj_w, conv_w, conv_b, dt_bias, A_log, D, norm_w, out_proj_w):
            b, s, _ = input_states.shape
            proj = input_states @ in_proj_w.T
            gate = proj[..., :INTER]
            h_BC = proj[..., INTER:INTER + CONV_DIM]
            dt = proj[..., INTER + CONV_DIM:]
            xc = jnp.transpose(h_BC, (0, 2, 1))
            yc = jax.lax.conv_general_dilated(xc, conv_w, (1,), [(K - 1, 0)], feature_group_count=CONV_DIM, dimension_numbers=('NCH', 'OIH', 'NCH'))
            h_BC = jax.nn.silu(jnp.transpose(yc + conv_b[None, :, None], (0, 2, 1)))
            hidden = h_BC[..., :INTER]
            Bx = h_BC[..., INTER:INTER + G * N]
            Cx = h_BC[..., INTER + G * N:]
            A = -jnp.exp(A_log)
            dt2 = jax.nn.softplus(dt + dt_bias)
            hid = hidden.reshape(b, s, H, P)
            pad = (CS - s % CS) % CS
            total = s + pad
            n_c = total // CS

            def padseq(t):
                return jnp.pad(t, [(0, 0), (0, pad)] + [(0, 0)] * (t.ndim - 2))
            D_res = padseq(hid) * D[None, None, :, None]
            hid_c = padseq(hid * dt2[..., None]).reshape(b, n_c, CS, H, P)
            rep = H // G
            B_c = padseq(jnp.tile(Bx.reshape(b, s, G, N), (1, 1, rep, 1))).reshape(b, n_c, CS, H, N)
            C_c = padseq(jnp.tile(Cx.reshape(b, s, G, N), (1, 1, rep, 1))).reshape(b, n_c, CS, H, N)
            A_c = jnp.transpose(padseq(A * dt2).reshape(b, n_c, CS, H), (0, 3, 1, 2))
            A_cum = jnp.cumsum(A_c, axis=-1)
            L = jnp.exp(_segsum(A_c))
            Gm = jnp.einsum('bcihn,bcjhn->bcijh', C_c, B_c)
            M = Gm * jnp.transpose(L, (0, 2, 3, 4, 1))
            Yd = jnp.einsum('bcijh,bcjhp->bcihp', M, hid_c)
            decay = jnp.exp(A_cum[..., -1:] - A_cum)
            B_dec = B_c * jnp.transpose(decay, (0, 2, 3, 1))[..., None]
            state = jnp.einsum('bclhn,bclhp->bchpn', B_dec, hid_c)
            Sd_out = jnp.exp(A_cum)
            Yoff = jnp.einsum('bclhn,bchpn->bclhp', C_c, state) * jnp.transpose(Sd_out, (0, 2, 3, 1))[..., None]
            y = (Yd + Yoff + D_res.reshape(b, n_c, CS, H, P)).reshape(b, total, H, P)[:, :s]
            y = y.reshape(b, s, INTER)
            yg = y * jax.nn.silu(gate)
            var = jnp.mean(yg * yg, axis=-1, keepdims=True)
            normed = norm_w * (yg * jax.lax.rsqrt(var + EPS))
            return normed @ out_proj_w.T
        key = jax.random.key(seed)
        ks = jax.random.split(key, 4)
        return {'input_states': jax.random.normal(ks[0], (1, 512, EMB), jnp.float32), 'in_proj_w': jax.random.normal(ks[1], (PROJ, EMB), jnp.float32) * 0.02, 'conv_w': jax.random.normal(ks[2], (CONV_DIM, 1, K), jnp.float32) * 0.1, 'conv_b': jnp.zeros((CONV_DIM,), jnp.float32), 'dt_bias': jnp.ones((H,), jnp.float32), 'A_log': jnp.log(jnp.arange(1, H + 1, dtype=jnp.float32)), 'D': jnp.ones((H,), jnp.float32), 'norm_w': jnp.ones((INTER,), jnp.float32), 'out_proj_w': jax.random.normal(ks[3], (EMB, INTER), jnp.float32) * 0.02}
    _L0_attn_in = _L0_attn_setup()

    def _L0_ffn_setup():
        import jax, jax.numpy as jnp
        import numpy as np
        TOPK = 2
        key = jax.random.key(seed)
        ks = jax.random.split(key, 6)
        B, T, H, S, r, ad = (2, 512, 256, 32, 16, 32)
        h = jax.random.normal(ks[0], (B, T, H), dtype=jnp.float32)
        Wr = jax.random.normal(ks[1], (S, H), dtype=jnp.float32) * 0.02
        U = jax.random.normal(ks[2], (S, H, r), dtype=jnp.float32) * 0.02
        V = jax.random.normal(ks[3], (S, r, H), dtype=jnp.float32) * 0.02
        attr = jax.random.normal(ks[4], (S, ad), dtype=jnp.float32) * 0.02
        Wa = jax.random.normal(ks[5], (1, ad), dtype=jnp.float32) * 0.02
        return {'h': h, 'Wr': Wr, 'U': U, 'V': V, 'attr': attr, 'Wa': Wa}
    _L0_ffn_in = _L0_ffn_setup()

    def _L1_attn_setup():
        import jax, jax.numpy as jnp
        import numpy as np
        D_MODEL = 256
        NUM_HEADS = 16
        HEAD_DIM = D_MODEL // NUM_HEADS
        B, T = (4, 256)
        key = jax.random.key(seed)
        ks = jax.random.split(key, 9)
        s = 1.0 / np.sqrt(D_MODEL)
        inp = {'x': jax.random.normal(ks[0], (B, T, D_MODEL), dtype=jnp.float32)}
        for i, name in enumerate(['q', 'k', 'v', 'o']):
            inp[f'W{name}'] = jax.random.uniform(ks[1 + 2 * i], (D_MODEL, D_MODEL), minval=-s, maxval=s, dtype=jnp.float32)
            inp[f'b{name}'] = jax.random.uniform(ks[2 + 2 * i], (D_MODEL,), minval=-s, maxval=s, dtype=jnp.float32)
        return inp
    _L1_attn_in = _L1_attn_setup()

    def _L1_ffn_setup():
        import jax, jax.numpy as jnp
        import numpy as np

        def _sparsify_2to4(h):
            B, S, I = h.shape
            g = h.reshape(B, S, I // 4, 4)
            a = jnp.abs(g)
            _, idx = jax.lax.top_k(a, 2)
            pos = jnp.arange(4)
            mask = (pos == idx[..., 0:1]) | (pos == idx[..., 1:2])
            return (g * mask.astype(g.dtype)).reshape(B, S, I)
        key = jax.random.key(seed)
        k1, k2, k3, k4 = jax.random.split(key, 4)
        B, S, H, I = (4, 256, 256, 1024)
        x = jax.random.normal(k1, (B, S, H), dtype=jnp.float32)
        w_gate = jax.random.normal(k2, (H, I), dtype=jnp.float32) / np.sqrt(H)
        w_up = jax.random.normal(k3, (H, I), dtype=jnp.float32) / np.sqrt(H)
        w_down = jax.random.normal(k4, (I, H), dtype=jnp.float32) / np.sqrt(I)
        return {'x': x, 'w_gate': w_gate, 'w_up': w_up, 'w_down': w_down}
    _L1_ffn_in = _L1_ffn_setup()
    _d = {'L0_attn_input_states': _L0_attn_in['input_states'], 'L0_attn_in_proj_w': _L0_attn_in['in_proj_w'], 'L0_attn_conv_w': _L0_attn_in['conv_w'], 'L0_attn_conv_b': _L0_attn_in['conv_b'], 'L0_attn_dt_bias': _L0_attn_in['dt_bias'], 'L0_attn_A_log': _L0_attn_in['A_log'], 'L0_attn_D': _L0_attn_in['D'], 'L0_attn_norm_w': _L0_attn_in['norm_w'], 'L0_attn_out_proj_w': _L0_attn_in['out_proj_w'], 'L0_ffn_Wr': _L0_ffn_in['Wr'], 'L0_ffn_U': _L0_ffn_in['U'], 'L0_ffn_V': _L0_ffn_in['V'], 'L0_ffn_attr': _L0_ffn_in['attr'], 'L0_ffn_Wa': _L0_ffn_in['Wa'], 'L1_attn_Wq': _L1_attn_in['Wq'], 'L1_attn_bq': _L1_attn_in['bq'], 'L1_attn_Wk': _L1_attn_in['Wk'], 'L1_attn_bk': _L1_attn_in['bk'], 'L1_attn_Wv': _L1_attn_in['Wv'], 'L1_attn_bv': _L1_attn_in['bv'], 'L1_attn_Wo': _L1_attn_in['Wo'], 'L1_attn_bo': _L1_attn_in['bo'], 'L1_ffn_w_gate': _L1_ffn_in['w_gate'], 'L1_ffn_w_up': _L1_ffn_in['w_up'], 'L1_ffn_w_down': _L1_ffn_in['w_down']}
    _x0 = _d['L0_attn_input_states']
    _d['L0_attn_input_states'] = jax.random.normal(jax.random.fold_in(jax.random.key(seed), 1), (4, 256, 256), dtype=_x0.dtype)
    del _x0
    return _d

def reference(L0_attn_input_states, L0_attn_in_proj_w, L0_attn_conv_w, L0_attn_conv_b, L0_attn_dt_bias, L0_attn_A_log, L0_attn_D, L0_attn_norm_w, L0_attn_out_proj_w, L0_ffn_Wr, L0_ffn_U, L0_ffn_V, L0_ffn_attr, L0_ffn_Wa, L1_attn_Wq, L1_attn_bq, L1_attn_Wk, L1_attn_bk, L1_attn_Wv, L1_attn_bv, L1_attn_Wo, L1_attn_bo, L1_ffn_w_gate, L1_ffn_w_up, L1_ffn_w_down):

    def _L0_attn_ref(input_states, in_proj_w, conv_w, conv_b, dt_bias, A_log, D, norm_w, out_proj_w):
        import jax, jax.numpy as jnp
        import numpy as np
        H, P, N, G, K, CS = (64, 64, 128, 8, 4, 32)
        EMB = 256
        INTER = H * P
        CONV_DIM = INTER + 2 * G * N
        PROJ = INTER + CONV_DIM + H
        EPS = 1e-06

        def _segsum(x):
            L = x.shape[-1]
            lo = jnp.tril(jnp.ones((L, L), bool), -1)
            cum = jnp.cumsum(jnp.where(lo, x[..., None], 0.0), axis=-2)
            return jnp.where(jnp.tril(jnp.ones((L, L), bool)), cum, -jnp.inf)

        def _ssd(input_states, in_proj_w, conv_w, conv_b, dt_bias, A_log, D, norm_w, out_proj_w):
            b, s, _ = input_states.shape
            proj = input_states @ in_proj_w.T
            gate = proj[..., :INTER]
            h_BC = proj[..., INTER:INTER + CONV_DIM]
            dt = proj[..., INTER + CONV_DIM:]
            xc = jnp.transpose(h_BC, (0, 2, 1))
            yc = jax.lax.conv_general_dilated(xc, conv_w, (1,), [(K - 1, 0)], feature_group_count=CONV_DIM, dimension_numbers=('NCH', 'OIH', 'NCH'))
            h_BC = jax.nn.silu(jnp.transpose(yc + conv_b[None, :, None], (0, 2, 1)))
            hidden = h_BC[..., :INTER]
            Bx = h_BC[..., INTER:INTER + G * N]
            Cx = h_BC[..., INTER + G * N:]
            A = -jnp.exp(A_log)
            dt2 = jax.nn.softplus(dt + dt_bias)
            hid = hidden.reshape(b, s, H, P)
            pad = (CS - s % CS) % CS
            total = s + pad
            n_c = total // CS

            def padseq(t):
                return jnp.pad(t, [(0, 0), (0, pad)] + [(0, 0)] * (t.ndim - 2))
            D_res = padseq(hid) * D[None, None, :, None]
            hid_c = padseq(hid * dt2[..., None]).reshape(b, n_c, CS, H, P)
            rep = H // G
            B_c = padseq(jnp.tile(Bx.reshape(b, s, G, N), (1, 1, rep, 1))).reshape(b, n_c, CS, H, N)
            C_c = padseq(jnp.tile(Cx.reshape(b, s, G, N), (1, 1, rep, 1))).reshape(b, n_c, CS, H, N)
            A_c = jnp.transpose(padseq(A * dt2).reshape(b, n_c, CS, H), (0, 3, 1, 2))
            A_cum = jnp.cumsum(A_c, axis=-1)
            L = jnp.exp(_segsum(A_c))
            Gm = jnp.einsum('bcihn,bcjhn->bcijh', C_c, B_c)
            M = Gm * jnp.transpose(L, (0, 2, 3, 4, 1))
            Yd = jnp.einsum('bcijh,bcjhp->bcihp', M, hid_c)
            decay = jnp.exp(A_cum[..., -1:] - A_cum)
            B_dec = B_c * jnp.transpose(decay, (0, 2, 3, 1))[..., None]
            state = jnp.einsum('bclhn,bclhp->bchpn', B_dec, hid_c)
            Sd_out = jnp.exp(A_cum)
            Yoff = jnp.einsum('bclhn,bchpn->bclhp', C_c, state) * jnp.transpose(Sd_out, (0, 2, 3, 1))[..., None]
            y = (Yd + Yoff + D_res.reshape(b, n_c, CS, H, P)).reshape(b, total, H, P)[:, :s]
            y = y.reshape(b, s, INTER)
            yg = y * jax.nn.silu(gate)
            var = jnp.mean(yg * yg, axis=-1, keepdims=True)
            normed = norm_w * (yg * jax.lax.rsqrt(var + EPS))
            return normed @ out_proj_w.T
        return _ssd(input_states, in_proj_w, conv_w, conv_b, dt_bias, A_log, D, norm_w, out_proj_w)

    def _L0_ffn_ref(h, Wr, U, V, attr, Wa):
        import jax, jax.numpy as jnp
        import numpy as np
        TOPK = 2
        S = Wr.shape[0]
        sc = jnp.einsum('bth,sh->bts', h, Wr)
        _, idx = jax.lax.top_k(sc, TOPK)
        m = jax.nn.one_hot(idx, S, dtype=sc.dtype).sum(axis=-2)
        g = jax.nn.softmax(sc, axis=-1) * m
        g = g / (g.sum(axis=-1, keepdims=True) + 1e-08)
        hU = jnp.einsum('bth,shr->btsr', h, U)
        out = jnp.einsum('bts,btsr,srh->bth', g, hU, V)
        aw = jax.nn.sigmoid(attr @ Wa[0])
        gate = (g @ aw)[..., None]
        return out * (0.9 + 0.2 * gate)

    def _L1_attn_ref(x, Wq, bq, Wk, bk, Wv, bv, Wo, bo):
        import jax, jax.numpy as jnp
        import numpy as np
        D_MODEL = 256
        NUM_HEADS = 16
        HEAD_DIM = D_MODEL // NUM_HEADS
        B, T = (4, 256)
        Bx, Tx, _ = x.shape
        H, Dh = (NUM_HEADS, HEAD_DIM)
        q = (x @ Wq.T + bq).reshape(Bx, Tx, H, Dh).transpose(0, 2, 1, 3)
        k = (x @ Wk.T + bk).reshape(Bx, Tx, H, Dh).transpose(0, 2, 1, 3)
        v = (x @ Wv.T + bv).reshape(Bx, Tx, H, Dh).transpose(0, 2, 1, 3)
        scale = 1.0 / np.sqrt(Dh).astype(np.float32)
        scores = jnp.einsum('bhqd,bhkd->bhqk', q, k) * scale
        attn = jax.nn.softmax(scores, axis=-1)
        out = jnp.einsum('bhqk,bhkd->bhqd', attn, v)
        out = out.transpose(0, 2, 1, 3).reshape(Bx, Tx, H * Dh)
        return out @ Wo.T + bo

    def _L1_ffn_ref(x, w_gate, w_up, w_down):
        import jax, jax.numpy as jnp
        import numpy as np

        def _sparsify_2to4(h):
            B, S, I = h.shape
            g = h.reshape(B, S, I // 4, 4)
            a = jnp.abs(g)
            _, idx = jax.lax.top_k(a, 2)
            pos = jnp.arange(4)
            mask = (pos == idx[..., 0:1]) | (pos == idx[..., 1:2])
            return (g * mask.astype(g.dtype)).reshape(B, S, I)
        h = jax.nn.silu(jnp.einsum('bsh,hi->bsi', x, w_gate)) * jnp.einsum('bsh,hi->bsi', x, w_up)
        h_sparse = _sparsify_2to4(h)
        return jnp.einsum('bsi,ih->bsh', h_sparse, w_down)
    x = L0_attn_input_states
    xn = _layernorm(x, axis=-1)
    s = _L0_attn_ref(xn, L0_attn_in_proj_w, L0_attn_conv_w, L0_attn_conv_b, L0_attn_dt_bias, L0_attn_A_log, L0_attn_D, L0_attn_norm_w, L0_attn_out_proj_w)
    g = _silu(_L0_ffn_ref(xn, L0_ffn_Wr, L0_ffn_U, L0_ffn_V, L0_ffn_attr, L0_ffn_Wa))
    x = x + s * g
    xn = _layernorm(x, axis=-1)
    s = _L1_attn_ref(xn, L1_attn_Wq, L1_attn_bq, L1_attn_Wk, L1_attn_bk, L1_attn_Wv, L1_attn_bv, L1_attn_Wo, L1_attn_bo)
    g = _silu(_L1_ffn_ref(xn, L1_ffn_w_gate, L1_ffn_w_up, L1_ffn_w_down))
    x = x + s * g
    return x

_drawn_inputs = setup_inputs


def setup_inputs(seed=0):
    import zlib

    import numpy as np

    out = dict(_drawn_inputs(seed))
    spreads = {'L0_attn_conv_b': (0.0, 0.68),
     'L0_attn_dt_bias': (1.0, 0.6),
     'L0_attn_D': (1.0, 0.6),
     'L0_attn_norm_w': (1.0, 0.6)}
    factors = {'L0_attn_in_proj_w': 4.705,
     'L0_attn_conv_w': 8.0,
     'L0_attn_A_log': 8.0,
     'L0_attn_out_proj_w': 4.657,
     'L0_ffn_Wr': 4.837,
     'L0_ffn_U': 4.661,
     'L0_ffn_V': 4.671,
     'L0_ffn_attr': 22.513,
     'L0_ffn_Wa': 8.0,
     'L1_attn_Wq': 8.0,
     'L1_attn_bq': 8.0,
     'L1_attn_Wk': 8.0,
     'L1_attn_bk': 64.0,
     'L1_attn_Wv': 7.737,
     'L1_attn_bv': 8.0,
     'L1_attn_Wo': 5.661,
     'L1_attn_bo': 21.792,
     'L1_ffn_w_gate': 4.058,
     'L1_ffn_w_up': 3.796,
     'L1_ffn_w_down': 3.793}
    for name, (base, spread) in spreads.items():
        noise = np.random.default_rng([zlib.crc32(name.encode()), seed]).standard_normal(out[name].shape)
        drawn = base * np.exp(spread * noise) if base else spread * noise
        out[name] = jnp.asarray(drawn.astype(out[name].dtype))
    for name, factor in factors.items():
        out[name] = (out[name] * factor).astype(out[name].dtype)
    return out
```

```python
from contextlib import ExitStack

import concourse.bass as bass
from concourse import mybir

F32 = mybir.dt.float32
BF16 = mybir.dt.bfloat16
U32 = mybir.dt.uint32
ALU = mybir.AluOpType
ACT = mybir.ActivationFunctionType
AX = mybir.AxisListType

P = 128
TOK, BATCH, SEQ, EMB = 1024, 4, 256, 256
TT = TOK // P
KE = EMB // P
HALF = TOK // 2
HT = HALF // P
HEADS, HD, STATE, GROUPS, TAPS, CS = 64, 64, 128, 8, 4, 32
INTER = HEADS * HD
CT = INTER // P
CONV = INTER + 2 * GROUPS * STATE
CONV_T = CONV // P
PROJ = INTER + CONV + HEADS
EXPERTS, RANK = 32, 16
AH, AD = 16, 16
FF = 1024
FT = FF // P
LN_EPS, RMS_EPS = 1e-5, 1e-6


def build(nc, t_in, out):
    ctx = ExitStack()
    with ctx:
        def sb(name, shape, dt=F32):
            return ctx.enter_context(nc.sbuf_tensor(name, shape, dt))

        def sem(name):
            return ctx.enter_context(nc.semaphore(name))

        bank = [ctx.enter_context(nc.psum_tensor(f"bank{i}", [P, 512], F32)) for i in range(8)]

        ident = sb("ident", [P, P])
        later = sb("later", [P, P])
        chunk = sb("chunk", [P, P])
        upto = sb("upto", [P, CS])
        diag = sb("diag", [P, CS])
        future = sb("future", [P, CS], BF16)
        ident_b = sb("ident_b", [P, P], BF16)
        zeros = sb("zeros", [P, 512], BF16)
        ones = sb("ones", [P, 2])
        expert_no = sb("expert_no", [P, EXPERTS])
        conv_w = sb("conv_w_sb", [P, CONV_T, TAPS])
        conv_b = sb("conv_b_sb", [P, CONV_T])
        norm_w = sb("norm_w_sb", [P, CT])
        dt_bias = sb("dt_bias_sb", [P, HEADS])
        a_row = sb("a_row", [P, HEADS])
        d_row = sb("d_row", [P, HEADS])
        w_dt = sb("w_dt", [P, KE, HEADS])
        w_router = sb("w_router", [P, KE, EXPERTS])
        w_a = sb("w_a", [P, EXPERTS])
        wq = sb("wq", [P, KE, AH, 32])
        wk = sb("wk", [P, KE, AH, 32])
        wv = sb("wv", [P, KE, EMB])
        wo = sb("wo", [P, KE, EMB])
        bq = sb("bq_sb", [P, 4])
        bk = sb("bk_sb", [P, 4])
        bq4 = sb("bq4", [P, 4])
        bv = sb("bv_sb", [P, EMB])
        bo = sb("bo_sb", [P, EMB])

        x = sb("x_sb", [P, TT, EMB])
        xn = sb("xn", [P, TT, EMB])
        xnT = sb("xnT", [P, KE, TOK])
        gff = sb("gff", [P, TT, EMB])
        s0 = sb("s0", [P, TT, EMB])
        s1 = sb("s1", [P, TT, EMB])
        adt = sb("adt", [P, TT, HEADS])
        dts = sb("dts", [P, TT, HEADS])
        decay = sb("decay", [P, TT, HEADS])
        gc = sb("gc", [P, TT, GROUPS, CS])
        dd = sb("dd", [P, HEADS, CS])
        ssq = sb("ssq", [P, 2, HALF])
        stats = sb("stats", [P, TT, 6])
        mv = sb("mv", [P, TT, 2])
        sd = sb("sd", [P, TT])
        rstd = sb("rstd", [P, TT])
        wring = sb("wring", [P, 4, 2, KE, P])
        big = sb("big", [P, 8192])
        w_out = big[:, :].rearrange("p (c e) -> p c e", c=CT)
        w_gate = big[:, 0:2048].rearrange("p (k m g c) -> p k m g c", k=KE, m=4, g=2)
        w_up = big[:, 2048:4096].rearrange("p (k m g c) -> p k m g c", k=KE, m=4, g=2)
        w_down = big[:, 4096:6144].rearrange("p (m g e) -> p m g e", m=4, g=2)

        area = sb("area", [P, 17408])
        at = [0]

        def carve(n):
            at[0] += n
            return area[:, at[0] - n:at[0]]

        bt = [carve(TOK) for _ in range(2)]
        ct = [carve(TOK) for _ in range(2)]
        cv = [carve(HALF) for _ in range(2)]
        hs = carve(HALF)
        hT = [carve(HALF).rearrange("p (t c) -> p t c", t=HT) for _ in range(2)]
        sg = [carve(HALF) for _ in range(2)]
        yg = [carve(HALF) for _ in range(2)]
        sq = [carve(HALF) for _ in range(2)]
        r1 = carve(HALF).rearrange("p (t h i) -> p t h i", t=HT, h=4)
        e1 = carve(HALF).rearrange("p (t h i) -> p t h i", t=HT, h=4)
        e2 = carve(HALF).rearrange("p (t h i) -> p t h i", t=HT, h=4)
        ms = carve(HALF).rearrange("p (t h i) -> p t h i", t=HT, h=4)
        mc = carve(HALF).rearrange("p (t h i) -> p t h i", t=HT, h=4)
        early = at[0]
        mb = carve(2 * HT * 4 * P).rearrange("p (s t h i) -> p s t h i", s=2, t=HT, h=4)
        assert at[0] <= 17408
        at[0] = 0
        hug = [carve(512) for _ in range(2)]
        huT = [carve(512) for _ in range(2)]
        w_u = carve(KE * EXPERTS * RANK).rearrange("p (k s) -> p k s", k=KE)
        w_v = carve(4 * EMB).rearrange("p (k e) -> p k e", k=4)
        attr = carve(EXPERTS * EXPERTS).rearrange("p (a b) -> p a b", a=EXPERTS)
        awt = carve(EXPERTS * EXPERTS).rearrange("p (a b) -> p a b", a=EXPERTS)
        sp = [carve(TT * HEADS).rearrange("p (t h) -> p t h", t=TT) for _ in range(3)]
        sc, pe_, sel0, sel1 = [carve(TT * EXPERTS).rearrange("p (t s) -> p t s", t=TT) for _ in range(4)]
        sel = [sel0, sel1]
        assert at[0] <= early
        at[0] = 0
        xb = carve(512).rearrange("p (k t) -> p k t", k=KE)
        qT = carve(1024).rearrange("p (n t) -> p n t", n=4)
        kT = carve(1024).rearrange("p (n t) -> p n t", n=4)
        vb = carve(512).rearrange("p (n e) -> p n e", n=2)
        pr = [carve(512).rearrange("p (q k) -> p q k", q=2) for _ in range(2)]
        pT = [carve(512).rearrange("p (k q) -> p k q", k=2) for _ in range(2)]
        ob = carve(512).rearrange("p (q h d) -> p q h d", q=2, h=AH)
        oT = carve(512).rearrange("p (k q) -> p k q", k=KE)
        nmx = carve(32).rearrange("p (h q) -> p h q", h=AH)
        den = carve(32).rearrange("p (q h) -> p q h", q=2)
        rden = carve(32).rearrange("p (q h) -> p q h", q=2)
        sgu = [carve(512) for _ in range(2)]
        hm = carve(2048).rearrange("p (m t) -> p m t", m=4)
        ha = carve(2048).rearrange("p (m t) -> p m t", m=4)
        hk = carve(2048).rearrange("p (m t) -> p m t", m=4)
        g1 = [carve(512) for _ in range(2)]
        cmpb = carve(1536).bitcast(BF16).rearrange("p (n t) -> p n t", n=6)
        wins = carve(1024).bitcast(BF16).rearrange("p (n t) -> p n t", n=4)
        assert at[0] <= 17408
        eps_ln = sb("eps_ln", [P, 1])
        eps_rms = sb("eps_rms", [P, 1])
        top = sb("top", [P, TT, 8])
        topi = sb("topi", [P, TT, 8], U32)
        topf = sb("topf", [P, TT, 8])
        rsum = [sb(f"rsum{i}", [P, TT]) for i in range(4)]
        aw = sb("aw", [P, EXPERTS])

        x_in = sem("x_in")
        const_in = sem("const_in")
        moe_in = sem("moe_in")
        bc_in = [sem(f"bc_in{i}") for i in range(4)]
        wout_in = sem("wout_in")
        attn_in = sem("attn_in")
        wvo_in = sem("wvo_in")
        ff_in = sem("ff_in")
        w_in = [sem(f"w_in{i}") for i in range(4)]
        pool_const = sem("pool_const")
        dve_step = sem("dve_step")
        act_step = sem("act_step")
        ln_tile = sem("ln_tile")
        xT_done = sem("xT_done")
        xT_ready = sem("xT_ready")
        dt_done = sem("dt_done")
        adt_ready = sem("adt_ready")
        suffix_done = sem("suffix_done")
        decay_ready = sem("decay_ready")
        sc_done = sem("sc_done")
        route_exp = sem("route_exp")
        hu_done = sem("hu_done")
        hug_ready = sem("hug_ready")
        huT_done = sem("huT_done")
        huT_ready = sem("huT_ready")
        moe_done = sem("moe_done")
        gff_ready = sem("gff_ready")
        bcp_done = sem("bcp_done")
        bc_tap = sem("bc_tap")
        bc_conv = sem("bc_conv")
        bc_silu = sem("bc_silu")
        g_done = sem("g_done")
        g_ready = sem("g_ready")
        r1_ready = sem("r1_ready")
        seg_done = sem("seg_done")
        exp_done = sem("exp_done")
        e2d_ready = sem("e2d_ready")
        m_add = sem("m_add")
        m_g = sem("m_g")
        m_dt = sem("m_dt")
        m_ready = sem("m_ready")
        mb_ready = sem("mb_ready")
        hid_done = sem("hid_done")
        gate_done = sem("gate_done")
        tap_done = sem("tap_done")
        conv_done = sem("conv_done")
        hs_ready = sem("hs_ready")
        t_done = sem("t_done")
        hT_ready = sem("hT_ready")
        y_done = sem("y_done")
        sg_ready = sem("sg_ready")
        yg_ready = sem("yg_ready")
        sq_ready = sem("sq_ready")
        ssq_done = sem("ssq_done")
        out_done = sem("out_done")
        s0_ready = sem("s0_ready")
        ss_done = sem("ss_done")
        xb_ready = sem("xb_ready")
        qkv_done = sem("qkv_done")
        qk_ready = sem("qk_ready")
        v_ready = sem("v_ready")
        s_done = sem("s_done")
        mx_ready = sem("mx_ready")
        p_ready = sem("p_ready")
        pT_done = sem("pT_done")
        pT_ready = sem("pT_ready")
        pv_done = sem("pv_done")
        ob_ready = sem("ob_ready")
        oT_done = sem("oT_done")
        oT_ready = sem("oT_ready")
        wo_done = sem("wo_done")
        s1_ready = sem("s1_ready")
        gu_done = sem("gu_done")
        sgu_ready = sem("sgu_ready")
        hm_ready = sem("hm_ready")
        ha_ready = sem("ha_ready")
        hk_ready = sem("hk_ready")
        g1_ready = sem("g1_ready")
        y_ready = sem("y_ready")
        y_out = sem("y_out")
        chain = sem("chain")
        conv_step = sem("conv_step")
        rden_ready = sem("rden_ready")
        ff_step = sem("ff_step")
        kept_used = sem("kept_used")
        fin_step = sem("fin_step")

        x_dram = t_in["x"].rearrange("(t p) e -> p t e", p=P)
        out_dram = out.rearrange("(t p) e -> p t e", p=P)
        win_dram = t_in["w_in"].rearrange("(k p) c -> p k c", p=P)
        NJ = CT // 4
        block = ctx.enter_context(nc.Block())

        @block.sync
        def _(sp_):
            sp_.dma_start(x[:, 0:HT, :], x_dram[:, 0:HT, :]).then_inc(x_in, 16)
            sp_.dma_start(x[:, HT:TT, :], x_dram[:, HT:TT, :]).then_inc(x_in, 16)
            for dst, name in ((ident, "ident"), (later, "later"), (chunk, "chunk"), (upto, "upto"), (diag, "diag"),
                              (future, "future"), (ident_b, "ident_b"), (expert_no, "expert_no"),
                              (conv_b, "conv_b"), (norm_w, "norm_w")):
                sp_.dma_start(dst[:, :], t_in[name]).then_inc(const_in, 16)
            sp_.dma_start(conv_w[:, :, :], t_in["conv_w"]).then_inc(const_in, 16)
            for dst, name in ((dt_bias, "dt_bias"), (a_row, "a_log"), (d_row, "d")):
                sp_.dma_start(dst[:, :], t_in[name].partition_broadcast(P)).then_inc(const_in, 16)
            sp_.dma_start(w_dt[:, :, :], win_dram[:, :, INTER + CONV:PROJ]).then_inc(const_in, 16)
            sp_.dma_start(w_router[:, :, :], t_in["w_router"].rearrange("(k p) s -> p k s", p=P)).then_inc(moe_in, 16)
            sp_.dma_start(w_a[:, :], t_in["w_a"].partition_broadcast(P)).then_inc(moe_in, 16)
            sp_.dma_start(attr[:, :, :].rearrange("p a b -> p (a b)"), t_in["attr"].partition_broadcast(P)).then_inc(moe_in, 16)
            sp_.dma_start(w_u[:, :, :], t_in["w_u"].rearrange("(k p) s -> p k s", p=P)).then_inc(moe_in, 16)
            sp_.dma_start(w_v[:, :, :], t_in["w_v"].rearrange("(k p) e -> p k e", p=P)).then_inc(moe_in, 16)
            base = 2 * INTER
            for g in range(GROUPS):
                if g >= 4:
                    sp_.wait_ge(bcp_done, 4 * (g - 4) + 4)
                for i in range(2):
                    c0 = base + (i * GROUPS + g) * P
                    sp_.dma_start(wring[:, g % 4, i, :, :], win_dram[:, :, c0:c0 + P]).then_inc(bc_in[g % 4], 16)
                if g == 3:
                    sp_.dma_start(w_out, t_in["w_out"].rearrange("(c p) e -> p c e", p=P)).then_inc(wout_in, 16)
            def w_tile(c, s):
                sp_.dma_start(wring[:, s, 0, :, :], win_dram[:, :, bass.ds(c * P + INTER, P)]).then_inc(w_in[s], 16)
                sp_.dma_start(wring[:, s, 1, :, :], win_dram[:, :, bass.ds(c * P, P)]).then_inc(w_in[s], 16)
            for s in range(4):
                sp_.wait_ge(bcp_done, 4 * (4 + s) + 4)
                w_tile(s, s)
            with sp_.Fori(1, NJ) as j:
                for s in range(4):
                    sp_.wait_ge(gate_done, 4 * j + s - 3)
                    w_tile(4 * j + s, s)
            with sp_.Fori(0, NJ) as j:
                for s in range(4):
                    sp_.wait_ge(gate_done, 4 * j + (CT + s - 3))
                    w_tile(4 * j + s, s)
            for w, name in ((wv, "wv"), (wo, "wo")):
                sp_.dma_start(w[:, :, :], t_in[name].rearrange("(k p) e -> p k e", p=P)).then_inc(wvo_in, 16)
            sp_.wait_ge(out_done, 2 * CT)
            sp_.dma_start(big[:, 0:2048].rearrange("p (k c) -> p k c", k=KE),
                          t_in["w_gate"].rearrange("(k p) c -> p k c", p=P)).then_inc(ff_in, 16)
            sp_.dma_start(big[:, 2048:4096].rearrange("p (k c) -> p k c", k=KE),
                          t_in["w_up"].rearrange("(k p) c -> p k c", p=P)).then_inc(ff_in, 16)
            sp_.dma_start(big[:, 4096:6144].rearrange("p (k c) -> p k c", k=FT),
                          t_in["w_down"].rearrange("(k p) c -> p k c", p=P)).then_inc(ff_in, 16)
            for h in range(2):
                sp_.wait_ge(y_ready, 2 * h + 2)
                sp_.dma_start(out_dram[:, h * HT:(h + 1) * HT, :], s1[:, h * HT:(h + 1) * HT, :]).then_inc(y_out, 16)
            sp_.wait_ge(y_out, 32)

        @block.gpsimd
        def _(pool):
            pool.memset(ones[:, :], 1.0).then_inc(pool_const, 1)
            pool.memset(zeros[:, :], 0.0).then_inc(pool_const, 1)
            pool.memset(wq[:, :, :, :], 0.0).then_inc(pool_const, 1)
            pool.memset(wk[:, :, :, :], 0.0).then_inc(pool_const, 1)
            pool.memset(bq[:, :], 0.0).then_inc(pool_const, 1)
            pool.memset(bk[:, :], 0.0).then_inc(pool_const, 1)
            pool.memset(ssq[:, :, :], 0.0).then_inc(ssq_done, 1)
            pool.memset(mb[:, :, :, :, :], 0.0).then_inc(pool_const, 1)
            pool.wait_ge(const_in, 16 * 15)
            pool.tensor_tensor(dd[:, :, :], diag[:, None, :].broadcast_to([P, HEADS, CS]),
                               d_row[:, :, None].broadcast_to([P, HEADS, CS]), ALU.mult).then_inc(pool_const, 1)
            pool.wait_ge(pool_const, 8)
            for w, name in ((wq, "wq"), (wk, "wk")):
                for k in range(KE):
                    pool.dma_start(w[:, k, :, 0:AD], t_in[name][k * P:(k + 1) * P, :].rearrange("p (h d) -> p h d", h=AH))\
                        .then_inc(attn_in, 16)
            for b, name in ((bq, "bq"), (bk, "bk")):
                for r in range(4):
                    pool.dma_start(b[32 * r:32 * r + AD, :], t_in[name][r]).then_inc(attn_in, 16)
            pool.dma_start(bv[:, :], t_in["bv"].partition_broadcast(P)).then_inc(attn_in, 16)
            pool.dma_start(bo[:, :], t_in["bo"].partition_broadcast(P)).then_inc(attn_in, 16)
            pool.wait_ge(wout_in, 16)
            pool.tensor_tensor(w_out, w_out, norm_w[:, :, None].broadcast_to([P, CT, EMB]), ALU.mult)\
                .then_inc(pool_const, 1)
            pool.wait_ge(adt_ready, 1)

            def mask_a(half, p):
                a = adt[:, half * HT:(half + 1) * HT, bass.ds(4 * p, 4)]
                return pool.tensor_tensor(r1, a[:, :, :, None].broadcast_to([P, HT, 4, CS]),
                                          upto[:, None, None, :].broadcast_to([P, HT, 4, CS]), ALU.mult)

            def m_first(half, p, n):
                pool.wait_ge(exp_done, n + 1)
                e = decay[:, half * HT:(half + 1) * HT, bass.ds(4 * p, 4)]
                pool.tensor_tensor(e2, e2, e[:, :, :, None].broadcast_to([P, HT, 4, CS]), ALU.mult).then_inc(e2d_ready, 1)

            def m_last(half, p, n):
                pool.wait_ge(m_g, n + 1)
                e = dts[:, half * HT:(half + 1) * HT, bass.ds(4 * p, 4)]
                pool.tensor_tensor(ms, ms, e[:, :, :, None].broadcast_to([P, HT, 4, CS]), ALU.mult).then_inc(m_dt, 1)
                pool.wait_ge(m_dt, n + 1)
                pool.wait_ge(mb_ready, n)
                d = dd[:, bass.ds(4 * p, 4), :]
                pool.tensor_tensor(mc, ms, d[:, None, :, :].broadcast_to([P, HT, 4, CS]), ALU.add).then_inc(m_ready, 1)

            def add_square(half, n, s):
                pool.wait_ge(sq_ready, n + 1)
                pool.wait_ge(ssq_done, n + 1)
                pool.tensor_tensor(ssq[:, half, :], ssq[:, half, :], sq[s % 2], ALU.add).then_inc(ssq_done, 1)

            mask_a(0, 0).then_inc(r1_ready, 1)
            pool.wait_ge(decay_ready, 1)
            m_first(0, 0, 0)
            pool.wait_ge(seg_done, 1)
            mask_a(0, 1).then_inc(r1_ready, 1)
            m_last(0, 0, 0)

            def body(half, j, last):
                for q in range(2):
                    pair = 2 * j + q
                    n = pair + half * (CT // 2)
                    over = last and q == 1
                    if not (over and half == 1):
                        nh, npair = (half + 1, 0) if over else (half, pair + 1)
                        m_first(nh, npair, n + 1)
                    if not (last and half == 1):
                        pool.wait_ge(seg_done, n + 2)
                        mask_a(half + 1 if last else half, q if last else pair + 2).then_inc(r1_ready, 1)
                    add_square(half, 2 * n, 0)
                    if not (over and half == 1):
                        m_last(nh, npair, n + 1)
                    add_square(half, 2 * n + 1, 1)

            for half in range(2):
                body(half, 0, False)
                with pool.Fori(1, NJ - 1) as j:
                    body(half, j, False)
                body(half, NJ - 1, True)

        @block.scalar
        def _(act):
            act.wait_ge(dve_step, 1)
            act.activation(sd[:, :], mv[:, :, 1], ACT.Sqrt, bias=eps_ln[:, :]).then_inc(act_step, 1)
            act.wait_ge(xT_done, 1)
            for i in range(4):
                act.activation(xnT[:, i // 2, (i % 2) * HALF:(i % 2 + 1) * HALF], bank[i][:, :], ACT.Copy).then_inc(xT_ready, 1)
            act.wait_ge(dve_step, 2)
            act.activation(sp[1][:, :, :], sp[0][:, :, :], ACT.Abs).then_inc(act_step, 1)
            act.wait_ge(act_step, 2)
            act.activation(sp[1][:, :, :], sp[1][:, :, :], ACT.Exp, scale=-1.0).then_inc(act_step, 1)
            act.wait_ge(const_in, 16 * 15)
            act.activation(a_row[:, :], a_row[:, :], ACT.Exp).then_inc(act_step, 1)
            act.wait_ge(dve_step, 3)
            act.activation(decay[:, :, :], sp[2][:, :, :], ACT.Ln).then_inc(act_step, 1)
            act.wait_ge(suffix_done, 1)
            act.activation(decay[:, :, :], bank[5][:, :], ACT.Exp).then_inc(decay_ready, 1)
            act.wait_ge(route_exp, 1)
            act.activation(pe_[:, :, :], pe_[:, :, :], ACT.Exp).then_inc(act_step, 1)
            act.activation(aw[:, :], aw[:, :], ACT.Exp, scale=-1.0).then_inc(act_step, 1)
            for t in range(TT):
                act.wait_ge(huT_done, t + 1)
                act.activation(huT[t % 2], bank[2 + t % 2][:, :], ACT.Copy).then_inc(huT_ready, 1)
                if t >= 1:
                    act.wait_ge(moe_done, t)
                    act.activation(gff[:, t - 1, :], bank[6 + (t - 1) % 2][:, 0:EMB], ACT.Silu).then_inc(gff_ready, 1)
            act.wait_ge(moe_done, TT)
            act.activation(gff[:, TT - 1, :], bank[6 + (TT - 1) % 2][:, 0:EMB], ACT.Silu).then_inc(gff_ready, 1)

            def bc_first_tap(g, u):
                act.wait_ge(bcp_done, 4 * g + u + 1)
                if 4 * g + u >= 2:
                    act.wait_ge(bc_silu, 4 * g + u - 1)
                tile = INTER // P + (u // 2) * GROUPS + g
                act.activation(cv[u % 2], bank[u][:, :], ACT.Identity, scale=conv_w[:, tile, TAPS - 1:TAPS],
                               bias=conv_b[:, tile:tile + 1]).then_inc(bc_tap, 1)

            def bc_silu_of(g, u):
                act.wait_ge(bc_conv, 4 * g + u + 1)
                dst = (bt, ct)[u // 2][g % 2]
                act.activation(dst[:, (u % 2) * HALF:(u % 2 + 1) * HALF], cv[u % 2], ACT.Silu).then_inc(bc_silu, 1)

            def g_blocks(g):
                act.wait_ge(g_done, g + 1)
                for i in range(2):
                    src = bank[4 + i][:, :].rearrange("p (t c) -> p t c", t=HT)
                    for q in range(4):
                        last = act.activation(gc[32 * q:32 * q + 32, i * HT:(i + 1) * HT, g, :],
                                              src[32 * q:32 * q + 32, :, 32 * q:32 * q + 32], ACT.Copy)
                last.then_inc(g_ready, 1)

            for g in range(GROUPS + 1):
                for u in range(4):
                    if g < GROUPS:
                        bc_first_tap(g, u)
                    if (g, u) != (0, 0) and (g < GROUPS or u == 0):
                        bc_silu_of(g if u else g - 1, (u - 1) % 4)
                if g >= 1:
                    g_blocks(g - 1)

            def first_tap(c, n):
                act.wait_ge(hid_done, n + 1)
                act.wait_ge(hs_ready, n)
                act.activation(cv[0], bank[0][:, :], ACT.Identity, scale=conv_w[:, bass.ds(c, 1), TAPS - 1],
                               bias=conv_b[:, bass.ds(c, 1)]).then_inc(tap_done, 1)

            def silu_gate(n, s):
                act.wait_ge(gate_done, n + 1)
                act.activation(sg[s % 2], bank[1][:, :], ACT.Silu).then_inc(sg_ready, 1)

            def silu_hidden(n):
                act.wait_ge(conv_done, n + 1)
                act.activation(hs, cv[0], ACT.Silu).then_inc(hs_ready, 1)

            def exps(n):
                act.wait_ge(seg_done, n + 1)
                act.wait_ge(m_add, n)
                act.activation(e1, bank[4][:, :].rearrange("p (t h i) -> p t h i", t=HT, h=4), ACT.Exp)
                act.activation(e2, bank[5][:, :].rearrange("p (t h i) -> p t h i", t=HT, h=4), ACT.Exp).then_inc(exp_done, 1)

            def place(n, q):
                act.wait_ge(m_ready, n + 1)
                if isinstance(n, int) and n == 0:
                    act.wait_ge(pool_const, 8)
                else:
                    act.wait_ge(y_done, 2 * n - 1)
                for r in range(4):
                    last = act.activation(mb[32 * r:32 * r + 32, q % 2, :, :, 32 * r:32 * r + 32],
                                          mc[32 * r:32 * r + 32, :, :, :], ACT.Copy)
                last.then_inc(mb_ready, 1)

            def square(n, s):
                act.wait_ge(yg_ready, n + 1)
                act.wait_ge(ssq_done, n + 1)
                act.activation(sq[s % 2], yg[s % 2], ACT.Square).then_inc(sq_ready, 1)

            act.wait_ge(r1_ready, 1)
            exps(0)
            first_tap(0, 0)
            silu_gate(0, 0)
            silu_hidden(0)
            place(0, 0)

            def body(half, j, last):
                for s in range(4):
                    c = 4 * j + s
                    n = c + half * CT
                    over = last and s == 3
                    more = not (over and half == 1)
                    pair = 2 * j + (s // 2) + half * (CT // 2)
                    build_next = not (last and s >= 2 and half == 1)
                    if more:
                        first_tap(0 if over else c + 1, n + 1)
                    if more:
                        silu_hidden(n + 1)
                    if s % 2 == 0 and build_next:
                        exps(pair + 1)
                    if s % 2 == 1 and build_next:
                        place(pair + 1, s // 2 + 1)
                    if more:
                        silu_gate(n + 1, s + 1)
                    square(n, s)

            for half in range(2):
                body(half, 0, False)
                with act.Fori(1, NJ - 1) as j:
                    body(half, j, False)
                body(half, NJ - 1, True)

            act.wait_ge(ss_done, 1)
            act.activation(rstd[:, :], bank[0][:, 0:TT], ACT.Sqrt, scale=1.0 / INTER, bias=eps_rms[:, :]).then_inc(act_step, 1)
            act.wait_ge(dve_step, 4)
            act.activation(sd[:, :], mv[:, :, 1], ACT.Sqrt, bias=eps_ln[:, :]).then_inc(act_step, 1)
            act.wait_ge(xT_done, 2)
            for i in range(4):
                act.activation(xnT[:, i // 2, (i % 2) * HALF:(i % 2 + 1) * HALF], bank[i][:, :], ACT.Copy).then_inc(xT_ready, 1)
            act.wait_ge(attn_in, 16 * 14)
            act.mul(bq4[:, :], bq[:, :], 0.25).then_inc(act_step, 1)
            act.wait_ge(act_step, 10)
            act.wait_ge(xT_ready, 8)
            with act.Fori(0, BATCH) as b:
                act.wait_ge(qkv_done, 3 * b)
                act.activation(xb, xnT[:, :, bass.ds(b * SEQ, SEQ)], ACT.Copy).then_inc(xb_ready, 1)
                for i in range(2):
                    act.wait_ge(qkv_done, 3 * b + i + 1)
                    for n in range(4):
                        src = bank[2 * i + n // 2][:, (n % 2) * SEQ:(n % 2 + 1) * SEQ]
                        last = act.activation((qT, kT)[i][:, n, :], src, ACT.Identity, scale=(0.25, 1.0)[i],
                                              bias=(bq4, bk)[i][:, n:n + 1])
                    last.then_inc(qk_ready, 1)
                for h in range(AH):
                    act.wait_ge(mx_ready, b * AH + h + 1)
                    if h >= 2:
                        act.wait_ge(pT_done, b * AH + h - 1)
                    for q in range(2):
                        last = act.activation(pr[h % 2][:, q, :], bank[h % 4][:, q * SEQ:(q + 1) * SEQ], ACT.Exp,
                                              bias=nmx[:, h, q:q + 1], accum_out=den[:, q, h:h + 1])
                    last.then_inc(p_ready, 1)
                act.wait_ge(oT_done, b + 1)
                act.activation(oT.rearrange("p k q -> p (k q)"), bank[7][:, :], ACT.Copy).then_inc(oT_ready, 1)
            with act.Fori(0, 2) as hf:
                for gt in range(2):
                    for m in range(4):
                        i = 4 * gt + m
                        act.wait_ge(gu_done, 8 * hf + i + 1)
                        act.activation(sgu[i % 2], bank[2 * (i % 2)][:, :], ACT.Silu).then_inc(sgu_ready, 1)
                        act.wait_ge(hm_ready, 8 * hf + i + 1)
                        act.activation(ha[:, m, :], hm[:, m, :], ACT.Abs).then_inc(ha_ready, 1)
                act.wait_ge(kept_used, 2 * hf + 2)
                act.wait_ge(y_ready, 2 * hf)
                for i in range(2):
                    act.activation(g1[i], bank[6 + i][:, :], ACT.Silu).then_inc(g1_ready, 1)

        @block.vector
        def _(dve):
            steps = [0]

            def link(ins):
                ins.then_inc(chain, 1)
                steps[0] += 1
                dve.wait_ge(chain, steps[0])

            dve.memset(eps_ln[:, :], LN_EPS)
            link(dve.memset(eps_rms[:, :], RMS_EPS))

            def ln_stats():
                for t in range(TT):
                    link_last = dve.bn_stats(stats[:, t, :], x[:, t, :])
                link(link_last)
                for t in range(TT):
                    link_last = dve.bn_aggr(mv[:, t, :], stats[:, t, :])
                link_last.then_inc(dve_step, 1)

            def ln_apply():
                link(dve.reciprocal(rstd[:, :], sd[:, :]))
                for t in range(TT):
                    dve.tensor_scalar(xn[:, t, :], x[:, t, :], mv[:, t, 0:1], rstd[:, t:t + 1],
                                      ALU.subtract, ALU.mult).then_inc(ln_tile, 1)

            dve.wait_ge(x_in, 32)
            ln_stats()
            dve.wait_ge(act_step, 1)
            ln_apply()
            dve.wait_ge(const_in, 16 * 15)
            dve.wait_ge(dt_done, 1)
            dve.tensor_tensor(sp[0][:, :, :], bank[4][:, :].rearrange("p (t h) -> p t h", t=TT),
                              dt_bias[:, None, :].broadcast_to([P, TT, HEADS]), ALU.add).then_inc(dve_step, 1)
            dve.wait_ge(act_step, 3)
            dve.tensor_scalar(sp[2][:, :, :], sp[1][:, :, :], 1.0, None, ALU.add).then_inc(dve_step, 1)
            dve.wait_ge(dve_step, 3)
            link(dve.tensor_scalar(adt[:, :, :], sp[2][:, :, :], -1.0, 1e-30, ALU.add, ALU.max))
            link(dve.reciprocal(dts[:, :, :], adt[:, :, :]))
            link(dve.tensor_tensor(dts[:, :, :], dts[:, :, :], sp[1][:, :, :], ALU.mult))
            dve.wait_ge(act_step, 5)
            link(dve.tensor_tensor(dts[:, :, :], dts[:, :, :], decay[:, :, :], ALU.mult))
            link(dve.tensor_scalar(adt[:, :, :], sp[2][:, :, :], 1.0, None, ALU.is_equal))
            link(dve.tensor_tensor(adt[:, :, :], adt[:, :, :], sp[1][:, :, :], ALU.mult))
            link(dve.tensor_tensor(dts[:, :, :], dts[:, :, :], adt[:, :, :], ALU.add))
            link(dve.scalar_tensor_tensor(dts[:, :, :], sp[0][:, :, :], 0.0, dts[:, :, :], ALU.max, ALU.add))
            link(dve.tensor_scalar(a_row[:, :], a_row[:, :], -1.0, None, ALU.mult))
            dve.tensor_tensor(adt[:, :, :], dts[:, :, :], a_row[:, None, :].broadcast_to([P, TT, HEADS]),
                              ALU.mult).then_inc(adt_ready, 1)

            dve.wait_ge(sc_done, 1)
            link(dve.tensor_copy(sc[:, :, :], bank[6][:, 0:TT * EXPERTS].rearrange("p (t s) -> p t s", t=TT)))
            for t in range(TT):
                last = dve.max(top[:, t, :], sc[:, t, :])
            link(last)
            for t in range(TT):
                last = dve.max_index(topi[:, t, :], top[:, t, :], sc[:, t, :])
            link(last)
            dve.tensor_tensor(pe_[:, :, :], sc[:, :, :], top[:, :, 0:1].broadcast_to([P, TT, EXPERTS]), ALU.subtract)
            dve.wait_ge(moe_in, 16 * 5)
            link(dve.tensor_tensor(awt[:, :, :], attr[:, :, :], w_a[:, None, :].broadcast_to([P, EXPERTS, EXPERTS]), ALU.mult))
            link(dve.tensor_reduce(aw[:, :], awt[:, :, :], AX.X, ALU.add))
            link(dve.tensor_copy(topf[:, :, :], topi[:, :, :]))
            dve.tensor_copy(rsum[3][:, :], topf[:, :, 0]).then_inc(route_exp, 1)
            for i in range(2):
                last = dve.tensor_tensor(sel[i][:, :, :], expert_no[:, None, :].broadcast_to([P, TT, EXPERTS]),
                                         topf[:, :, i:i + 1].broadcast_to([P, TT, EXPERTS]), ALU.is_equal)
            link(last)
            link(dve.tensor_tensor(sel[0][:, :, :], sel[0][:, :, :], sel[1][:, :, :], ALU.add))
            dve.wait_ge(act_step, 7)
            link(dve.tensor_scalar(aw[:, :], aw[:, :], 1.0, None, ALU.add))
            link(dve.reciprocal(aw[:, :], aw[:, :]))
            link(dve.tensor_reduce(rsum[0][:, :], pe_[:, :, :], AX.X, ALU.add))
            link(dve.reciprocal(rsum[1][:, :], rsum[0][:, :]))
            link(dve.tensor_tensor(pe_[:, :, :], pe_[:, :, :], rsum[1][:, :, None].broadcast_to([P, TT, EXPERTS]), ALU.mult))
            link(dve.tensor_tensor(pe_[:, :, :], pe_[:, :, :], sel[0][:, :, :], ALU.mult))
            link(dve.tensor_reduce(rsum[0][:, :], pe_[:, :, :], AX.X, ALU.add))
            link(dve.tensor_scalar(rsum[0][:, :], rsum[0][:, :], 1e-8, None, ALU.add))
            link(dve.reciprocal(rsum[1][:, :], rsum[0][:, :]))
            link(dve.tensor_tensor(pe_[:, :, :], pe_[:, :, :], rsum[1][:, :, None].broadcast_to([P, TT, EXPERTS]), ALU.mult))
            link(dve.tensor_tensor(sel[1][:, :, :], pe_[:, :, :], aw[:, None, :].broadcast_to([P, TT, EXPERTS]), ALU.mult))
            link(dve.tensor_reduce(rsum[2][:, :], sel[1][:, :, :], AX.X, ALU.add))
            link(dve.tensor_scalar(rsum[2][:, :], rsum[2][:, :], 0.2, 0.9, ALU.mult, ALU.add))
            link(dve.tensor_tensor(pe_[:, :, :], pe_[:, :, :], rsum[2][:, :, None].broadcast_to([P, TT, EXPERTS]), ALU.mult))
            for t in range(TT):
                dve.wait_ge(hu_done, t + 1)
                dve.tensor_tensor(hug[t % 2].rearrange("p (s r) -> p s r", s=EXPERTS),
                                  bank[t % 2][:, :].rearrange("p (s r) -> p s r", s=EXPERTS),
                                  pe_[:, t, :, None].broadcast_to([P, EXPERTS, RANK]), ALU.mult).then_inc(hug_ready, 1)

            def conv(dst, src, w, last_sem):
                d = dst.rearrange("p (b t) -> p b t", b=2)
                s = src.rearrange("p (b t) -> p b t", b=2)
                for k in range(1, TAPS):
                    ins = dve.scalar_tensor_tensor(d[:, :, k:SEQ], s[:, :, 0:SEQ - k], w(TAPS - 1 - k),
                                                   d[:, :, k:SEQ], ALU.mult, ALU.add)
                    if k < TAPS - 1:
                        yield ins
                ins.then_inc(last_sem, 1)

            for g in range(GROUPS):
                for u in range(4):
                    dve.wait_ge(bc_tap, 4 * g + u + 1)
                    tile = INTER // P + (u // 2) * GROUPS + g
                    for ins in conv(cv[u % 2], bank[u][:, :], lambda k: conv_w[:, tile, k:k + 1], bc_conv):
                        link(ins)

            def transposed(n, s):
                dve.wait_ge(t_done, n + 1)
                dve.tensor_copy(hT[s % 2], bank[2][:, :].rearrange("p (t c) -> p t c", t=HT)).then_inc(hT_ready, 1)

            def hidden_conv(c, n):
                dve.wait_ge(tap_done, n + 1)
                k = 0
                for ins in conv(cv[0], bank[0][:, :], lambda k: conv_w[:, bass.ds(c, 1), k], conv_done):
                    k += 1
                    ins.then_inc(conv_step, 1)
                    dve.wait_ge(conv_step, 2 * n + k)

            def gated(n, s):
                dve.wait_ge(y_done, n + 1)
                dve.wait_ge(sg_ready, n + 1)
                dve.tensor_tensor(yg[s % 2], bank[3][:, :], sg[s % 2], ALU.mult).then_inc(yg_ready, 1)

            def m_middle(n, q, half):
                dve.wait_ge(e2d_ready, n + 1)
                dve.wait_ge(m_ready, n)
                dve.tensor_tensor(ms, e1, e2, ALU.add).then_inc(m_add, 1)
                dve.wait_ge(m_add, n + 1)
                g0 = 4 * (q % 2)
                dve.tensor_tensor(ms, ms, gc[:, half * HT:(half + 1) * HT, g0:g0 + 4, :], ALU.mult).then_inc(m_g, 1)

            dve.wait_ge(g_ready, GROUPS)
            m_middle(0, 0, 0)
            hidden_conv(0, 0)

            def keep_sums(half):
                dve.wait_ge(out_done, (half + 1) * CT)
                for i in range(2):
                    t0 = half * HT + 2 * i
                    dve.tensor_copy(s0[:, t0:t0 + 2, :], bank[6 + i][:, :].rearrange("p (t e) -> p t e", t=2)).then_inc(s0_ready, 1)

            def body(half, j, last):
                for s in range(4):
                    c = 4 * j + s
                    n = c + half * CT
                    over = last and s == 3
                    transposed(n, s)
                    if not (over and half == 1):
                        hidden_conv(0 if over else c + 1, n + 1)
                    gated(n, s)
                    if half == 1 and isinstance(j, int) and c == 0:
                        keep_sums(0)
                    if s % 2 == 0 and not (last and s == 2 and half == 1):
                        over = last and s == 2
                        m_middle(2 * j + s // 2 + 1 + half * (CT // 2), s // 2 + 1, half + 1 if over else half)

            for half in range(2):
                body(half, 0, False)
                with dve.Fori(1, NJ - 1) as j:
                    body(half, j, False)
                body(half, NJ - 1, True)
            keep_sums(1)

            dve.wait_ge(act_step, 8)
            link(dve.reciprocal(rstd[:, :], rstd[:, :]))
            dve.wait_ge(gff_ready, TT)
            for t in range(TT):
                last = dve.scalar_tensor_tensor(s0[:, t, :], s0[:, t, :], rstd[:, t:t + 1], gff[:, t, :], ALU.mult, ALU.mult)
            link(last)
            link(dve.tensor_tensor(x[:, :, :], x[:, :, :], s0[:, :, :], ALU.add))
            ln_stats()
            dve.wait_ge(act_step, 9)
            ln_apply()
            dve.wait_ge(attn_in, 16 * 14)
            with dve.Fori(0, BATCH) as b:
                dve.wait_ge(qkv_done, 3 * b + 3)
                for i in range(2):
                    last = dve.tensor_tensor(vb[:, i, :], bank[4][:, i * EMB:(i + 1) * EMB], bv[:, :], ALU.add)
                last.then_inc(v_ready, 1)
                for h in range(AH + 1):
                    if h < AH:
                        dve.wait_ge(s_done, b * AH + h + 1)
                        dve.tensor_reduce(nmx[:, h, :], bank[h % 4][:, :].rearrange("p (q k) -> p q k", q=2),
                                          AX.X, ALU.max, negate=True).then_inc(mx_ready, 1)
                    if h >= 1:
                        dve.wait_ge(pT_done, b * AH + h)
                        dve.tensor_copy(pT[(h - 1) % 2].rearrange("p k q -> p (k q)"), bank[4 + (h - 1) % 2][:, :]).then_inc(pT_ready, 1)
                dve.wait_ge(p_ready, (b + 1) * AH)
                dve.reciprocal(rden, den).then_inc(rden_ready, 1)
                dve.wait_ge(rden_ready, b + 1)
                dve.wait_ge(pv_done, (b + 1) * AH)
                dve.tensor_tensor(ob, bank[6][:, :].rearrange("p (q h d) -> p q h d", q=2, h=AH),
                                  rden[:, :, :, None].broadcast_to([P, 2, AH, AD]), ALU.mult).then_inc(ob_ready, 1)
                dve.wait_ge(wo_done, b + 1)
                dve.tensor_tensor(s1[:, bass.ds(2 * b, 2), :], bank[5][:, :].rearrange("p (q e) -> p q e", q=2),
                                  bo[:, None, :].broadcast_to([P, 2, EMB]), ALU.add).then_inc(s1_ready, 1)
            pairs = [(0, 1), (0, 2), (0, 3), (1, 2), (1, 3), (2, 3)]
            with dve.Fori(0, 2) as hf:
                for gt in range(2):
                    dve.wait_ge(hk_ready, 8 * hf + 4 * gt)
                    for m in range(4):
                        i = 4 * gt + m
                        dve.wait_ge(sgu_ready, 8 * hf + i + 1)
                        dve.tensor_tensor(hm[:, m, :], bank[2 * (i % 2) + 1][:, :], sgu[i % 2], ALU.mult).then_inc(hm_ready, 1)
                    n = 2 * hf + gt
                    dve.wait_ge(ha_ready, 4 * n + 4)
                    for i, (a, b2) in enumerate(pairs):
                        last = dve.tensor_tensor(cmpb[:, i, :], ha[:, a, :], ha[:, b2, :], ALU.is_ge)
                    last.then_inc(ff_step, 1)
                    dve.wait_ge(ff_step, 3 * n + 1)
                    dve.tensor_tensor(wins[:, 0, :], cmpb[:, 0, :], cmpb[:, 1, :], ALU.add)
                    dve.tensor_tensor(wins[:, 1, :], cmpb[:, 3, :], cmpb[:, 0, :], ALU.subtract)
                    dve.tensor_tensor(wins[:, 2, :], cmpb[:, 5, :], cmpb[:, 1, :], ALU.subtract)
                    dve.tensor_tensor(wins[:, 3, :], cmpb[:, 2, :], cmpb[:, 4, :], ALU.add).then_inc(ff_step, 1)
                    dve.wait_ge(ff_step, 3 * n + 2)
                    dve.tensor_tensor(wins[:, 0, :], wins[:, 0, :], cmpb[:, 2, :], ALU.add)
                    dve.tensor_tensor(wins[:, 1, :], wins[:, 1, :], cmpb[:, 4, :], ALU.add)
                    dve.tensor_tensor(wins[:, 2, :], wins[:, 2, :], cmpb[:, 3, :], ALU.subtract)
                    dve.tensor_tensor(wins[:, 3, :], wins[:, 3, :], cmpb[:, 5, :], ALU.add).then_inc(ff_step, 1)
                    dve.wait_ge(ff_step, 3 * n + 3)
                    dve.wait_ge(kept_used, n)
                    for m, (thr, op) in enumerate(((2.0, ALU.is_ge), (1.0, ALU.is_ge), (0.0, ALU.is_ge), (1.0, ALU.is_le))):
                        dve.scalar_tensor_tensor(hk[:, m, :], wins[:, m, :], thr, hm[:, m, :], op, ALU.mult).then_inc(hk_ready, 1)
                for i in range(2):
                    dve.wait_ge(g1_ready, 2 * hf + i + 1)
                    s = s1[:, bass.ds(hf * HT + 2 * i, 2), :]
                    dve.tensor_tensor(s, s, g1[i].rearrange("p (t e) -> p t e", t=2), ALU.mult).then_inc(fin_step, 1)
                    dve.wait_ge(fin_step, 2 * hf + i + 1)
                    dve.tensor_tensor(s, s, x[:, bass.ds(hf * HT + 2 * i, 2), :], ALU.add).then_inc(y_ready, 1)

        @block.tensor
        def _(pe):
            def ln_transposes(n):
                for t in range(TT):
                    pe.wait_ge(ln_tile, n * TT + t + 1)
                    for k in range(KE):
                        last = pe.transpose(bank[2 * k + t // HT][:, (t % HT) * P:(t % HT + 1) * P],
                                            xn[:, t, k * P:(k + 1) * P], ident[:, :])
                last.then_inc(xT_done, 1)

            pe.wait_ge(const_in, 16 * 15)
            ln_transposes(0)
            pe.wait_ge(xT_ready, 4)
            for t in range(TT):
                for k in range(KE):
                    last = pe.matmul(bank[4][:, t * HEADS:(t + 1) * HEADS], xnT[:, k, t * P:(t + 1) * P], w_dt[:, k, :],
                                     start=(k == 0), stop=(k == KE - 1))
            last.then_inc(dt_done, 1)
            pe.wait_ge(moe_in, 16 * 5)
            for t in range(TT):
                for k in range(KE):
                    last = pe.matmul(bank[6][:, t * EXPERTS:(t + 1) * EXPERTS], xnT[:, k, t * P:(t + 1) * P],
                                     w_router[:, k, :], start=(k == 0), stop=(k == KE - 1))
            last.then_inc(sc_done, 1)
            pe.wait_ge(adt_ready, 1)
            pe.matmul(bank[5][:, :], later[:, :], adt[:, :, :].rearrange("p t h -> p (t h)"), start=True, stop=True)\
                .then_inc(suffix_done, 1)

            def expert_up(t):
                for k in range(KE):
                    last = pe.matmul(bank[t % 2][:, :], xnT[:, k, t * P:(t + 1) * P], w_u[:, k, :],
                                     start=(k == 0), stop=(k == KE - 1))
                last.then_inc(hu_done, 1)

            expert_up(0)
            expert_up(1)
            for t in range(TT):
                pe.wait_ge(hug_ready, t + 1)
                if t >= 2:
                    pe.wait_ge(huT_ready, t - 1)
                for c in range(4):
                    last = pe.transpose(bank[2 + t % 2][:, c * P:(c + 1) * P], hug[t % 2][:, c * P:(c + 1) * P], ident[:, :])
                last.then_inc(huT_done, 1)
                if t + 2 < TT:
                    expert_up(t + 2)
                pe.wait_ge(huT_ready, t + 1)
                if t >= 2:
                    pe.wait_ge(gff_ready, t - 1)
                for c in range(4):
                    last = pe.matmul(bank[6 + t % 2][:, 0:EMB], huT[t % 2][:, c * P:(c + 1) * P], w_v[:, c, :],
                                     start=(c == 0), stop=(c == 3))
                last.then_inc(moe_done, 1)

            def bc_project(g, u):
                pe.wait_ge(bc_in[g % 4], 32 * (g // 4 + 1))
                if g >= 1:
                    pe.wait_ge(bc_conv, 4 * g + u - 3)
                half = u % 2
                for k in range(KE):
                    last = pe.matmul(bank[u][:, :], wring[:, g % 4, u // 2, k, :], xnT[:, k, half * HALF:(half + 1) * HALF],
                                     start=(k == 0), stop=(k == KE - 1))
                last.then_inc(bcp_done, 1)

            def g_product(g):
                pe.wait_ge(bc_silu, 4 * g + 4)
                pe.wait_ge(g_ready, g)
                if g == 0:
                    pe.wait_ge(decay_ready, 1)
                for t in range(TT):
                    last = pe.matmul(bank[4 + t // HT][:, (t % HT) * P:(t % HT + 1) * P], bt[g % 2][:, t * P:(t + 1) * P],
                                     ct[g % 2][:, t * P:(t + 1) * P], start=True, stop=True)
                last.then_inc(g_done, 1)

            pe.wait_ge(gff_ready, TT)
            for g in range(GROUPS + 1):
                if g < GROUPS:
                    for u in range(4):
                        bc_project(g, u)
                if g >= 1:
                    g_product(g - 1)

            def segments(n):
                pe.wait_ge(r1_ready, n + 1)
                pe.wait_ge(exp_done, n)
                r = r1.rearrange("p t h i -> p (t h i)")
                pe.matmul(bank[4][:, :], later[:, :], r, start=True, stop=False)
                pe.matmul(bank[4][:, :].rearrange("p (a i) -> p a i", i=CS), ident_b[:, :],
                          future[:, None, :].broadcast_to([P, 16, CS]), start=False, stop=True)
                pe.matmul(bank[5][:, :], chunk[:, :], r, start=True, stop=True).then_inc(seg_done, 1)

            def project(i, s, half, done):
                for k in range(KE):
                    last = pe.matmul(bank[i][:, :], wring[:, s % 4, i, k, :], xnT[:, k, half * HALF:(half + 1) * HALF],
                                     start=(k == 0), stop=(k == KE - 1))
                last.then_inc(done, 1)

            pe.wait_ge(g_ready, GROUPS)
            segments(0)
            pe.wait_ge(w_in[0], 32)
            project(0, 0, 0, hid_done)
            project(1, 0, 0, gate_done)

            def zero_sums():
                for i in range(2):
                    pe.matmul(bank[6 + i][:, :], ident_b[:, :], zeros[:, :], start=True, stop=False, skip_group_check=True)

            def body(half, j, last_body):
                for s in range(4):
                    c = 4 * j + s
                    n = c + half * CT
                    over = last_body and s == 3
                    more = not (over and half == 1)
                    pair = 2 * j + s // 2 + half * (CT // 2)
                    pe.wait_ge(hs_ready, n + 1)
                    for t in range(HT):
                        last = pe.transpose(bank[2][:, t * P:(t + 1) * P], hs[:, t * P:(t + 1) * P], ident[:, :])
                    last.then_inc(t_done, 1)
                    if more:
                        pe.wait_ge(w_in[(s + 1) % 4], 32 * (j + (s + 1) // 4 + half * NJ + 1))
                        project(0, s + 1, half + 1 if over else half, hid_done)
                    if s % 2 == 0 and not (last_body and s == 2 and half == 1):
                        segments(pair + 1)
                    if isinstance(j, int) and c == 0:
                        if half == 1:
                            project_out(CT - 1, n - 1, 3)
                    else:
                        if isinstance(j, int) and c == 1:
                            if half == 1:
                                pe.wait_ge(s0_ready, 2)
                            zero_sums()
                        project_out(c - 1, n - 1, s - 1)
                    pe.wait_ge(hT_ready, n + 1)
                    pe.wait_ge(mb_ready, pair + 1)
                    for t in range(HT):
                        for h in range(2):
                            last = pe.matmul(bank[3][HD * h:HD * h + HD, t * P:(t + 1) * P], hT[s % 2][:, t, HD * h:HD * h + HD],
                                             mb[:, s // 2, t, 2 * (s % 2) + h, :], start=True, stop=True, skip_group_check=True)
                    last.then_inc(y_done, 1)
                    if more:
                        pe.wait_ge(sg_ready, n + 1)
                        project(1, s + 1, half + 1 if over else half, gate_done)

            def project_out(c, n, s):
                pe.wait_ge(yg_ready, n + 1)
                w = w_out[:, bass.ds(c, 1), :].rearrange("p a e -> p (a e)")
                for t in range(HT):
                    last = pe.matmul(bank[6 + t // 2][:, (t % 2) * EMB:(t % 2 + 1) * EMB], yg[s % 2][:, t * P:(t + 1) * P],
                                     w, start=False, stop=False, skip_group_check=True)
                last.then_inc(out_done, 1)

            pe.wait_ge(pool_const, 9)
            for half in range(2):
                body(half, 0, False)
                with pe.Fori(1, NJ - 1) as j:
                    body(half, j, False)
                body(half, NJ - 1, True)
            project_out(CT - 1, 2 * CT - 1, 3)
            pe.wait_ge(ssq_done, 2 * CT + 1)
            for t in range(TT):
                last = pe.matmul(bank[0][:, t:t + 1], ssq[:, t // HT, (t % HT) * P:(t % HT + 1) * P], ones[:, 0:1],
                                 start=True, stop=True)
            last.then_inc(ss_done, 1)

            pe.wait_ge(act_step, 8)
            ln_transposes(1)
            pe.wait_ge(attn_in, 16 * 14)
            pe.wait_ge(wvo_in, 32)
            with pe.Fori(0, BATCH) as b:
                pe.wait_ge(xb_ready, b + 1)
                for i, w in enumerate((wq, wk)):
                    for n in range(4):
                        for k in range(KE):
                            last = pe.matmul(bank[2 * i + n // 2][:, (n % 2) * SEQ:(n % 2 + 1) * SEQ],
                                             w[:, k, 4 * n:4 * n + 4, :].rearrange("p h d -> p (h d)"), xb[:, k, :],
                                             start=(k == 0), stop=(k == KE - 1))
                    last.then_inc(qkv_done, 1)
                for i in range(2):
                    for k in range(KE):
                        last = pe.matmul(bank[4][:, i * EMB:(i + 1) * EMB], xb[:, k, i * P:(i + 1) * P], wv[:, k, :],
                                         start=(k == 0), stop=(k == KE - 1))
                last.then_inc(qkv_done, 1)
                pe.wait_ge(qk_ready, 2 * b + 2)
                pe.wait_ge(v_ready, b + 1)

                def scores(h):
                    r, n = h % 4, h // 4
                    if h >= 4:
                        pe.wait_ge(p_ready, b * AH + h - 3)
                    for q in range(2):
                        last = pe.matmul(bank[r][:, q * SEQ:(q + 1) * SEQ], qT[32 * r:32 * r + 32, n, q * P:(q + 1) * P],
                                         kT[32 * r:32 * r + 32, n, :], start=True, stop=True, tile_position=(32 * r, 0))
                    last.then_inc(s_done, 1)

                def turn(h):
                    pe.wait_ge(p_ready, b * AH + h + 1)
                    if h >= 2:
                        pe.wait_ge(pT_ready, b * AH + h - 1)
                    for k in range(2):
                        for q in range(2):
                            last = pe.transpose(bank[4 + h % 2][:, (2 * k + q) * P:(2 * k + q + 1) * P],
                                                pr[h % 2][:, q, k * P:(k + 1) * P], ident[:, :])
                    last.then_inc(pT_done, 1)

                def weigh(h):
                    pe.wait_ge(pT_ready, b * AH + h + 1)
                    for q in range(2):
                        for k in range(2):
                            last = pe.matmul(bank[6][:, q * EMB + h * AD:q * EMB + (h + 1) * AD],
                                             pT[h % 2][:, k, q * P:(q + 1) * P], vb[:, k, h * AD:(h + 1) * AD],
                                             start=(k == 0), stop=(k == 1))
                    last.then_inc(pv_done, 1)

                scores(0)
                scores(1)
                for h in range(AH):
                    if h + 2 < AH:
                        scores(h + 2)
                    turn(h)
                    if h >= 1:
                        weigh(h - 1)
                weigh(AH - 1)
                pe.wait_ge(ob_ready, b + 1)
                for k in range(KE):
                    for q in range(2):
                        last = pe.transpose(bank[7][:, (2 * k + q) * P:(2 * k + q + 1) * P],
                                            ob[:, q, 8 * k:8 * k + 8, :].rearrange("p h d -> p (h d)"), ident[:, :])
                last.then_inc(oT_done, 1)
                pe.wait_ge(oT_ready, b + 1)
                for q in range(2):
                    for k in range(KE):
                        last = pe.matmul(bank[5][:, q * EMB:(q + 1) * EMB], oT[:, k, q * P:(q + 1) * P], wo[:, k, :],
                                         start=(k == 0), stop=(k == KE - 1))
                last.then_inc(wo_done, 1)
            pe.wait_ge(ff_in, 48)
            pe.wait_ge(s1_ready, BATCH)
            with pe.Fori(0, 2) as hf:
                pe.wait_ge(g1_ready, 2 * hf)
                for i in range(2):
                    pe.matmul(bank[6 + i][:, :], ident_b[:, :], zeros[:, :], start=True, stop=False, skip_group_check=True)

                def up(i):
                    gt, m = i // 4, i % 4
                    if i >= 2:
                        pe.wait_ge(hm_ready, 8 * hf + i - 1)
                    for a, w in enumerate((w_gate, w_up)):
                        for k in range(KE):
                            last = pe.matmul(bank[2 * (i % 2) + a][:, :], w[:, k, m, gt, :], xnT[:, k, bass.ds(hf * HALF, HALF)],
                                             start=(k == 0), stop=(k == KE - 1))
                    last.then_inc(gu_done, 1)

                def down(gt):
                    for m in range(4):
                        pe.wait_ge(hk_ready, 8 * hf + 4 * gt + m + 1)
                        for t in range(HT):
                            last = pe.matmul(bank[6 + t // 2][:, (t % 2) * EMB:(t % 2 + 1) * EMB], hk[:, m, t * P:(t + 1) * P],
                                             w_down[:, m, gt, :], start=False, stop=False, skip_group_check=True)
                    last.then_inc(kept_used, 1)

                for i in range(6):
                    up(i)
                down(0)
                up(6)
                up(7)
                down(1)


_F32_INS = {
    "x": (TOK, EMB), "w_in": (EMB, PROJ), "w_out": (INTER, EMB), "conv_w": (P, CONV_T, TAPS), "conv_b": (P, CONV_T),
    "norm_w": (P, CT), "dt_bias": (1, HEADS), "a_log": (1, HEADS), "d": (1, HEADS), "w_router": (EMB, EXPERTS),
    "w_a": (1, EXPERTS), "attr": (1, EXPERTS * EXPERTS), "w_u": (EMB, EXPERTS * RANK), "w_v": (EXPERTS * RANK, EMB),
    "wq": (EMB, EMB), "wk": (EMB, EMB), "wv": (EMB, EMB), "wo": (EMB, EMB), "bq": (4, AD, 4), "bk": (4, AD, 4),
    "bv": (1, EMB), "bo": (1, EMB), "w_gate": (EMB, FF), "w_up": (EMB, FF), "w_down": (FF, EMB),
}

_CONST_INS = {"ident": (P, P), "later": (P, P), "chunk": (P, P), "upto": (P, CS), "diag": (P, CS), "expert_no": (P, EXPERTS)}
_BF16_INS = {"future": (P, CS), "ident_b": (P, P)}


def kernel(**inputs):
    import ml_dtypes
    import numpy as np
    import concourse.bacc as bacc
    from concourse.bass_utils import run_bass_kernel_spmd as run

    a = {k: np.asarray(v) for k, v in inputs.items()}
    m, f = "L0_attn_", "L0_ffn_"
    q, w = "L1_attn_", "L1_ffn_"
    by_member = np.arange(FF).reshape(FF // 4, 4).T.reshape(-1)
    data = {
        "x": a[m + "input_states"].reshape(TOK, EMB),
        "w_in": a[m + "in_proj_w"].T,
        "w_out": a[m + "out_proj_w"].T,
        "conv_w": a[m + "conv_w"].reshape(CONV_T, P, TAPS).transpose(1, 0, 2),
        "conv_b": a[m + "conv_b"].reshape(CONV_T, P).T,
        "norm_w": a[m + "norm_w"].reshape(CT, P).T,
        "dt_bias": a[m + "dt_bias"].reshape(1, HEADS),
        "a_log": a[m + "A_log"].reshape(1, HEADS),
        "d": a[m + "D"].reshape(1, HEADS),
        "w_router": a[f + "Wr"].T,
        "w_a": a[f + "Wa"],
        "attr": a[f + "attr"].reshape(1, EXPERTS * EXPERTS),
        "w_u": a[f + "U"].transpose(1, 0, 2).reshape(EMB, EXPERTS * RANK),
        "w_v": a[f + "V"].reshape(EXPERTS * RANK, EMB),
        "wq": a[q + "Wq"].T, "wk": a[q + "Wk"].T, "wv": a[q + "Wv"].T, "wo": a[q + "Wo"].T,
        "bq": a[q + "bq"].reshape(4, 4, AD).transpose(1, 2, 0),
        "bk": a[q + "bk"].reshape(4, 4, AD).transpose(1, 2, 0),
        "bv": a[q + "bv"].reshape(1, EMB), "bo": a[q + "bo"].reshape(1, EMB),
        "w_gate": a[w + "w_gate"][:, by_member], "w_up": a[w + "w_up"][:, by_member],
        "w_down": a[w + "w_down"][by_member, :],
    }
    k, j = np.arange(P)[:, None], np.arange(P)[None, :]
    same, i = k // CS == j // CS, np.arange(CS)[None, :]
    data["ident"] = (k == j).astype(np.float32)
    data["later"] = (same & (k > j)).astype(np.float32)
    data["chunk"] = same.astype(np.float32)
    data["upto"] = (k % CS <= i).astype(np.float32)
    data["diag"] = (k % CS == i).astype(np.float32)
    data["expert_no"] = np.broadcast_to(np.arange(EXPERTS, dtype=np.float32), (P, EXPERTS))
    data["future"] = np.where(i < k % CS, -30000.0, 0.0).astype(ml_dtypes.bfloat16)
    data["ident_b"] = (k == j).astype(ml_dtypes.bfloat16)

    nc = bacc.Bacc("TRN2", target_bir_lowering=False, num_devices=1)
    arrays, aps = {}, {}
    for name, shape in {**_F32_INS, **_CONST_INS, **_BF16_INS}.items():
        arrays[name + "_dram"] = np.ascontiguousarray(data[name]).reshape(shape)
        dt = BF16 if name in _BF16_INS else F32
        aps[name] = nc.dram_tensor(name + "_dram", shape, dt, kind="ExternalInput").ap()
    out = nc.dram_tensor("out_dram", (TOK, EMB), F32, kind="ExternalOutput").ap()
    build(nc, aps, out)
    r = run(nc, [arrays], core_ids=[0])
    return r.results[0]["out_dram"].reshape(BATCH, SEQ, EMB)
```

```python
from contextlib import ExitStack

import concourse.bass as bass
from concourse import mybir

F32 = mybir.dt.float32
BF16 = mybir.dt.bfloat16
F16 = mybir.dt.float16
U32 = mybir.dt.uint32
ALU = mybir.AluOpType
ACT = mybir.ActivationFunctionType
AX = mybir.AxisListType

P = 128
TOK, BATCH, SEQ, EMB = 1024, 4, 256, 256
TT = TOK // P
KE = EMB // P
HALF = TOK // 2
HT = HALF // P
HEADS, HD, STATE, GROUPS, TAPS, CS = 64, 64, 128, 8, 4, 32
INTER = HEADS * HD
CT = INTER // P
CONV = INTER + 2 * GROUPS * STATE
CONV_T = CONV // P
PROJ = INTER + CONV + HEADS
EXPERTS, RANK = 32, 16
AH, AD = 16, 16
FF = 1024
FT = FF // P
LN_EPS, RMS_EPS = 1e-5, 1e-6
X_SCALE, W_SCALE = 2048.0, 64.0
UNSCALE = 1.0 / (X_SCALE * W_SCALE)


def build(nc, t_in, out):
    ctx = ExitStack()
    with ctx:
        def sb(name, shape, dt=F32):
            return ctx.enter_context(nc.sbuf_tensor(name, shape, dt))

        def sem(name):
            return ctx.enter_context(nc.semaphore(name))

        bank = [ctx.enter_context(nc.psum_tensor(f"bank{i}", [P, 512], F32)) for i in range(8)]

        ident = sb("ident", [P, P])
        later = sb("later", [P, P])
        chunk = sb("chunk", [P, P])
        upto = sb("upto", [P, CS])
        diag = sb("diag", [P, CS])
        future = sb("future", [P, CS], BF16)
        ident_b = sb("ident_b", [P, P], BF16)
        zeros = sb("zeros", [P, 512], BF16)
        ones = sb("ones", [P, 2])
        w_scale = sb("w_scale", [P, 1])
        expert_no = sb("expert_no", [P, EXPERTS])
        conv_w = sb("conv_w_sb", [P, CONV_T, TAPS])
        conv_b = sb("conv_b_sb", [P, CONV_T])
        norm_w = sb("norm_w_sb", [P, CT])
        dt_bias = sb("dt_bias_sb", [P, HEADS])
        a_row = sb("a_row", [P, HEADS])
        d_row = sb("d_row", [P, HEADS])
        dtr16 = sb("dtr16", [P, 2, KE, HEADS + EXPERTS], F16)
        w_a = sb("w_a", [P, EXPERTS])
        wqk16 = sb("wqk16", [P, 2, 2, KE, 4 * P], F16)
        wv16 = sb("wv16", [P, 2, KE, EMB], F16)
        wo = sb("wo", [P, 4, EMB])
        bq = sb("bq_sb", [P, 4])
        bk = sb("bk_sb", [P, 4])
        bq4 = sb("bq4", [P, 4])
        bv = sb("bv_sb", [P, EMB])
        bo = sb("bo_sb", [P, EMB])

        x = sb("x_sb", [P, TT, EMB])
        xn = sb("xn", [P, TT, EMB])
        x16 = [sb(n, [P, KE, TOK], F16) for n in ("xh", "xl")]
        gff = sb("gff", [P, TT, EMB])
        s0 = sb("s0", [P, TT, EMB])
        s1 = sb("s1", [P, TT, EMB])
        adt = sb("adt", [P, TT, HEADS])
        dts = sb("dts", [P, TT, HEADS])
        decay = sb("decay", [P, TT, HEADS])
        gc = sb("gc", [P, TT, GROUPS, CS])
        dd = sb("dd", [P, HEADS, CS])
        ssq = sb("ssq", [P, 2, HALF])
        stats = sb("stats", [P, TT, 6])
        mv = sb("mv", [P, TT, 2])
        sd = sb("sd", [P, TT])
        rstd = sb("rstd", [P, TT])
        wring = sb("wring", [P, 4, 2, KE, P])
        wt16 = sb("wt16", [P, 2, 2, 2, KE, P], F16)
        big = sb("big", [P, 8192])
        w_out = big[:, :].rearrange("p (c e) -> p c e", c=CT)
        w_gu = big[:, 0:4096]
        w_down = big[:, 4096:6144].rearrange("p (m g e) -> p m g e", m=4, g=2)

        AREA = 16384
        area = sb("area", [P, AREA])
        at = [0]

        def carve(n):
            at[0] += n
            return area[:, at[0] - n:at[0]]

        bt = [carve(TOK) for _ in range(2)]
        ct = [carve(TOK) for _ in range(2)]
        cv = [carve(HALF) for _ in range(2)]
        hs = carve(HALF)
        hT = [carve(HALF).rearrange("p (t c) -> p t c", t=HT) for _ in range(2)]
        sg = [carve(HALF) for _ in range(2)]
        yg = [carve(HALF) for _ in range(2)]
        sq = [carve(HALF) for _ in range(2)]
        r1 = carve(HALF).rearrange("p (t h i) -> p t h i", t=HT, h=4)
        e1 = carve(HALF).rearrange("p (t h i) -> p t h i", t=HT, h=4)
        e2 = carve(HALF).rearrange("p (t h i) -> p t h i", t=HT, h=4)
        ms = carve(HALF).rearrange("p (t h i) -> p t h i", t=HT, h=4)
        mc = carve(HALF).rearrange("p (t h i) -> p t h i", t=HT, h=4)
        early = at[0]
        mb = carve(2 * HT * 4 * P).rearrange("p (s t h i) -> p s t h i", s=2, t=HT, h=4)
        assert at[0] <= AREA
        at[0] = 0
        dtr = carve(KE * (HEADS + EXPERTS)).rearrange("p (k c) -> p k c", k=KE)
        attr = carve(EXPERTS * EXPERTS).rearrange("p (a b) -> p a b", a=EXPERTS)
        awt = carve(EXPERTS * EXPERTS).rearrange("p (a b) -> p a b", a=EXPERTS)
        sp = [carve(TT * HEADS).rearrange("p (t h) -> p t h", t=TT) for _ in range(3)]
        assert at[0] <= 4 * TOK
        at[0] = 4 * TOK + 3 * HALF
        hug = [carve(512) for _ in range(2)]
        huT = [carve(512) for _ in range(2)]
        w_v = carve(4 * EMB).rearrange("p (k e) -> p k e", k=4)
        wu16 = carve(KE * EXPERTS * RANK).bitcast(F16).rearrange("p (s k c) -> p s k c", s=2, k=KE)
        at[0] += HALF
        at[0] += 2 * HALF
        sc, pe_, sel0, sel1 = [carve(TT * EXPERTS).rearrange("p (t s) -> p t s", t=TT) for _ in range(4)]
        sel = [sel0, sel1]
        assert at[0] <= early
        w_u = s1[:, 0:4, :].rearrange("p t e -> p (t e)")
        wv = s1[:, 4:6, :]
        wqk = xn[:, :, :].rearrange("p t e -> p (t e)").rearrange("p (w k h d) -> p w k h d", w=2, k=KE, h=AH)
        at[0] = 0
        qT = carve(1024).rearrange("p (n t) -> p n t", n=4)
        kT = carve(1024).rearrange("p (n t) -> p n t", n=4)
        vb = carve(1024).rearrange("p (k h d) -> p k h d", k=2, h=AH)
        pr = [carve(512).rearrange("p (q k) -> p q k", q=2) for _ in range(2)]
        pn = [carve(512).rearrange("p (q k) -> p q k", q=2) for _ in range(2)]
        pT = [carve(512).rearrange("p (k q) -> p k q", k=2) for _ in range(2)]
        oT = carve(1024).rearrange("p (n q) -> p n q", n=4)
        nmx = carve(32).rearrange("p (h q) -> p h q", h=AH)
        den = carve(32).rearrange("p (q h) -> p q h", q=2)
        rden = carve(32).rearrange("p (q h) -> p q h", q=2)
        sgu = [carve(512) for _ in range(2)]
        wgu16 = carve(4096).bitcast(F16).rearrange("p (s a k m g c) -> p s a k m g c", s=2, a=2, k=KE, m=4, g=2)
        hm = s0[:, :, :].rearrange("p t e -> p (t e)").rearrange("p (m t) -> p m t", m=4)
        ha = dd[:, :, :].rearrange("p h i -> p (h i)").rearrange("p (m t) -> p m t", m=4)
        hk = gc[:, :, :, :].rearrange("p t g i -> p (t g i)").rearrange("p (m t) -> p m t", m=4)
        g1 = [carve(512) for _ in range(2)]
        cmpb = carve(1536).bitcast(BF16).rearrange("p (n t) -> p n t", n=6)
        wins = carve(1024).bitcast(BF16).rearrange("p (n t) -> p n t", n=4)
        assert at[0] <= AREA
        eps_ln = sb("eps_ln", [P, 1])
        eps_rms = sb("eps_rms", [P, 1])
        top = sb("top", [P, TT, 8])
        topi = sb("topi", [P, TT, 8], U32)
        topf = sb("topf", [P, TT, 8])
        rsum = [sb(f"rsum{i}", [P, TT]) for i in range(4)]
        aw = sb("aw", [P, EXPERTS])

        x_in = sem("x_in")
        const_in = sem("const_in")
        moe_in = sem("moe_in")
        wout_in = sem("wout_in")
        attn_in = sem("attn_in")
        wv_in = sem("wv_in")
        ff_in = sem("ff_in")
        w_in = [sem(f"w_in{i}") for i in range(4)]
        pool_const = sem("pool_const")
        dve_step = sem("dve_step")
        act_step = sem("act_step")
        ln_tile = sem("ln_tile")
        xT_done = sem("xT_done")
        dt_done = sem("dt_done")
        adt_ready = sem("adt_ready")
        suffix_done = sem("suffix_done")
        decay_ready = sem("decay_ready")
        sc_done = sem("sc_done")
        route_exp = sem("route_exp")
        hu_done = sem("hu_done")
        hug_ready = sem("hug_ready")
        huT_done = sem("huT_done")
        huT_ready = sem("huT_ready")
        moe_done = sem("moe_done")
        gff_ready = sem("gff_ready")
        bcp_done = sem("bcp_done")
        bc_tap = sem("bc_tap")
        bc_conv = sem("bc_conv")
        bc_silu = sem("bc_silu")
        g_done = sem("g_done")
        g_ready = sem("g_ready")
        r1_ready = sem("r1_ready")
        seg_done = sem("seg_done")
        exp_done = sem("exp_done")
        e2d_ready = sem("e2d_ready")
        m_add = sem("m_add")
        m_g = sem("m_g")
        m_dt = sem("m_dt")
        m_ready = sem("m_ready")
        mb_ready = sem("mb_ready")
        hid_done = sem("hid_done")
        gate_done = sem("gate_done")
        tap_done = sem("tap_done")
        conv_done = sem("conv_done")
        hs_ready = sem("hs_ready")
        t_done = sem("t_done")
        hT_ready = sem("hT_ready")
        y_done = sem("y_done")
        sg_ready = sem("sg_ready")
        yg_ready = sem("yg_ready")
        sq_ready = sem("sq_ready")
        ssq_done = sem("ssq_done")
        out_done = sem("out_done")
        s0_ready = sem("s0_ready")
        ss_done = sem("ss_done")
        wh_ready = sem("wh_ready")
        wl_ready = sem("wl_ready")
        early16 = sem("early16")
        attn16 = sem("attn16")
        attn_hi = sem("attn_hi")
        cmp_done = sem("cmp_done")
        wins_ready = sem("wins_ready")
        ff16 = sem("ff16")
        xh_ready = sem("xh_ready")
        x16_ready = sem("x16_ready")
        qkv_done = sem("qkv_done")
        qk_ready = sem("qk_ready")
        v_ready = sem("v_ready")
        s_done = sem("s_done")
        mx_ready = sem("mx_ready")
        p_ready = sem("p_ready")
        pT_done = sem("pT_done")
        pT_ready = sem("pT_ready")
        pv_done = sem("pv_done")
        pn_ready = sem("pn_ready")
        oT_ready = sem("oT_ready")
        wo_done = sem("wo_done")
        s1_ready = sem("s1_ready")
        gate_up_done = sem("gate_up_done")
        sgu_ready = sem("sgu_ready")
        hm_ready = sem("hm_ready")
        ha_ready = sem("ha_ready")
        hk_ready = sem("hk_ready")
        g1_ready = sem("g1_ready")
        y_ready = sem("y_ready")
        y_out = sem("y_out")
        chain = sem("chain")
        conv_step = sem("conv_step")
        rden_ready = sem("rden_ready")
        ff_step = sem("ff_step")
        kept_used = sem("kept_used")
        fin_step = sem("fin_step")

        x_dram = t_in["x"].rearrange("(t p) e -> p t e", p=P)
        out_dram = out.rearrange("(t p) e -> p t e", p=P)
        win_dram = t_in["w_in"].rearrange("(k p) c -> p k c", p=P)
        NJ = CT // 4
        block = ctx.enter_context(nc.Block())

        @block.sync
        def _(sp_):
            sp_.dma_start(x[:, 0:HT, :], x_dram[:, 0:HT, :]).then_inc(x_in, 16)
            sp_.dma_start(x[:, HT:TT, :], x_dram[:, HT:TT, :]).then_inc(x_in, 16)
            for dst, name in ((ident, "ident"), (later, "later"), (chunk, "chunk"), (upto, "upto"), (diag, "diag"),
                              (future, "future"), (ident_b, "ident_b"), (expert_no, "expert_no"),
                              (conv_b, "conv_b"), (norm_w, "norm_w")):
                sp_.dma_start(dst[:, :], t_in[name]).then_inc(const_in, 16)
            sp_.dma_start(conv_w[:, :, :], t_in["conv_w"]).then_inc(const_in, 16)
            for dst, name in ((dt_bias, "dt_bias"), (a_row, "a_log"), (d_row, "d")):
                sp_.dma_start(dst[:, :], t_in[name].partition_broadcast(P)).then_inc(const_in, 16)
            sp_.dma_start(dtr[:, :, 0:HEADS], win_dram[:, :, INTER + CONV:PROJ]).then_inc(const_in, 16)
            sp_.dma_start(dtr[:, :, HEADS:HEADS + EXPERTS], t_in["w_router"].rearrange("(k p) s -> p k s", p=P)).then_inc(const_in, 16)
            sp_.dma_start(w_a[:, :], t_in["w_a"].partition_broadcast(P)).then_inc(moe_in, 16)
            sp_.dma_start(attr.rearrange("p a b -> p (a b)"), t_in["attr"].partition_broadcast(P)).then_inc(moe_in, 16)
            sp_.dma_start(w_u.rearrange("p (k s) -> p k s", k=KE), t_in["w_u"].rearrange("(k p) s -> p k s", p=P)).then_inc(moe_in, 16)
            sp_.dma_start(w_v, t_in["w_v"].rearrange("(k p) e -> p k e", p=P)).then_inc(moe_in, 16)
            base = 2 * INTER
            for g in range(GROUPS):
                if g >= 4:
                    sp_.wait_ge(wl_ready, g - 3)
                for i in range(2):
                    c0 = base + (i * GROUPS + g) * P
                    sp_.dma_start(wring[:, g % 4, i, :, :], win_dram[:, :, c0:c0 + P]).then_inc(w_in[g % 4], 16)
                if g == 3:
                    sp_.dma_start(w_out, t_in["w_out"].rearrange("(c p) e -> p c e", p=P)).then_inc(wout_in, 16)
                    sp_.dma_start(wv, t_in["wv"].rearrange("(k p) e -> p k e", p=P)).then_inc(wv_in, 16)
            for half in range(2):
                with sp_.Fori(0, NJ) as j:
                    for s in range(4):
                        sp_.wait_ge(wl_ready, 4 * j + (s + half * CT + GROUPS - 3))
                        sp_.dma_start(wring[:, s, 0, :, :], win_dram[:, :, bass.ds(j * (4 * P) + (INTER + s * P), P)]).then_inc(w_in[s], 16)
                        sp_.dma_start(wring[:, s, 1, :, :], win_dram[:, :, bass.ds(j * (4 * P) + s * P, P)]).then_inc(w_in[s], 16)
            sp_.wait_ge(out_done, 2 * CT)
            sp_.dma_start(big[:, 0:2048].rearrange("p (k c) -> p k c", k=KE),
                          t_in["w_gate"].rearrange("(k p) c -> p k c", p=P)).then_inc(ff_in, 16)
            sp_.dma_start(big[:, 2048:4096].rearrange("p (k c) -> p k c", k=KE),
                          t_in["w_up"].rearrange("(k p) c -> p k c", p=P)).then_inc(ff_in, 16)
            sp_.dma_start(big[:, 4096:6144].rearrange("p (k c) -> p k c", k=FT),
                          t_in["w_down"].rearrange("(k p) c -> p k c", p=P)).then_inc(ff_in, 16)
            for h in range(2):
                sp_.wait_ge(y_ready, 2 * h + 2)
                sp_.dma_start(out_dram[:, h * HT:(h + 1) * HT, :], s1[:, h * HT:(h + 1) * HT, :]).then_inc(y_out, 16)
            sp_.wait_ge(y_out, 32)

        @block.gpsimd
        def _(pool):
            pool.memset(ones[:, :], 1.0).then_inc(pool_const, 1)
            pool.memset(zeros[:, :], 0.0).then_inc(pool_const, 1)
            pool.memset(w_scale[:, :], W_SCALE).then_inc(pool_const, 1)
            pool.memset(wo[:, :, :], 0.0).then_inc(pool_const, 1)
            pool.memset(bq[:, :], 0.0).then_inc(pool_const, 1)
            pool.memset(bk[:, :], 0.0).then_inc(pool_const, 1)
            pool.memset(ssq[:, :, :], 0.0).then_inc(ssq_done, 1)
            pool.memset(mb[:, :, :, :, :], 0.0).then_inc(pool_const, 1)
            def hi_part(raw_slot, slot, landed):
                pool.wait_ge(w_in[raw_slot], landed)
                pool.tensor_tensor(wt16[:, slot, 0, :, :, :].rearrange("p a k c -> p (a k c)"),
                                   wring[:, raw_slot, :, :, :].rearrange("p a k c -> p (a k c)"),
                                   w_scale[:, :].broadcast_to([P, 2 * KE * P]), ALU.mult)\
                    .then_inc(wh_ready, 1)

            pool.wait_ge(pool_const, 3)
            hi_part(0, 0, 32)
            hi_part(1, 1, 32)
            pool.wait_ge(const_in, 16 * 16)
            pool.tensor_tensor(dd[:, :, :], diag[:, None, :].broadcast_to([P, HEADS, CS]),
                               d_row[:, :, None].broadcast_to([P, HEADS, CS]), ALU.mult).then_inc(pool_const, 1)
            pool.wait_ge(xT_done, 1)
            pool.memset(wqk, 0.0).then_inc(pool_const, 1)
            pool.wait_ge(pool_const, 9)
            for i, name in ((0, "wq"), (1, "wk")):
                for k in range(KE):
                    pool.dma_start(wqk[:, i, k, :, 0:AD], t_in[name][k * P:(k + 1) * P, :].rearrange("p (h d) -> p h d", h=AH))\
                        .then_inc(attn_in, 16)
            for b, name in ((bq, "bq"), (bk, "bk")):
                for r in range(4):
                    pool.dma_start(b[32 * r:32 * r + AD, :], t_in[name][r]).then_inc(attn_in, 16)
            wo_dram = t_in["wo"].rearrange("(n r d) e -> r d n e", n=4, r=4)
            for r in range(4):
                pool.dma_start(wo[32 * r:32 * r + AD, :, :], wo_dram[r]).then_inc(attn_in, 16)
            pool.dma_start(bv[:, :], t_in["bv"].partition_broadcast(P)).then_inc(attn_in, 16)
            pool.dma_start(bo[:, :], t_in["bo"].partition_broadcast(P)).then_inc(attn_in, 16)
            pool.wait_ge(attn_in, 16 * 18)
            pool.tensor_tensor(wqk16[:, 0, :, :, :].rearrange("p w k c -> p (w k c)"), wqk.rearrange("p w k h d -> p (w k h d)"),
                               w_scale[:, :].broadcast_to([P, 2 * KE * 4 * P]), ALU.mult).then_inc(attn_hi, 1)
            pool.wait_ge(wv_in, 16)
            pool.tensor_tensor(wv16[:, 0, :, :], wv, w_scale[:, :, None].broadcast_to([P, KE, EMB]), ALU.mult).then_inc(attn_hi, 1)
            pool.wait_ge(adt_ready, 1)

            def mask_a(half, p):
                a = adt[:, half * HT:(half + 1) * HT, bass.ds(4 * p, 4)]
                return pool.tensor_tensor(r1, a[:, :, :, None].broadcast_to([P, HT, 4, CS]),
                                          upto[:, None, None, :].broadcast_to([P, HT, 4, CS]), ALU.mult)

            def m_first(half, p, n):
                pool.wait_ge(exp_done, n + 1)
                e = decay[:, half * HT:(half + 1) * HT, bass.ds(4 * p, 4)]
                pool.tensor_tensor(e2, e2, e[:, :, :, None].broadcast_to([P, HT, 4, CS]), ALU.mult).then_inc(e2d_ready, 1)

            def m_last(half, p, n):
                pool.wait_ge(m_g, n + 1)
                e = dts[:, half * HT:(half + 1) * HT, bass.ds(4 * p, 4)]
                pool.tensor_tensor(ms, ms, e[:, :, :, None].broadcast_to([P, HT, 4, CS]), ALU.mult).then_inc(m_dt, 1)
                pool.wait_ge(m_dt, n + 1)
                pool.wait_ge(mb_ready, n)
                d = dd[:, bass.ds(4 * p, 4), :]
                pool.tensor_tensor(mc, ms, d[:, None, :, :].broadcast_to([P, HT, 4, CS]), ALU.add).then_inc(m_ready, 1)

            def add_square(half, n, s):
                pool.wait_ge(sq_ready, n + 1)
                pool.wait_ge(ssq_done, n + 1)
                pool.tensor_tensor(ssq[:, half, :], ssq[:, half, :], sq[s % 2], ALU.add).then_inc(ssq_done, 1)

            for w in range(2, GROUPS + 2):
                pool.wait_ge(bcp_done, 4 * (w - 1))
                hi_part(w % 4, w % 2, 32 * (w // 4 + 1))
                if w >= GROUPS - 2:
                    pool.wait_ge(wout_in, 16)
                    c = slice((w - GROUPS + 2) * (CT // 4), (w - GROUPS + 3) * (CT // 4))
                    pool.tensor_tensor(w_out[:, c, :], w_out[:, c, :], norm_w[:, c, None].broadcast_to([P, CT // 4, EMB]), ALU.mult)\
                        .then_inc(pool_const, 1)
                if w == 2:
                    mask_a(0, 0).then_inc(r1_ready, 1)
                    pool.wait_ge(decay_ready, 1)
                    m_first(0, 0, 0)
                    pool.wait_ge(seg_done, 1)
                    mask_a(0, 1).then_inc(r1_ready, 1)

            m_last(0, 0, 0)

            def tile_after_next(half, j, s):
                pool.wait_ge(gate_done, 4 * j + s + half * CT + 1)
                hi_part((s + 2) % 4, s % 2, 32 * (j + (s + 2) // 4 + half * NJ + 3))

            def body(half, j, last):
                for q in range(2):
                    pair = 2 * j + q
                    n = pair + half * (CT // 2)
                    over = last and q == 1
                    build_next = not (over and half == 1)
                    if build_next:
                        nh, npair = (half + 1, 0) if over else (half, pair + 1)
                        tile_after_next(half, j, 2 * q)
                    if not (isinstance(n, int) and n == 0):
                        add_square(half - (isinstance(j, int) and j == 0 and q == 0), 2 * n - 1, 1)
                    if build_next:
                        m_first(nh, npair, n + 1)
                        m_last(nh, npair, n + 1)
                        tile_after_next(half, j, 2 * q + 1)
                    if not (last and half == 1):
                        pool.wait_ge(seg_done, n + 2)
                        mask_a(half + 1 if last else half, q if last else pair + 2).then_inc(r1_ready, 1)
                    add_square(half, 2 * n, 0)

            for half in range(2):
                body(half, 0, False)
                with pool.Fori(1, NJ - 1) as j:
                    body(half, j, False)
                body(half, NJ - 1, True)
            add_square(1, 2 * CT - 1, 1)

            with pool.Fori(0, 2) as hf:
                for gt in range(2):
                    b = 2 * hf + gt
                    for h in range(AH):
                        if h >= 2:
                            pool.wait_ge(pT_done, b * AH + h - 1)
                        pool.wait_ge(rden_ready, b * AH + h + 1)
                        pool.tensor_tensor(pn[h % 2], pr[h % 2], rden[:, :, h, None].broadcast_to([P, 2, SEQ]), ALU.mult)\
                            .then_inc(pn_ready, 1)

        @block.scalar
        def _(act):
            act.wait_ge(dve_step, 1)
            act.activation(sd[:, :], mv[:, :, 1], ACT.Sqrt, bias=eps_ln[:, :]).then_inc(act_step, 1)
            act.wait_ge(xT_done, 1)
            for i in range(4):
                act.activation(x16[0][:, i // 2, (i % 2) * HALF:(i % 2 + 1) * HALF], bank[i][:, :], ACT.Copy, scale=X_SCALE)\
                    .then_inc(xh_ready, 1)
            act.wait_ge(dve_step, 2)
            act.activation(sp[1], sp[0], ACT.Abs).then_inc(act_step, 1)
            act.wait_ge(act_step, 2)
            act.activation(sp[1], sp[1], ACT.Exp, scale=-1.0).then_inc(act_step, 1)
            act.wait_ge(const_in, 16 * 16)
            act.activation(a_row[:, :], a_row[:, :], ACT.Exp).then_inc(act_step, 1)
            act.wait_ge(dve_step, 3)
            act.activation(decay[:, :, :], sp[2], ACT.Ln).then_inc(act_step, 1)
            act.wait_ge(suffix_done, 1)
            act.activation(decay[:, :, :], bank[5][:, :], ACT.Exp).then_inc(decay_ready, 1)
            act.wait_ge(route_exp, 1)
            act.activation(pe_, pe_, ACT.Exp).then_inc(act_step, 1)
            act.activation(aw[:, :], aw[:, :], ACT.Exp, scale=-1.0).then_inc(act_step, 1)
            def exps(n):
                act.wait_ge(seg_done, n + 1)
                if not isinstance(n, int) or n > 0:
                    act.wait_ge(m_add, n)
                act.activation(e1, bank[4][:, :].rearrange("p (t h i) -> p t h i", t=HT, h=4), ACT.Exp)
                act.activation(e2, bank[5][:, :].rearrange("p (t h i) -> p t h i", t=HT, h=4), ACT.Exp).then_inc(exp_done, 1)

            def bc_first_tap(g, u):
                act.wait_ge(bcp_done, 4 * g + u + 1)
                if 4 * g + u >= 2:
                    act.wait_ge(bc_silu, 4 * g + u - 1)
                tile = INTER // P + (u // 2) * GROUPS + g
                act.activation(cv[u % 2], bank[u][:, :], ACT.Identity, scale=conv_w[:, tile, TAPS - 1:TAPS],
                               bias=conv_b[:, tile:tile + 1]).then_inc(bc_tap, 1)

            def bc_silu_of(g, u):
                act.wait_ge(bc_conv, 4 * g + u + 1)
                dst = (bt, ct)[u // 2][g % 2]
                act.activation(dst[:, (u % 2) * HALF:(u % 2 + 1) * HALF], cv[u % 2], ACT.Silu).then_inc(bc_silu, 1)

            def g_blocks(g):
                act.wait_ge(g_done, g + 1)
                for i in range(2):
                    src = bank[4 + i][:, :].rearrange("p (t c) -> p t c", t=HT)
                    for q in range(4):
                        last = act.activation(gc[32 * q:32 * q + 32, i * HT:(i + 1) * HT, g, :],
                                              src[32 * q:32 * q + 32, :, 32 * q:32 * q + 32], ACT.Copy)
                last.then_inc(g_ready, 1)

            for g in range(GROUPS + 1):
                for u in range(4):
                    if g < GROUPS:
                        bc_first_tap(g, u)
                    if (g, u) != (0, 0) and (g < GROUPS or u == 0):
                        bc_silu_of(g if u else g - 1, (u - 1) % 4)
                    if g < TT and u == 1:
                        act.wait_ge(huT_done, g + 1)
                        act.activation(huT[g % 2], bank[7][:, :], ACT.Copy).then_inc(huT_ready, 1)
                if g == 0:
                    exps(0)
                if g >= 1:
                    g_blocks(g - 1)
                if g < TT:
                    act.wait_ge(moe_done, g + 1)
                    act.activation(gff[:, g, :], bank[6][:, 0:EMB], ACT.Silu).then_inc(gff_ready, 1)

            def first_tap(c, n):
                act.wait_ge(hid_done, n + 1)
                if not isinstance(n, int) or n > 0:
                    act.wait_ge(hs_ready, n)
                act.activation(cv[0], bank[0][:, :], ACT.Identity, scale=conv_w[:, bass.ds(c, 1), TAPS - 1],
                               bias=conv_b[:, bass.ds(c, 1)]).then_inc(tap_done, 1)

            def silu_gate(n, s):
                act.wait_ge(gate_done, n + 1)
                act.activation(sg[s % 2], bank[1][:, :], ACT.Silu, scale=UNSCALE).then_inc(sg_ready, 1)

            def silu_hidden(n):
                act.wait_ge(conv_done, n + 1)
                act.activation(hs, cv[0], ACT.Silu).then_inc(hs_ready, 1)

            def place(n, q):
                act.wait_ge(m_ready, n + 1)
                if isinstance(n, int) and n == 0:
                    act.wait_ge(pool_const, 9)
                else:
                    act.wait_ge(y_done, 2 * n - 1)
                for r in range(4):
                    last = act.activation(mb[32 * r:32 * r + 32, q % 2, :, :, 32 * r:32 * r + 32],
                                          mc[32 * r:32 * r + 32, :, :, :], ACT.Copy)
                last.then_inc(mb_ready, 1)

            def square(n, s):
                act.wait_ge(yg_ready, n + 1)
                if not isinstance(n, int) or n > 1:
                    act.wait_ge(ssq_done, n)
                act.activation(sq[s % 2], yg[s % 2], ACT.Square).then_inc(sq_ready, 1)

            act.wait_ge(bc_silu, 4 * GROUPS - 1)
            first_tap(0, 0)
            silu_hidden(0)
            place(0, 0)

            def body(half, j, last):
                for s in range(4):
                    c = 4 * j + s
                    n = c + half * CT
                    over = last and s == 3
                    more = not (over and half == 1)
                    pair = 2 * j + (s // 2) + half * (CT // 2)
                    build_next = not (last and s >= 2 and half == 1)
                    if more:
                        first_tap(0 if over else c + 1, n + 1)
                    silu_gate(n, s)
                    if not (isinstance(n, int) and n == 0):
                        square(n - 1, s + 1)
                    if s % 2 == 0 and build_next:
                        exps(pair + 1)
                    if more:
                        silu_hidden(n + 1)
                    if s % 2 == 1 and build_next:
                        place(pair + 1, s // 2 + 1)

            for half in range(2):
                body(half, 0, False)
                with act.Fori(1, NJ - 1) as j:
                    body(half, j, False)
                body(half, NJ - 1, True)
            square(2 * CT - 1, 3)

            act.wait_ge(ss_done, 1)
            act.activation(rstd[:, :], bank[0][:, 0:TT], ACT.Sqrt, scale=1.0 / INTER, bias=eps_rms[:, :]).then_inc(act_step, 1)
            act.wait_ge(dve_step, 4)
            act.activation(sd[:, :], mv[:, :, 1], ACT.Sqrt, bias=eps_ln[:, :]).then_inc(act_step, 1)
            act.wait_ge(xT_done, 2)
            for i in range(4):
                act.activation(x16[0][:, i // 2, (i % 2) * HALF:(i % 2 + 1) * HALF], bank[i][:, :], ACT.Copy, scale=X_SCALE)\
                    .then_inc(xh_ready, 1)
            act.wait_ge(attn_in, 16 * 18)
            act.mul(bq4[:, :], bq[:, :], 0.25).then_inc(act_step, 1)
            act.wait_ge(act_step, 10)
            with act.Fori(0, 2) as hf:
                for gt in range(2):
                    b = u = 2 * hf + gt
                    for i in range(4):
                        act.wait_ge(qkv_done, 5 * b + i + 1)
                        for n in range(2):
                            last = act.activation((qT, kT)[i // 2][:, 2 * (i % 2) + n, :], bank[i % 3][:, n * SEQ:(n + 1) * SEQ],
                                                  ACT.Identity, scale=UNSCALE * (0.25, 1.0)[i // 2],
                                                  bias=(bq4, bk)[i // 2][:, 2 * (i % 2) + n:2 * (i % 2) + n + 1])
                        last.then_inc(qk_ready, 1)
                    for h in range(AH):
                        act.wait_ge(mx_ready, b * AH + h + 1)
                        if h >= 2:
                            act.wait_ge(pn_ready, b * AH + h - 1)
                        for q in range(2):
                            last = act.activation(pr[h % 2][:, q, :], bank[h % 2][:, q * SEQ:(q + 1) * SEQ], ACT.Exp,
                                                  bias=nmx[:, h, q:q + 1], accum_out=den[:, q, h:h + 1])
                        last.then_inc(p_ready, 1)
                        if h in (4, 5, 7, 8):
                            m = (4, 5, 7, 8).index(h)
                            act.wait_ge(hm_ready, 4 * u + m + 1)
                            act.activation(ha[:, m, :], hm[:, m, :], ACT.Abs).then_inc(ha_ready, 1)
                        if h in (0, 4):
                            for m in (h // 2, h // 2 + 1):
                                act.wait_ge(gate_up_done, 8 * u + 2 * h // 2 + m % 2 + 1)
                                act.activation(sgu[m % 2], bank[4 + m % 2][:, :], ACT.Silu, scale=UNSCALE).then_inc(sgu_ready, 1)
                    for i in range(2):
                        act.wait_ge(pv_done, b * AH + 8 * i + 8)
                        act.activation(oT[:, 2 * i:2 * i + 2, :].rearrange("p n q -> p (n q)"), bank[3 + i][:, :], ACT.Copy)\
                            .then_inc(oT_ready, 1)
                act.wait_ge(kept_used, 2 * hf + 2)
                for i in range(2):
                    act.activation(g1[i], bank[6 + i][:, :], ACT.Silu).then_inc(g1_ready, 1)

        @block.vector
        def _(dve):
            steps = [0]

            def link(ins):
                ins.then_inc(chain, 1)
                steps[0] += 1
                dve.wait_ge(chain, steps[0])

            dve.memset(eps_ln[:, :], LN_EPS)
            link(dve.memset(eps_rms[:, :], RMS_EPS))

            def ln_stats():
                for t in range(TT):
                    link_last = dve.bn_stats(stats[:, t, :], x[:, t, :])
                link(link_last)
                for t in range(TT):
                    link_last = dve.bn_aggr(mv[:, t, :], stats[:, t, :])
                link_last.then_inc(dve_step, 1)

            def lo_part(slot, raw_slot, w):
                dve.wait_ge(wh_ready, w + 1)
                dve.scalar_tensor_tensor(wt16[:, slot, 1, :, :, :].rearrange("p a k c -> p (a k c)"),
                                         wring[:, raw_slot, :, :, :].rearrange("p a k c -> p (a k c)"), W_SCALE,
                                         wt16[:, slot, 0, :, :, :].rearrange("p a k c -> p (a k c)"),
                                         ALU.mult, ALU.subtract).then_inc(wl_ready, 1)

            def split(hi, lo, raw):
                link(dve.tensor_scalar(hi, raw, W_SCALE, None, ALU.mult))
                return dve.scalar_tensor_tensor(lo, raw, W_SCALE, hi, ALU.mult, ALU.subtract)

            def x_lo(n):
                for i in range(4):
                    dve.wait_ge(xh_ready, 4 * n + i + 1)
                    d = (slice(None), i // 2, slice((i % 2) * HALF, (i % 2 + 1) * HALF))
                    dve.scalar_tensor_tensor(x16[1][d], bank[i][:, :], X_SCALE, x16[0][d], ALU.mult, ALU.subtract)\
                        .then_inc(x16_ready, 1)

            def ln_apply():
                link(dve.reciprocal(rstd[:, :], sd[:, :]))
                for t in range(TT):
                    dve.tensor_scalar(xn[:, t, :], x[:, t, :], mv[:, t, 0:1], rstd[:, t:t + 1],
                                      ALU.subtract, ALU.mult).then_inc(ln_tile, 1)

            dve.wait_ge(x_in, 32)
            ln_stats()
            dve.wait_ge(act_step, 1)
            ln_apply()
            dve.wait_ge(const_in, 16 * 16)
            split(dtr16[:, 0, :, :], dtr16[:, 1, :, :], dtr).then_inc(early16, 1)
            link(dve.tensor_scalar(conv_w[:, :, :], conv_w[:, :, :], UNSCALE, None, ALU.mult))
            x_lo(0)
            dve.wait_ge(moe_in, 16 * 4)
            split(wu16[:, 0, :, :].rearrange("p k c -> p (k c)"), wu16[:, 1, :, :].rearrange("p k c -> p (k c)"), w_u)\
                .then_inc(early16, 1)
            dve.wait_ge(dt_done, 1)
            dve.scalar_tensor_tensor(sp[0], bank[4][:, :].rearrange("p (t h) -> p t h", t=TT), UNSCALE,
                                     dt_bias[:, None, :].broadcast_to([P, TT, HEADS]), ALU.mult, ALU.add).then_inc(dve_step, 1)
            dve.wait_ge(act_step, 3)
            dve.tensor_scalar(sp[2], sp[1], 1.0, None, ALU.add).then_inc(dve_step, 1)
            dve.wait_ge(dve_step, 3)
            link(dve.tensor_scalar(adt[:, :, :], sp[2], -1.0, 1e-30, ALU.add, ALU.max))
            link(dve.reciprocal(dts[:, :, :], adt[:, :, :]))
            link(dve.tensor_tensor(dts[:, :, :], dts[:, :, :], sp[1], ALU.mult))
            dve.wait_ge(act_step, 5)
            link(dve.tensor_tensor(dts[:, :, :], dts[:, :, :], decay[:, :, :], ALU.mult))
            link(dve.tensor_scalar(adt[:, :, :], sp[2], 1.0, None, ALU.is_equal))
            link(dve.tensor_tensor(adt[:, :, :], adt[:, :, :], sp[1], ALU.mult))
            link(dve.tensor_tensor(dts[:, :, :], dts[:, :, :], adt[:, :, :], ALU.add))
            link(dve.scalar_tensor_tensor(dts[:, :, :], sp[0], 0.0, dts[:, :, :], ALU.max, ALU.add))
            link(dve.tensor_scalar(a_row[:, :], a_row[:, :], -1.0, None, ALU.mult))
            dve.tensor_tensor(adt[:, :, :], dts[:, :, :], a_row[:, None, :].broadcast_to([P, TT, HEADS]),
                              ALU.mult).then_inc(adt_ready, 1)

            lo_part(0, 0, 0)
            lo_part(1, 1, 1)
            dve.wait_ge(sc_done, 1)
            link(dve.tensor_scalar(sc, bank[7][:, 0:TT * EXPERTS].rearrange("p (t s) -> p t s", t=TT), UNSCALE, None, ALU.mult))
            for t in range(TT):
                last = dve.max(top[:, t, :], sc[:, t, :])
            link(last)
            for t in range(TT):
                last = dve.max_index(topi[:, t, :], top[:, t, :], sc[:, t, :])
            link(last)
            dve.tensor_tensor(pe_, sc, top[:, :, 0:1].broadcast_to([P, TT, EXPERTS]), ALU.subtract)
            dve.wait_ge(moe_in, 16 * 4)
            link(dve.tensor_tensor(awt, attr, w_a[:, None, :].broadcast_to([P, EXPERTS, EXPERTS]), ALU.mult))
            link(dve.tensor_reduce(aw[:, :], awt, AX.X, ALU.add))
            link(dve.tensor_copy(topf[:, :, :], topi[:, :, :]))
            dve.tensor_copy(rsum[3][:, :], topf[:, :, 0]).then_inc(route_exp, 1)
            for i in range(2):
                last = dve.tensor_tensor(sel[i], expert_no[:, None, :].broadcast_to([P, TT, EXPERTS]),
                                         topf[:, :, i:i + 1].broadcast_to([P, TT, EXPERTS]), ALU.is_equal)
            link(last)
            link(dve.tensor_tensor(sel[0], sel[0], sel[1], ALU.add))
            dve.wait_ge(act_step, 7)
            link(dve.tensor_scalar(aw[:, :], aw[:, :], 1.0, None, ALU.add))
            link(dve.reciprocal(aw[:, :], aw[:, :]))
            link(dve.tensor_reduce(rsum[0][:, :], pe_, AX.X, ALU.add))
            link(dve.reciprocal(rsum[1][:, :], rsum[0][:, :]))
            link(dve.tensor_tensor(pe_, pe_, rsum[1][:, :, None].broadcast_to([P, TT, EXPERTS]), ALU.mult))
            link(dve.tensor_tensor(pe_, pe_, sel[0], ALU.mult))
            link(dve.tensor_reduce(rsum[0][:, :], pe_, AX.X, ALU.add))
            link(dve.tensor_scalar(rsum[0][:, :], rsum[0][:, :], 1e-8, None, ALU.add))
            link(dve.reciprocal(rsum[1][:, :], rsum[0][:, :]))
            link(dve.tensor_tensor(pe_, pe_, rsum[1][:, :, None].broadcast_to([P, TT, EXPERTS]), ALU.mult))
            link(dve.tensor_tensor(sel[1], pe_, aw[:, None, :].broadcast_to([P, TT, EXPERTS]), ALU.mult))
            link(dve.tensor_reduce(rsum[2][:, :], sel[1], AX.X, ALU.add))
            link(dve.tensor_scalar(rsum[2][:, :], rsum[2][:, :], 0.2, 0.9, ALU.mult, ALU.add))
            link(dve.tensor_scalar(rsum[2][:, :], rsum[2][:, :], UNSCALE, None, ALU.mult))
            link(dve.tensor_tensor(pe_, pe_, rsum[2][:, :, None].broadcast_to([P, TT, EXPERTS]), ALU.mult))
            def weigh_experts(t):
                dve.wait_ge(hu_done, t + 1)
                dve.tensor_tensor(hug[t % 2].rearrange("p (s r) -> p s r", s=EXPERTS),
                                  bank[6][:, :].rearrange("p (s r) -> p s r", s=EXPERTS),
                                  pe_[:, t, :, None].broadcast_to([P, EXPERTS, RANK]), ALU.mult).then_inc(hug_ready, 1)

            def conv(dst, src, w, last_sem):
                d = dst.rearrange("p (b t) -> p b t", b=2)
                s = src.rearrange("p (b t) -> p b t", b=2)
                for k in range(1, TAPS):
                    ins = dve.scalar_tensor_tensor(d[:, :, k:SEQ], s[:, :, 0:SEQ - k], w(TAPS - 1 - k),
                                                   d[:, :, k:SEQ], ALU.mult, ALU.add)
                    if k < TAPS - 1:
                        yield ins
                ins.then_inc(last_sem, 1)

            def attn_lo(i):
                dve.wait_ge(attn_hi, 2)
                if i < 4:
                    hi, lo = [wqk16[:, part, i // 2, i % 2, :] for part in range(2)]
                    raw = wqk[:, i // 2, i % 2, :, :].rearrange("p h d -> p (h d)")
                else:
                    hi, lo = [wv16[:, part, :, :] for part in range(2)]
                    raw = wv
                dve.scalar_tensor_tensor(lo, raw, W_SCALE, hi, ALU.mult, ALU.subtract).then_inc(attn16, 1)

            for g in range(GROUPS):
                for u in range(4):
                    if u == 3:
                        lo_part(g % 2, (g + 2) % 4, g + 2)
                    dve.wait_ge(bc_tap, 4 * g + u + 1)
                    tile = INTER // P + (u // 2) * GROUPS + g
                    for ins in conv(cv[u % 2], bank[u][:, :], lambda k: conv_w[:, tile, k:k + 1], bc_conv):
                        link(ins)
                    if u == 0:
                        weigh_experts(g)
                    if u == 3 and g >= 3:
                        attn_lo(g - 3)

            def transposed(n, s):
                dve.wait_ge(t_done, n + 1)
                dve.tensor_copy(hT[s % 2], bank[2][:, :].rearrange("p (t c) -> p t c", t=HT)).then_inc(hT_ready, 1)

            def hidden_conv(c, n):
                dve.wait_ge(tap_done, n + 1)
                k = 0
                for ins in conv(cv[0], bank[0][:, :], lambda k: conv_w[:, bass.ds(c, 1), k], conv_done):
                    k += 1
                    ins.then_inc(conv_step, 1)
                    dve.wait_ge(conv_step, 2 * n + k)

            def gated(n, s):
                dve.wait_ge(y_done, n + 1)
                dve.wait_ge(sg_ready, n + 1)
                dve.tensor_tensor(yg[s % 2], bank[3][:, :], sg[s % 2], ALU.mult).then_inc(yg_ready, 1)

            def m_middle(n, q, half):
                dve.wait_ge(e2d_ready, n + 1)
                dve.wait_ge(m_ready, n)
                dve.tensor_tensor(ms, e1, e2, ALU.add).then_inc(m_add, 1)
                dve.wait_ge(m_add, n + 1)
                if isinstance(n, int) and n == 0:
                    dve.wait_ge(g_ready, GROUPS)
                g0 = 4 * (q % 2)
                dve.tensor_tensor(ms, ms, gc[:, half * HT:(half + 1) * HT, g0:g0 + 4, :], ALU.mult).then_inc(m_g, 1)

            hidden_conv(0, 0)
            m_middle(0, 0, 0)

            def keep_sums(half):
                dve.wait_ge(out_done, (half + 1) * CT)
                for i in range(2):
                    t0 = half * HT + 2 * i
                    dve.tensor_copy(s0[:, t0:t0 + 2, :], bank[6 + i][:, :].rearrange("p (t e) -> p t e", t=2)).then_inc(s0_ready, 1)

            def body(half, j, last):
                for s in range(4):
                    c = 4 * j + s
                    n = c + half * CT
                    over = last and s == 3
                    transposed(n, s)
                    if not (over and half == 1):
                        hidden_conv(0 if over else c + 1, n + 1)
                    if not (last and s >= 2 and half == 1):
                        lo_part(s % 2, (s + 2) % 4, n + 2 + GROUPS)
                    gated(n, s)
                    if half == 1 and isinstance(j, int) and c == 0:
                        keep_sums(0)
                    if s % 2 == 0 and not (last and s == 2 and half == 1):
                        over = last and s == 2
                        m_middle(2 * j + s // 2 + 1 + half * (CT // 2), s // 2 + 1, half + 1 if over else half)

            for half in range(2):
                body(half, 0, False)
                with dve.Fori(1, NJ - 1) as j:
                    body(half, j, False)
                body(half, NJ - 1, True)
            keep_sums(1)

            dve.wait_ge(act_step, 8)
            link(dve.reciprocal(rstd[:, :], rstd[:, :]))
            dve.wait_ge(gff_ready, TT)
            for t in range(TT):
                last = dve.scalar_tensor_tensor(s0[:, t, :], s0[:, t, :], rstd[:, t:t + 1], gff[:, t, :], ALU.mult, ALU.mult)
            link(last)
            link(dve.tensor_tensor(x[:, :, :], x[:, :, :], s0[:, :, :], ALU.add))
            ln_stats()
            dve.wait_ge(act_step, 9)
            ln_apply()
            x_lo(1)
            dve.wait_ge(ff_in, 48)
            for a in range(2):
                raw = w_gu[:, a * 2048:(a + 1) * 2048]
                hi, lo = [wgu16[:, i, a, :, :, :, :].rearrange("p k m g c -> p (k m g c)") for i in range(2)]
                split(hi, lo, raw).then_inc(ff16, 1)
            link(dve.memset(vb, 0.0))
            pairs = [(0, 1), (0, 2), (1, 2), (0, 3), (1, 3), (2, 3)]
            w, c = [wins[:, i, :] for i in range(4)], [cmpb[:, i, :] for i in range(6)]
            keep = ((2.0, ALU.is_ge), (1.0, ALU.is_ge), (0.0, ALU.is_ge), (1.0, ALU.is_le))
            with dve.Fori(0, 2) as hf:
                for gt in range(2):
                    b = u = 2 * hf + gt
                    dve.wait_ge(qkv_done, 5 * b + 5)
                    for k in range(2):
                        last = dve.scalar_tensor_tensor(vb[:, k, :, 0:AD],
                                                        bank[1][:, k * EMB:(k + 1) * EMB].rearrange("p (h d) -> p h d", h=AH),
                                                                   UNSCALE, bv[:, :].rearrange("p (h d) -> p h d", h=AH), ALU.mult, ALU.add)
                    last.then_inc(v_ready, 1)

                    def feed_forward(h):
                        if h in (2, 3, 6, 7):
                            m = (2, 3, 6, 7).index(h)
                            dve.wait_ge(gate_up_done, 8 * u + 4 * (m // 2) + 3 + m % 2)
                            dve.scalar_tensor_tensor(hm[:, m, :], bank[4 + m % 2][:, :], UNSCALE, sgu[m % 2], ALU.mult, ALU.mult)\
                                .then_inc(hm_ready, 1)
                        for i in range(6):
                            if h == (5, 8, 9, 9, 10, 10)[i]:
                                dve.wait_ge(ha_ready, 4 * u + pairs[i][1] + 1)
                                dve.tensor_tensor(c[i], ha[:, pairs[i][0], :], ha[:, pairs[i][1], :], ALU.is_ge).then_inc(cmp_done, 1)
                        if h == 11:
                            dve.wait_ge(cmp_done, 6 * u + 6)
                            dve.tensor_tensor(w[0], c[0], c[1], ALU.add)
                            dve.tensor_tensor(w[1], c[2], c[0], ALU.subtract)
                            dve.tensor_tensor(w[2], c[1], c[2], ALU.add).then_inc(ff_step, 1)
                        if h == 12:
                            dve.wait_ge(ff_step, 2 * u + 1)
                            dve.tensor_tensor(w[0], w[0], c[3], ALU.add)
                            dve.tensor_tensor(w[1], w[1], c[4], ALU.add)
                            dve.tensor_tensor(w[3], c[3], c[4], ALU.add).then_inc(ff_step, 1)
                        if h == 13:
                            dve.wait_ge(ff_step, 2 * u + 2)
                            dve.tensor_tensor(w[2], c[5], w[2], ALU.subtract)
                            dve.tensor_tensor(w[3], w[3], c[5], ALU.add).then_inc(wins_ready, 1)
                        if h in (14, 15):
                            dve.wait_ge(wins_ready, u + 1)
                            for m in (2 * h - 28, 2 * h - 27):
                                dve.scalar_tensor_tensor(hk[:, m, :], w[m], keep[m][0], hm[:, m, :], keep[m][1], ALU.mult)\
                                    .then_inc(hk_ready, 1)

                    for h in range(AH + 2):
                        if h < AH:
                            dve.wait_ge(s_done, b * AH + h + 1)
                            dve.tensor_reduce(nmx[:, h, :], bank[h % 2][:, :].rearrange("p (q k) -> p q k", q=2),
                                              AX.X, ALU.max, negate=True).then_inc(mx_ready, 1)
                        if h >= 2:
                            dve.wait_ge(pT_done, b * AH + h - 1)
                            dve.tensor_copy(pT[h % 2].rearrange("p k q -> p (k q)"), bank[2][:, :]).then_inc(pT_ready, 1)
                        if h > 7:
                            feed_forward(h)
                        if h < AH:
                            dve.wait_ge(p_ready, b * AH + h + 1)
                            dve.reciprocal(rden[:, :, h], den[:, :, h]).then_inc(rden_ready, 1)
                        if h <= 7:
                            feed_forward(h)
                    dve.wait_ge(wo_done, b + 1)
                    for q in range(2):
                        last = dve.tensor_tensor(s1[:, bass.ds(hf * HT + 2 * gt + q, 1), :].rearrange("p a e -> p (a e)"),
                                                 bank[q][:, 0:EMB], bo[:, :], ALU.add)
                    last.then_inc(s1_ready, 1)
                for i in range(2):
                    dve.wait_ge(g1_ready, 2 * hf + i + 1)
                    dve.wait_ge(s1_ready, 2 * hf + 2)
                    s = s1[:, bass.ds(hf * HT + 2 * i, 2), :]
                    dve.tensor_tensor(s, s, g1[i].rearrange("p (t e) -> p t e", t=2), ALU.mult).then_inc(fin_step, 1)
                    dve.wait_ge(fin_step, 2 * hf + i + 1)
                    dve.tensor_tensor(s, s, x[:, bass.ds(hf * HT + 2 * i, 2), :], ALU.add).then_inc(y_ready, 1)

        @block.tensor
        def _(pe):
            def ln_transposes(n):
                for t in range(TT):
                    pe.wait_ge(ln_tile, n * TT + t + 1)
                    for k in range(KE):
                        last = pe.transpose(bank[2 * k + t // HT][:, (t % HT) * P:(t % HT + 1) * P],
                                            xn[:, t, k * P:(k + 1) * P], ident[:, :])
                last.then_inc(xT_done, 1)

            pe.wait_ge(const_in, 16 * 16)
            ln_transposes(0)
            def product(dst, left, right):
                for k in range(KE):
                    for i, (a, b) in enumerate(((0, 0), (0, 1), (1, 0))):
                        last = pe.matmul(dst, left(a, k), right(b, k), start=(k == 0 and i == 0), stop=(k == KE - 1 and i == 2))
                return last

            def x_cols(c0, n):
                return lambda i, k: x16[i][:, k, c0:c0 + n] if isinstance(c0, int) else x16[i][:, k, bass.ds(c0, n)]

            pe.wait_ge(x16_ready, 4)
            pe.wait_ge(early16, 1)
            for t in range(TT):
                last = product(bank[4][:, t * HEADS:(t + 1) * HEADS], x_cols(t * P, P), lambda i, k: dtr16[:, i, k, 0:HEADS])
            last.then_inc(dt_done, 1)
            for t in range(TT):
                last = product(bank[7][:, t * EXPERTS:(t + 1) * EXPERTS], x_cols(t * P, P),
                               lambda i, k: dtr16[:, i, k, HEADS:HEADS + EXPERTS])
            last.then_inc(sc_done, 1)
            pe.wait_ge(adt_ready, 1)
            pe.matmul(bank[5][:, :], later[:, :], adt[:, :, :].rearrange("p t h -> p (t h)"), start=True, stop=True)\
                .then_inc(suffix_done, 1)

            def segments(n):
                pe.wait_ge(r1_ready, n + 1)
                if not isinstance(n, int) or n > 0:
                    pe.wait_ge(exp_done, n)
                r = r1.rearrange("p t h i -> p (t h i)")
                pe.matmul(bank[4][:, :], later[:, :], r, start=True, stop=False)
                pe.matmul(bank[4][:, :].rearrange("p (a i) -> p a i", i=CS), ident_b[:, :],
                          future[:, None, :].broadcast_to([P, 16, CS]), start=False, stop=True)
                pe.matmul(bank[5][:, :], chunk[:, :], r, start=True, stop=True).then_inc(seg_done, 1)

            def expert_up(t):
                pe.wait_ge(gff_ready, t)
                product(bank[6][:, :], x_cols(t * P, P), lambda i, k: wu16[:, i, k, :]).then_inc(hu_done, 1)

            def expert_turn(t):
                pe.wait_ge(hug_ready, t + 1)
                for c in range(4):
                    last = pe.transpose(bank[7][:, c * P:(c + 1) * P], hug[t % 2][:, c * P:(c + 1) * P], ident[:, :])
                last.then_inc(huT_done, 1)

            def expert_down(t):
                pe.wait_ge(huT_ready, t + 1)
                for c in range(4):
                    last = pe.matmul(bank[6][:, 0:EMB], huT[t % 2][:, c * P:(c + 1) * P], w_v[:, c, :],
                                     start=(c == 0), stop=(c == 3))
                last.then_inc(moe_done, 1)

            def bc_project(g, u):
                pe.wait_ge(wl_ready, g + 1)
                if g >= 1:
                    pe.wait_ge(bc_conv, 4 * g + u - 3)
                product(bank[u][:, :], lambda i, k: wt16[:, g % 2, i, u // 2, k, :], x_cols((u % 2) * HALF, HALF)).then_inc(bcp_done, 1)

            def g_product(g):
                pe.wait_ge(bc_silu, 4 * g + 4)
                pe.wait_ge(g_ready, g)
                if g == 0:
                    pe.wait_ge(exp_done, 1)
                for t in range(TT):
                    last = pe.matmul(bank[4 + t // HT][:, (t % HT) * P:(t % HT + 1) * P], bt[g % 2][:, t * P:(t + 1) * P],
                                     ct[g % 2][:, t * P:(t + 1) * P], start=True, stop=True)
                last.then_inc(g_done, 1)

            def project(i, s, half, done):
                product(bank[i][:, :], lambda part, k: wt16[:, s % 2, part, i, k, :], x_cols(half * HALF, HALF)).then_inc(done, 1)

            for g in range(GROUPS + 1):
                if g == GROUPS:
                    pe.wait_ge(wl_ready, GROUPS + 1)
                    pe.wait_ge(bc_conv, 4 * GROUPS - 2)
                    project(0, 0, 0, hid_done)
                    project(1, 0, 0, gate_done)
                if g < GROUPS:
                    bc_project(g, 0)
                    if g == 0:
                        pe.wait_ge(early16, 2)
                    expert_up(g)
                    bc_project(g, 1)
                    bc_project(g, 2)
                    expert_turn(g)
                    bc_project(g, 3)
                if g == 0:
                    pe.wait_ge(decay_ready, 1)
                    segments(0)
                if g >= 1:
                    g_product(g - 1)
                if g < TT:
                    expert_down(g)

            pe.wait_ge(g_ready, GROUPS)

            def zero_sums():
                for i in range(2):
                    pe.matmul(bank[6 + i][:, :], ident_b[:, :], zeros[:, :], start=True, stop=False, skip_group_check=True)

            def body(half, j, last_body):
                for s in range(4):
                    c = 4 * j + s
                    n = c + half * CT
                    over = last_body and s == 3
                    more = not (over and half == 1)
                    pair = 2 * j + s // 2 + half * (CT // 2)
                    pe.wait_ge(hs_ready, n + 1)
                    for t in range(HT):
                        last = pe.transpose(bank[2][:, t * P:(t + 1) * P], hs[:, t * P:(t + 1) * P], ident[:, :])
                    last.then_inc(t_done, 1)
                    if more:
                        pe.wait_ge(wl_ready, n + 2 + GROUPS)
                        project(0, s + 1, half + 1 if over else half, hid_done)
                    if s % 2 == 0 and not (last_body and s == 2 and half == 1):
                        segments(pair + 1)
                    if isinstance(j, int) and c == 0:
                        if half == 1:
                            project_out(CT - 1, n - 1, 3)
                    else:
                        if isinstance(j, int) and c == 1:
                            if half == 1:
                                pe.wait_ge(s0_ready, 2)
                            zero_sums()
                        project_out(c - 1, n - 1, s - 1)
                    pe.wait_ge(hT_ready, n + 1)
                    pe.wait_ge(mb_ready, pair + 1)
                    for t in range(HT):
                        for h in range(2):
                            last = pe.matmul(bank[3][HD * h:HD * h + HD, t * P:(t + 1) * P], hT[s % 2][:, t, HD * h:HD * h + HD],
                                             mb[:, s // 2, t, 2 * (s % 2) + h, :], start=True, stop=True, skip_group_check=True)
                    last.then_inc(y_done, 1)
                    if more:
                        pe.wait_ge(sg_ready, n + 1)
                        project(1, s + 1, half + 1 if over else half, gate_done)

            def project_out(c, n, s):
                pe.wait_ge(yg_ready, n + 1)
                w = w_out[:, bass.ds(c, 1), :].rearrange("p a e -> p (a e)")
                for t in range(HT):
                    last = pe.matmul(bank[6 + t // 2][:, (t % 2) * EMB:(t % 2 + 1) * EMB], yg[s % 2][:, t * P:(t + 1) * P],
                                     w, start=False, stop=False, skip_group_check=True)
                last.then_inc(out_done, 1)

            pe.wait_ge(pool_const, 13)
            for half in range(2):
                body(half, 0, False)
                with pe.Fori(1, NJ - 1) as j:
                    body(half, j, False)
                body(half, NJ - 1, True)
            project_out(CT - 1, 2 * CT - 1, 3)
            pe.wait_ge(ssq_done, 2 * CT + 1)
            for t in range(TT):
                last = pe.matmul(bank[0][:, t:t + 1], ssq[:, t // HT, (t % HT) * P:(t % HT + 1) * P], ones[:, 0:1],
                                 start=True, stop=True)
            last.then_inc(ss_done, 1)

            pe.wait_ge(act_step, 8)
            ln_transposes(1)
            pe.wait_ge(x16_ready, 8)
            pe.wait_ge(attn16, 5)
            with pe.Fori(0, 2) as hf:
                zero_sums()
                for gt in range(2):
                    b = u = 2 * hf + gt
                    x0 = hf * HALF + gt * SEQ

                    def up(m, part):
                        if part == 1:
                            pe.wait_ge(sgu_ready, 4 * u + m + 1)
                        elif m >= 2:
                            pe.wait_ge(hm_ready, 4 * u + m - 1)
                        product(bank[4 + m % 2][:, :], lambda i, k: wgu16[:, i, part, k, m, gt, :], x_cols(hf * HALF, HALF))\
                            .then_inc(gate_up_done, 1)

                    def down(m):
                        pe.wait_ge(hk_ready, 4 * u + m + 1)
                        for t in range(HT):
                            last = pe.matmul(bank[6 + t // 2][:, (t % 2) * EMB:(t % 2 + 1) * EMB], hk[:, m, t * P:(t + 1) * P],
                                             w_down[:, m, gt, :], start=False, stop=False, skip_group_check=True)
                        if m == 3:
                            last.then_inc(kept_used, 1)

                    def scores(h):
                        r, n = h % 4, h // 4
                        if h >= 2:
                            pe.wait_ge(p_ready, b * AH + h - 1)
                        for q in range(2):
                            last = pe.matmul(bank[h % 2][:, q * SEQ:(q + 1) * SEQ], qT[32 * r:32 * r + 32, n, q * P:(q + 1) * P],
                                             kT[32 * r:32 * r + 32, n, :], start=True, stop=True, tile_position=(32 * r, 0))
                        last.then_inc(s_done, 1)

                    def turn(h):
                        pe.wait_ge(pn_ready, b * AH + h + 1)
                        if h >= 1:
                            pe.wait_ge(pT_ready, b * AH + h)
                        for k in range(2):
                            for q in range(2):
                                last = pe.transpose(bank[2][:, (2 * k + q) * P:(2 * k + q + 1) * P],
                                                    pn[h % 2][:, q, k * P:(k + 1) * P], ident[:, :])
                        last.then_inc(pT_done, 1)

                    def weigh(h):
                        r, n = h % 4, h // 4
                        if h == 8:
                            pe.wait_ge(hm_ready, 4 * u + 4)
                        pe.wait_ge(pT_ready, b * AH + h + 1)
                        for k in range(2):
                            last = pe.matmul(bank[3 + n // 2][32 * r:32 * r + 32, (n % 2) * SEQ:(n % 2 + 1) * SEQ], vb[:, k, h, :],
                                             pT[h % 2][:, k, :], start=(k == 0), stop=(k == 1), skip_group_check=True)
                        last.then_inc(pv_done, 1)

                    for i in range(4):
                        if i == 3:
                            pe.wait_ge(qk_ready, 4 * b + 1)
                        for n in range(2):
                            c0 = (2 * (i % 2) + n) * P
                            last = product(bank[i % 3][:, n * SEQ:(n + 1) * SEQ],
                                           lambda part, k: wqk16[:, part, i // 2, k, c0:c0 + P], x_cols(x0, SEQ))
                        last.then_inc(qkv_done, 1)
                    pe.wait_ge(qk_ready, 4 * b + 2)
                    for i in range(2):
                        last = product(bank[1][:, i * EMB:(i + 1) * EMB], x_cols(x0 + i * P, P), lambda part, k: wv16[:, part, k, :])
                    last.then_inc(qkv_done, 1)
                    pe.wait_ge(ff16, 2)
                    up(0, 0)
                    up(1, 0)
                    pe.wait_ge(qk_ready, 4 * b + 4)
                    scores(0)
                    pe.wait_ge(v_ready, b + 1)
                    for i in range(AH + 2):
                        if i + 1 < AH:
                            scores(i + 1)
                        if 1 <= i <= 6:
                            up(*((0, 1), (1, 1), (2, 0), (3, 0), (2, 1), (3, 1))[i - 1])
                        if 1 <= i <= AH:
                            turn(i - 1)
                        if i >= 2:
                            weigh(i - 2)
                        if i >= 15:
                            down(i - 15)
                    down(3)
                    for n in range(4):
                        if n % 2 == 0:
                            pe.wait_ge(oT_ready, 2 * b + n // 2 + 1)
                        for q in range(2):
                            last = pe.matmul(bank[q][:, 0:EMB], oT[:, n, q * P:(q + 1) * P], wo[:, n, :],
                                             start=(n == 0), stop=(n == 3))
                    last.then_inc(wo_done, 1)
                    pe.wait_ge(s1_ready, b + 1)
                pe.wait_ge(g1_ready, 2 * hf + 2)


_F32_INS = {
    "x": (TOK, EMB), "w_in": (EMB, PROJ), "w_out": (INTER, EMB), "conv_w": (P, CONV_T, TAPS), "conv_b": (P, CONV_T),
    "norm_w": (P, CT), "dt_bias": (1, HEADS), "a_log": (1, HEADS), "d": (1, HEADS), "w_router": (EMB, EXPERTS),
    "w_a": (1, EXPERTS), "attr": (1, EXPERTS * EXPERTS), "w_u": (EMB, EXPERTS * RANK), "w_v": (EXPERTS * RANK, EMB),
    "wq": (EMB, EMB), "wk": (EMB, EMB), "wv": (EMB, EMB), "wo": (EMB, EMB), "bq": (4, AD, 4), "bk": (4, AD, 4),
    "bv": (1, EMB), "bo": (1, EMB), "w_gate": (EMB, FF), "w_up": (EMB, FF), "w_down": (FF, EMB),
}

_CONST_INS = {"ident": (P, P), "later": (P, P), "chunk": (P, P), "upto": (P, CS), "diag": (P, CS), "expert_no": (P, EXPERTS)}
_BF16_INS = {"future": (P, CS), "ident_b": (P, P)}


def kernel(**inputs):
    import ml_dtypes
    import numpy as np
    import concourse.bacc as bacc
    from concourse.bass_utils import run_bass_kernel_spmd as run

    a = {k: np.asarray(v) for k, v in inputs.items()}
    m, f = "L0_attn_", "L0_ffn_"
    q, w = "L1_attn_", "L1_ffn_"
    by_member = np.arange(FF).reshape(FF // 4, 4).T.reshape(-1)
    data = {
        "x": a[m + "input_states"].reshape(TOK, EMB),
        "w_in": a[m + "in_proj_w"].T,
        "w_out": a[m + "out_proj_w"].T,
        "conv_w": a[m + "conv_w"].reshape(CONV_T, P, TAPS).transpose(1, 0, 2),
        "conv_b": a[m + "conv_b"].reshape(CONV_T, P).T,
        "norm_w": a[m + "norm_w"].reshape(CT, P).T,
        "dt_bias": a[m + "dt_bias"].reshape(1, HEADS),
        "a_log": a[m + "A_log"].reshape(1, HEADS),
        "d": a[m + "D"].reshape(1, HEADS),
        "w_router": a[f + "Wr"].T,
        "w_a": a[f + "Wa"],
        "attr": a[f + "attr"].reshape(1, EXPERTS * EXPERTS),
        "w_u": a[f + "U"].transpose(1, 0, 2).reshape(EMB, EXPERTS * RANK),
        "w_v": a[f + "V"].reshape(EXPERTS * RANK, EMB),
        "wq": a[q + "Wq"].T, "wk": a[q + "Wk"].T, "wv": a[q + "Wv"].T, "wo": a[q + "Wo"].T,
        "bq": a[q + "bq"].reshape(4, 4, AD).transpose(1, 2, 0),
        "bk": a[q + "bk"].reshape(4, 4, AD).transpose(1, 2, 0),
        "bv": a[q + "bv"].reshape(1, EMB), "bo": a[q + "bo"].reshape(1, EMB),
        "w_gate": a[w + "w_gate"][:, by_member], "w_up": a[w + "w_up"][:, by_member],
        "w_down": a[w + "w_down"][by_member, :],
    }
    k, j = np.arange(P)[:, None], np.arange(P)[None, :]
    same, i = k // CS == j // CS, np.arange(CS)[None, :]
    data["ident"] = (k == j).astype(np.float32)
    data["later"] = (same & (k > j)).astype(np.float32)
    data["chunk"] = same.astype(np.float32)
    data["upto"] = (k % CS <= i).astype(np.float32)
    data["diag"] = (k % CS == i).astype(np.float32)
    data["expert_no"] = np.broadcast_to(np.arange(EXPERTS, dtype=np.float32), (P, EXPERTS))
    data["future"] = np.where(i < k % CS, -30000.0, 0.0).astype(ml_dtypes.bfloat16)
    data["ident_b"] = (k == j).astype(ml_dtypes.bfloat16)

    nc = bacc.Bacc("TRN2", target_bir_lowering=False, num_devices=1)
    arrays, aps = {}, {}
    for name, shape in {**_F32_INS, **_CONST_INS, **_BF16_INS}.items():
        arrays[name + "_dram"] = np.ascontiguousarray(data[name]).reshape(shape)
        dt = BF16 if name in _BF16_INS else F32
        aps[name] = nc.dram_tensor(name + "_dram", shape, dt, kind="ExternalInput").ap()
    out = nc.dram_tensor("out_dram", (TOK, EMB), F32, kind="ExternalOutput").ap()
    build(nc, aps, out)
    r = run(nc, [arrays], core_ids=[0])
    return r.results[0]["out_dram"].reshape(BATCH, SEQ, EMB)
```

```python
from contextlib import ExitStack

import concourse.bass as bass
from concourse import mybir

F32 = mybir.dt.float32
BF16 = mybir.dt.bfloat16
F16 = mybir.dt.float16
U32 = mybir.dt.uint32
ALU = mybir.AluOpType
ACT = mybir.ActivationFunctionType
AX = mybir.AxisListType

P = 128
TOK, BATCH, SEQ, EMB = 1024, 4, 256, 256
TT = TOK // P
KE = EMB // P
HALF = TOK // 2
HT = HALF // P
HEADS, HD, STATE, GROUPS, TAPS, CS = 64, 64, 128, 8, 4, 32
INTER = HEADS * HD
CT = INTER // P
CONV = INTER + 2 * GROUPS * STATE
CONV_T = CONV // P
PROJ = INTER + CONV + HEADS
EXPERTS, RANK = 32, 16
AH, AD = 16, 16
FF = 1024
FT = FF // P
LN_EPS, RMS_EPS = 1e-5, 1e-6
X_SCALE, W_SCALE = 2048.0, 64.0
UNSCALE = 1.0 / (X_SCALE * W_SCALE)
P_SCALE = 32768.0


def build(nc, t_in, out):
    ctx = ExitStack()
    with ctx:
        def sb(name, shape, dt=F32):
            return ctx.enter_context(nc.sbuf_tensor(name, shape, dt))

        def sem(name):
            return ctx.enter_context(nc.semaphore(name))

        bank = [ctx.enter_context(nc.psum_tensor(f"bank{i}", [P, 512], F32)) for i in range(8)]

        ident = sb("ident", [P, P])
        later = sb("later", [P, P])
        later_b = sb("later_b", [P, P], BF16)
        chunk = sb("chunk", [P, P], BF16)
        upto = sb("upto", [P, CS], BF16)
        diag = sb("diag", [P, CS])
        future = sb("future", [P, CS], BF16)
        ident_b = sb("ident_b", [P, P], BF16)
        zeros = sb("zeros", [P, CS], BF16)
        ones = sb("ones", [P, 2])
        w_scale = sb("w_scale", [P, 1])
        expert_no = sb("expert_no", [P, EXPERTS])
        conv_w = sb("conv_w_sb", [P, CONV_T, TAPS])
        conv_b = sb("conv_b_sb", [P, CONV_T])
        norm_w = sb("norm_w_sb", [P, CT])
        d_row = sb("d_row", [P, HEADS])
        dtr16 = sb("dtr16", [P, 2, KE, HEADS + EXPERTS], F16)
        w_a = sb("w_a", [P, EXPERTS])
        wqk16 = sb("wqk16", [P, 2, 2, KE, 4 * P], F16)
        wv16 = sb("wv16", [P, 2, KE, EMB], F16)
        wo = sb("wo", [P, 4, EMB])
        bq = sb("bq_sb", [P, 4])
        bk = sb("bk_sb", [P, 4])
        bq4 = sb("bq4", [P, 4])
        bq_lo = sb("bq_lo", [P, 4])
        mix = sb("mix_sb", [P, 2])
        q_lo = sb("q_lo", [P, 1])
        bv = sb("bv_sb", [P, EMB])
        bo = sb("bo_sb", [P, EMB])

        x = sb("x_sb", [P, TT, EMB])
        xn = sb("xn", [P, TT, EMB])
        x16 = [sb(n, [P, KE, TOK], F16) for n in ("xh", "xl")]
        gff = sb("gff", [P, TT, EMB])
        s0 = sb("s0", [P, TT, EMB])
        s1 = sb("s1", [P, TT, EMB])
        adt = sb("adt", [P, TT, HEADS])
        dts = sb("dts", [P, TT, HEADS])
        decay = sb("decay", [P, TT, HEADS])
        gc = sb("gc", [P, TT, GROUPS, CS])
        dd = sb("dd", [P, HEADS, CS])
        r1 = sb("r1", [P, 3, HT, 4, CS], BF16)
        ssq = sb("ssq", [P, 2, HALF])
        stats = sb("stats", [P, TT, 6])
        mv = sb("mv", [P, TT, 2])
        sd = sb("sd", [P, TT])
        rstd = sb("rstd", [P, TT])
        wring = sb("wring", [P, 4, 2, KE, P])
        wt16 = sb("wt16", [P, 2, 2, 2, KE, P], F16)
        big = sb("big", [P, 8192])
        w_out = big[:, :].rearrange("p (c e) -> p c e", c=CT)
        w_gu = big[:, 0:4096]
        w_down = big[:, 4096:6144].rearrange("p (m g e) -> p m g e", m=4, g=2)

        AREA = 16640
        area = sb("area", [P, AREA])
        at = [0]

        def carve(n):
            at[0] += n
            return area[:, at[0] - n:at[0]]

        bt = [carve(TOK) for _ in range(2)]
        ct = [carve(TOK) for _ in range(2)]
        cv = [carve(HALF) for _ in range(2)]
        hs = carve(HALF)
        hT = [carve(HALF).rearrange("p (t c) -> p t c", t=HT) for _ in range(2)]
        sg = [carve(HALF) for _ in range(2)]
        yg = [carve(HALF) for _ in range(2)]
        sq = [carve(HALF) for _ in range(2)]
        adt3 = carve(3 * TT * HEADS // 2).bitcast(BF16).rearrange("p (s t h) -> p s t h", s=3, t=TT)
        e1 = carve(HALF).rearrange("p (t h i) -> p t h i", t=HT, h=4)
        e2 = carve(HALF).rearrange("p (t h i) -> p t h i", t=HT, h=4)
        ms = carve(HALF).rearrange("p (t h i) -> p t h i", t=HT, h=4)
        mc = carve(HALF).rearrange("p (t h i) -> p t h i", t=HT, h=4)
        early = at[0]
        mb = carve(2 * HT * 4 * P).rearrange("p (s t h i) -> p s t h i", s=2, t=HT, h=4)
        assert at[0] <= AREA
        at[0] = 0
        dtr = carve(KE * (HEADS + EXPERTS)).rearrange("p (k c) -> p k c", k=KE)
        attr = carve(EXPERTS * EXPERTS).rearrange("p (a b) -> p a b", a=EXPERTS)
        dt_bias, a_row = [carve(HEADS) for _ in range(2)]
        top, topf = [carve(TT * 8).rearrange("p (t m) -> p t m", t=TT) for _ in range(2)]
        topi = carve(TT * 8).bitcast(U32).rearrange("p (t m) -> p t m", t=TT)
        sp = [carve(TT * HEADS).rearrange("p (t h) -> p t h", t=TT) for _ in range(3)]
        assert at[0] <= 4 * TOK
        at[0] = 4 * TOK + 3 * HALF
        hug = [carve(512) for _ in range(2)]
        huT = [carve(512) for _ in range(2)]
        awt = area[:, at[0] - 2048:at[0] - 1024].rearrange("p (a b) -> p a b", a=EXPERTS)
        w_v = carve(4 * EMB).rearrange("p (k e) -> p k e", k=4)
        wu16 = carve(KE * EXPERTS * RANK).bitcast(F16).rearrange("p (s k c) -> p s k c", s=2, k=KE)
        at[0] += 3 * TT * HEADS // 2
        at[0] += 2 * HALF
        sc, pe_, sel0, sel1 = [carve(TT * EXPERTS).rearrange("p (t s) -> p t s", t=TT) for _ in range(4)]
        sel = [sel0, sel1]
        assert at[0] <= early
        w_u = s1[:, 0:4, :].rearrange("p t e -> p (t e)")
        wv = s1[:, 4:6, :]
        wqk = xn[:, :, :].rearrange("p t e -> p (t e)").rearrange("p (w k c) -> p w k c", w=2, k=KE)
        at[0] = 0
        q16 = carve(512).bitcast(F16).rearrange("p (n t) -> p n t", n=4)
        k16 = carve(1024).bitcast(F16).rearrange("p (s n t) -> p s n t", s=2, n=4)
        qk32 = [gff[:, 2 * i:2 * i + 2, :] for i in range(2)]
        v32 = carve(512).rearrange("p (k h d) -> p k h d", k=2, h=AH)
        v16 = carve(512).bitcast(F16).rearrange("p (k h s d) -> p k h s d", k=2, h=AH, s=2)
        pr = [carve(512).rearrange("p (q k) -> p q k", q=2) for _ in range(2)]
        pn = [carve(512).rearrange("p (q k) -> p q k", q=2) for _ in range(2)]
        pT = [carve(512).bitcast(F16).rearrange("p (s k q) -> p s k q", s=2, k=2) for _ in range(2)]
        oT = carve(1024).rearrange("p (n q) -> p n q", n=4)
        nmx = carve(32).rearrange("p (h q) -> p h q", h=AH)
        den = carve(32).rearrange("p (q h) -> p q h", q=2)
        rden = carve(32).rearrange("p (q h) -> p q h", q=2)
        sgu = [carve(512) for _ in range(2)] + [gff[:, 4 + 2 * i:6 + 2 * i, :].rearrange("p t e -> p (t e)") for i in range(2)]
        wgu16 = carve(4096).bitcast(F16).rearrange("p (s a k m g c) -> p s a k m g c", s=2, a=2, k=KE, m=4, g=2)
        hm = s0[:, :, :].rearrange("p t e -> p (t e)").rearrange("p (m t) -> p m t", m=4)
        ha = dd[:, :, :].rearrange("p h i -> p (h i)").rearrange("p (m t) -> p m t", m=4)
        hk = gc[:, :, :, :].rearrange("p t g i -> p (t g i)").rearrange("p (m t) -> p m t", m=4)
        g1 = [carve(512) for _ in range(2)]
        cmpb = carve(1536).bitcast(BF16).rearrange("p (n t) -> p n t", n=6)
        wins = carve(1024).bitcast(BF16).rearrange("p (n t) -> p n t", n=4)
        assert at[0] <= AREA
        win, beats = [wins[:, i, :] for i in range(4)], [cmpb[:, i, :] for i in range(6)]
        eps_ln = sb("eps_ln", [P, 1])
        eps_rms = sb("eps_rms", [P, 1])
        rsum = [sb(f"rsum{i}", [P, TT]) for i in range(4)]
        aw = sb("aw", [P, EXPERTS])

        def turn_bank(h):
            return bank[5 if h >= 3 and h % 2 else 2][:, :]

        x_in = sem("x_in")
        const_in = sem("const_in")
        moe_in = sem("moe_in")
        wout_in = sem("wout_in")
        attn_in = sem("attn_in")
        gate_in = sem("gate_in")
        up_in = sem("up_in")
        down_in = sem("down_in")
        w_in = [sem(f"w_in{i}") for i in range(4)]
        pool_const = sem("pool_const")
        dve_step = sem("dve_step")
        act_step = sem("act_step")
        ln_tile = sem("ln_tile")
        xT_done = sem("xT_done")
        dt_done = sem("dt_done")
        adt_ready = sem("adt_ready")
        adt_step = sem("adt_step")
        suffix_done = sem("suffix_done")
        decay_ready = sem("decay_ready")
        sc_done = sem("sc_done")
        route_exp = sem("route_exp")
        hu_done = sem("hu_done")
        hug_ready = sem("hug_ready")
        huT_done = sem("huT_done")
        huT_ready = sem("huT_ready")
        moe_done = sem("moe_done")
        gff_ready = sem("gff_ready")
        bcp_done = sem("bcp_done")
        bc_tap = sem("bc_tap")
        bc_conv = sem("bc_conv")
        bc_silu = sem("bc_silu")
        g_done = sem("g_done")
        g_ready = sem("g_ready")
        r1_ready = sem("r1_ready")
        seg_done = sem("seg_done")
        exp_done = sem("exp_done")
        e2d_ready = sem("e2d_ready")
        m_add = sem("m_add")
        m_g = sem("m_g")
        m_dt = sem("m_dt")
        m_ready = sem("m_ready")
        mb_ready = sem("mb_ready")
        hid_done = sem("hid_done")
        gate_done = sem("gate_done")
        tap_done = sem("tap_done")
        conv_done = sem("conv_done")
        hs_ready = sem("hs_ready")
        t_done = sem("t_done")
        hT_ready = sem("hT_ready")
        y_done = sem("y_done")
        sg_ready = sem("sg_ready")
        yg_ready = sem("yg_ready")
        sq_ready = sem("sq_ready")
        ssq_done = sem("ssq_done")
        out_done = sem("out_done")
        s0_ready = sem("s0_ready")
        ss_done = sem("ss_done")
        wh_ready = sem("wh_ready")
        wl_ready = sem("wl_ready")
        early16 = sem("early16")
        attn16 = sem("attn16")
        attn_hi = sem("attn_hi")
        cmp_done = sem("cmp_done")
        wins_ready = sem("wins_ready")
        ff_hi = sem("ff_hi")
        k32_ready = sem("k32_ready")
        ff16 = sem("ff16")
        xh_ready = sem("xh_ready")
        x16_ready = sem("x16_ready")
        qkv_done = sem("qkv_done")
        qk_read = sem("qk_read")
        qk_ready = sem("qk_ready")
        v_step = sem("v_step")
        pTh_ready = sem("pTh_ready")
        v_ready = sem("v_ready")
        s_done = sem("s_done")
        mx_ready = sem("mx_ready")
        p_ready = sem("p_ready")
        pT_done = sem("pT_done")
        pT_ready = sem("pT_ready")
        pv_done = sem("pv_done")
        pn_ready = sem("pn_ready")
        oT_ready = sem("oT_ready")
        wo_done = sem("wo_done")
        s1_ready = sem("s1_ready")
        gate_up_done = sem("gate_up_done")
        sgu_ready = sem("sgu_ready")
        hm_ready = sem("hm_ready")
        ha_ready = sem("ha_ready")
        hk_ready = sem("hk_ready")
        g1_ready = sem("g1_ready")
        y_ready = sem("y_ready")
        y_out = sem("y_out")
        chain = sem("chain")
        conv_step = sem("conv_step")
        rden_ready = sem("rden_ready")
        ff_step = sem("ff_step")
        kept_used = sem("kept_used")
        fin_step = sem("fin_step")

        x_dram = t_in["x"].rearrange("(t p) e -> p t e", p=P)
        out_dram = out.rearrange("(t p) e -> p t e", p=P)
        win_dram = t_in["w_in"].rearrange("(k p) c -> p k c", p=P)
        NJ = CT // 4
        block = ctx.enter_context(nc.Block())

        @block.sync
        def _(sp_):
            sp_.dma_start(x[:, 0:HT, :], x_dram[:, 0:HT, :]).then_inc(x_in, 16)
            sp_.dma_start(x[:, HT:TT, :], x_dram[:, HT:TT, :]).then_inc(x_in, 16)
            for dst, name in ((ident, "ident"), (later, "later"), (later_b, "later_b"), (chunk, "chunk"), (upto, "upto"), (diag, "diag"),
                              (future, "future"), (ident_b, "ident_b"), (expert_no, "expert_no"),
                              (conv_b, "conv_b"), (norm_w, "norm_w"), (mix, "mix")):
                sp_.dma_start(dst[:, :], t_in[name]).then_inc(const_in, 16)
            sp_.dma_start(conv_w[:, :, :], t_in["conv_w"]).then_inc(const_in, 16)
            for dst, name in ((dt_bias, "dt_bias"), (a_row, "a_log"), (d_row, "d")):
                sp_.dma_start(dst[:, :], t_in[name].partition_broadcast(P)).then_inc(const_in, 16)
            sp_.dma_start(dtr[:, :, 0:HEADS], win_dram[:, :, INTER + CONV:PROJ]).then_inc(const_in, 16)
            sp_.dma_start(dtr[:, :, HEADS:HEADS + EXPERTS], t_in["w_router"].rearrange("(k p) s -> p k s", p=P)).then_inc(const_in, 16)
            sp_.dma_start(w_a[:, :], t_in["w_a"].partition_broadcast(P)).then_inc(moe_in, 16)
            sp_.dma_start(attr.rearrange("p a b -> p (a b)"), t_in["attr"].partition_broadcast(P)).then_inc(moe_in, 16)
            sp_.dma_start(w_u.rearrange("p (k s) -> p k s", k=KE), t_in["w_u"].rearrange("(k p) s -> p k s", p=P)).then_inc(moe_in, 16)
            sp_.dma_start(w_v, t_in["w_v"].rearrange("(k p) e -> p k e", p=P)).then_inc(moe_in, 16)
            base = 2 * INTER
            for g in range(GROUPS):
                if g >= 4:
                    sp_.wait_ge(wl_ready, g - 3)
                for i in range(2):
                    c0 = base + (i * GROUPS + g) * P
                    sp_.dma_start(wring[:, g % 4, i, :, :], win_dram[:, :, c0:c0 + P]).then_inc(w_in[g % 4], 16)
                if g == 3:
                    sp_.dma_start(w_out, t_in["w_out"].rearrange("(c p) e -> p c e", p=P)).then_inc(wout_in, 16)
                    sp_.wait_ge(xT_done, 2)
                    for i, name in ((0, "wq"), (1, "wk")):
                        sp_.dma_start(wqk[:, i, :, :], t_in[name].rearrange("(k p) c -> p k c", p=P)).then_inc(attn_in, 16)
                    sp_.dma_start(wv, t_in["wv"].rearrange("(k p) e -> p k e", p=P)).then_inc(attn_in, 16)
                    sp_.dma_start(wo[:, :, :], t_in["wo"]).then_inc(attn_in, 16)
                    sp_.dma_start(bq[:, :], t_in["bq"]).then_inc(attn_in, 16)
                    sp_.dma_start(bk[:, :], t_in["bk"]).then_inc(attn_in, 16)
                    sp_.dma_start(bv[:, :], t_in["bv"].partition_broadcast(P)).then_inc(attn_in, 16)
                    sp_.dma_start(bo[:, :], t_in["bo"].partition_broadcast(P)).then_inc(attn_in, 16)
            for half in range(2):
                with sp_.Fori(0, NJ) as j:
                    for s in range(4):
                        sp_.wait_ge(wl_ready, 4 * j + (s + half * CT + GROUPS - 3))
                        sp_.dma_start(wring[:, s, 0, :, :], win_dram[:, :, bass.ds(j * (4 * P) + (INTER + s * P), P)]).then_inc(w_in[s], 16)
                        sp_.dma_start(wring[:, s, 1, :, :], win_dram[:, :, bass.ds(j * (4 * P) + s * P, P)]).then_inc(w_in[s], 16)
            sp_.wait_ge(out_done, 2 * CT)
            sp_.dma_start(big[:, 0:2048].rearrange("p (k c) -> p k c", k=KE),
                          t_in["w_gate"].rearrange("(k p) c -> p k c", p=P)).then_inc(gate_in, 16)
            sp_.dma_start(big[:, 2048:4096].rearrange("p (k c) -> p k c", k=KE),
                          t_in["w_up"].rearrange("(k p) c -> p k c", p=P)).then_inc(up_in, 16)
            sp_.dma_start(big[:, 4096:6144].rearrange("p (k c) -> p k c", k=FT),
                          t_in["w_down"].rearrange("(k p) c -> p k c", p=P)).then_inc(down_in, 16)
            for h in range(2):
                sp_.wait_ge(y_ready, 2 * h + 2)
                sp_.dma_start(out_dram[:, h * HT:(h + 1) * HT, :], s1[:, h * HT:(h + 1) * HT, :]).then_inc(y_out, 16)
            sp_.wait_ge(y_out, 32)

        @block.gpsimd
        def _(pool):
            pool.memset(ones[:, :], 1.0).then_inc(pool_const, 1)
            pool.memset(zeros[:, :], 0.0).then_inc(pool_const, 1)
            pool.memset(w_scale[:, :], W_SCALE).then_inc(pool_const, 1)
            pool.memset(ssq[:, :, :], 0.0).then_inc(ssq_done, 1)
            pool.memset(mb[:, :, :, :, :], 0.0).then_inc(pool_const, 1)
            def hi_part(raw_slot, slot, landed):
                pool.wait_ge(w_in[raw_slot], landed)
                pool.tensor_tensor(wt16[:, slot, 0, :, :, :].rearrange("p a k c -> p (a k c)"),
                                   wring[:, raw_slot, :, :, :].rearrange("p a k c -> p (a k c)"),
                                   w_scale[:, :].broadcast_to([P, 2 * KE * P]), ALU.mult)\
                    .then_inc(wh_ready, 1)

            pool.wait_ge(pool_const, 3)
            hi_part(0, 0, 32)
            hi_part(1, 1, 32)
            pool.wait_ge(const_in, 16 * 18)
            pool.tensor_tensor(dd[:, :, :], diag[:, None, :].broadcast_to([P, HEADS, CS]),
                               d_row[:, :, None].broadcast_to([P, HEADS, CS]), ALU.mult).then_inc(pool_const, 1)
            pool.wait_ge(bcp_done, 4)
            hi_part(2, 0, 32)
            pool.wait_ge(adt_ready, 1)
            left = r1[:, 0:2, :, :, :].rearrange("p s t h i -> p (s t h i)").bitcast(F32).rearrange("p (t h) -> p t h", t=TT)
            pool.tensor_copy(adt3[:, 0, :, :], adt[:, :, :]).then_inc(adt_step, 1)
            pool.wait_ge(adt_step, 1)
            pool.tensor_tensor(left, adt[:, :, :], adt3[:, 0, :, :], ALU.subtract).then_inc(adt_step, 1)
            pool.wait_ge(adt_step, 2)
            pool.tensor_copy(adt3[:, 1, :, :], left).then_inc(adt_step, 1)
            pool.wait_ge(adt_step, 3)
            pool.tensor_tensor(adt3[:, 2, :, :], left, adt3[:, 1, :, :], ALU.subtract).then_inc(adt_step, 1)
            pool.wait_ge(adt_step, 4)

            def mask_a(half, p):
                for part in range(3):
                    a = adt3[:, part, half * HT:(half + 1) * HT, bass.ds(4 * p, 4)]
                    last = pool.tensor_tensor(r1[:, part, :, :, :], a[:, :, :, None].broadcast_to([P, HT, 4, CS]),
                                              upto[:, None, None, :].broadcast_to([P, HT, 4, CS]), ALU.mult)
                return last

            def m_first(half, p, n):
                pool.wait_ge(exp_done, n + 1)
                e = decay[:, half * HT:(half + 1) * HT, bass.ds(4 * p, 4)]
                pool.tensor_tensor(e2, e2, e[:, :, :, None].broadcast_to([P, HT, 4, CS]), ALU.mult).then_inc(e2d_ready, 1)

            def m_last(half, p, n):
                pool.wait_ge(m_g, n + 1)
                e = dts[:, half * HT:(half + 1) * HT, bass.ds(4 * p, 4)]
                pool.tensor_tensor(ms, ms, e[:, :, :, None].broadcast_to([P, HT, 4, CS]), ALU.mult).then_inc(m_dt, 1)
                pool.wait_ge(m_dt, n + 1)
                if not isinstance(n, int) or n > 0:
                    pool.wait_ge(mb_ready, n)
                d = dd[:, bass.ds(4 * p, 4), :]
                pool.tensor_tensor(mc, ms, d[:, None, :, :].broadcast_to([P, HT, 4, CS]), ALU.add).then_inc(m_ready, 1)

            def add_square(half, n, s):
                pool.wait_ge(sq_ready, n + 1)
                pool.wait_ge(ssq_done, n + 1)
                pool.tensor_tensor(ssq[:, half, :], ssq[:, half, :], sq[s % 2], ALU.add).then_inc(ssq_done, 1)

            mask_a(0, 0).then_inc(r1_ready, 1)
            pool.wait_ge(decay_ready, 1)
            pool.wait_ge(attn_in, 16 * 8)
            pool.tensor_tensor(wqk16[:, 0, :, :, :].rearrange("p w k c -> p (w k c)"), wqk.rearrange("p w k c -> p (w k c)"),
                               w_scale[:, :].broadcast_to([P, 2 * KE * 4 * P]), ALU.mult).then_inc(attn_hi, 1)
            pool.tensor_tensor(wv16[:, 0, :, :], wv, w_scale[:, :, None].broadcast_to([P, KE, EMB]), ALU.mult).then_inc(attn_hi, 1)

            m_first(0, 0, 0)
            pool.wait_ge(seg_done, 1)
            mask_a(0, 1).then_inc(r1_ready, 1)
            for w in range(2, GROUPS + 2):
                if w > 2:
                    pool.wait_ge(bcp_done, 4 * (w - 1))
                    hi_part(w % 4, w % 2, 32 * (w // 4 + 1))
                if w >= GROUPS - 2:
                    pool.wait_ge(wout_in, 16)
                    c = slice((w - GROUPS + 2) * (CT // 4), (w - GROUPS + 3) * (CT // 4))
                    pool.tensor_tensor(w_out[:, c, :], w_out[:, c, :], norm_w[:, c, None].broadcast_to([P, CT // 4, EMB]), ALU.mult)\
                        .then_inc(pool_const, 1)

            def tile_after_next(half, j, s):
                pool.wait_ge(gate_done, 4 * j + s + half * CT + 1)
                hi_part((s + 2) % 4, s % 2, 32 * (j + (s + 2) // 4 + half * NJ + 3))

            def body(half, j, last):
                for q in range(2):
                    pair = 2 * j + q
                    n = pair + half * (CT // 2)
                    over = last and q == 1
                    build_next = not (over and half == 1)
                    m_last(half, pair, n)
                    if build_next:
                        nh, npair = (half + 1, 0) if over else (half, pair + 1)
                        tile_after_next(half, j, 2 * q)
                    if not (isinstance(n, int) and n == 0):
                        h = half - (isinstance(j, int) and j == 0 and q == 0)
                        add_square(h, 2 * n - 2, 0)
                        add_square(h, 2 * n - 1, 1)
                    if build_next:
                        tile_after_next(half, j, 2 * q + 1)
                        m_first(nh, npair, n + 1)
                    if not (last and half == 1):
                        pool.wait_ge(seg_done, n + 2)
                        mask_a(half + 1 if last else half, q if last else pair + 2).then_inc(r1_ready, 1)

            for half in range(2):
                body(half, 0, False)
                with pool.Fori(1, NJ - 1) as j:
                    body(half, j, False)
                body(half, NJ - 1, True)
            add_square(1, 2 * CT - 2, 0)
            add_square(1, 2 * CT - 1, 1)

            with pool.Fori(0, 2) as hf:
                for gt in range(2):
                    b = u = 2 * hf + gt
                    for h in range(AH):
                        if h >= 2:
                            pool.wait_ge(pT_done, b * AH + h - 1)
                        pool.wait_ge(rden_ready, b * AH + h + 1)
                        pool.tensor_tensor(pn[h % 2], pr[h % 2], rden[:, :, h, None].broadcast_to([P, 2, SEQ]), ALU.mult)\
                            .then_inc(pn_ready, 1)
                        if h == 7:
                            pool.wait_ge(cmp_done, 6 * u + 3)
                            pool.tensor_tensor(win[0], beats[0], beats[1], ALU.add)
                        if h == 8:
                            pool.tensor_tensor(win[1], beats[2], beats[0], ALU.subtract)
                        if h == 9:
                            pool.tensor_tensor(win[2], beats[1], beats[2], ALU.add).then_inc(ff_step, 1)
                        if h == 10:
                            pool.wait_ge(cmp_done, 6 * u + 5)
                            pool.tensor_tensor(win[3], beats[3], beats[4], ALU.add).then_inc(ff_step, 1)
                        if h == 11:
                            pool.wait_ge(ff_step, 2 * u + 2)
                            pool.tensor_tensor(win[0], win[0], beats[3], ALU.add).then_inc(wins_ready, 1)
                        if h == 12:
                            pool.tensor_tensor(win[1], win[1], beats[4], ALU.add).then_inc(wins_ready, 1)
                        if h == 13:
                            pool.wait_ge(cmp_done, 6 * u + 6)
                            pool.tensor_tensor(win[2], beats[5], win[2], ALU.subtract).then_inc(wins_ready, 1)
                        if h == 14:
                            pool.tensor_tensor(win[3], win[3], beats[5], ALU.add).then_inc(wins_ready, 1)

        @block.scalar
        def _(act):
            def w_hi(a):
                act.wait_ge((gate_in, up_in)[a], 16)
                act.wait_ge(ssq_done, 2 * CT + 1)
                act.activation(wgu16[:, 0, a, :, :, :, :].rearrange("p k m g c -> p (k m g c)"),
                               w_gu[:, a * 2048:(a + 1) * 2048], ACT.Copy, scale=W_SCALE).then_inc(ff_hi, 1)

            def x_hi(n):
                for half in range(2):
                    act.wait_ge(xT_done, 2 * n + half + 1)
                    for k in range(KE):
                        act.activation(x16[0][:, k, half * HALF:(half + 1) * HALF], bank[2 * k + half][:, :], ACT.Copy, scale=X_SCALE)\
                            .then_inc(xh_ready, 1)

            act.wait_ge(dve_step, 1)
            act.activation(sd[:, :], mv[:, :, 1], ACT.Sqrt, bias=eps_ln[:, :]).then_inc(act_step, 1)
            x_hi(0)
            act.wait_ge(dve_step, 2)
            act.activation(sp[1], sp[0], ACT.Abs).then_inc(act_step, 1)
            act.wait_ge(act_step, 2)
            act.activation(sp[1], sp[1], ACT.Exp, scale=-1.0).then_inc(act_step, 1)
            act.wait_ge(const_in, 16 * 18)
            act.activation(a_row[:, :], a_row[:, :], ACT.Exp).then_inc(act_step, 1)
            act.wait_ge(dve_step, 3)
            act.activation(decay[:, :, :], sp[2], ACT.Ln).then_inc(act_step, 1)
            act.wait_ge(suffix_done, 1)
            act.activation(decay[:, :, :], bank[5][:, :], ACT.Exp).then_inc(decay_ready, 1)
            act.wait_ge(route_exp, 1)
            act.activation(pe_, pe_, ACT.Exp).then_inc(act_step, 1)
            act.activation(aw[:, :], aw[:, :], ACT.Exp, scale=-1.0).then_inc(act_step, 1)
            def exps(n):
                act.wait_ge(seg_done, n + 1)
                if not isinstance(n, int) or n > 0:
                    act.wait_ge(m_add, n)
                act.activation(e1, bank[4][:, :].rearrange("p (t h i) -> p t h i", t=HT, h=4), ACT.Exp)
                act.activation(e2, bank[5][:, :].rearrange("p (t h i) -> p t h i", t=HT, h=4), ACT.Exp).then_inc(exp_done, 1)

            def bc_first_tap(g, u):
                act.wait_ge(bcp_done, 4 * g + u + 1)
                if 4 * g + u >= 2:
                    act.wait_ge(bc_silu, 4 * g + u - 1)
                tile = INTER // P + (u // 2) * GROUPS + g
                act.activation(cv[u % 2], bank[u][:, :], ACT.Identity, scale=conv_w[:, tile, TAPS - 1:TAPS],
                               bias=conv_b[:, tile:tile + 1]).then_inc(bc_tap, 1)

            def bc_silu_of(g, u):
                act.wait_ge(bc_conv, 4 * g + u + 1)
                dst = (bt, ct)[u // 2][g % 2]
                act.activation(dst[:, (u % 2) * HALF:(u % 2 + 1) * HALF], cv[u % 2], ACT.Silu).then_inc(bc_silu, 1)

            def g_blocks(g):
                act.wait_ge(g_done, g + 1)
                for i in range(2):
                    src = bank[4 + i][:, :].rearrange("p (t c) -> p t c", t=HT)
                    for q in range(4):
                        last = act.activation(gc[32 * q:32 * q + 32, i * HT:(i + 1) * HT, g, :],
                                              src[32 * q:32 * q + 32, :, 32 * q:32 * q + 32], ACT.Copy)
                last.then_inc(g_ready, 1)

            for g in range(GROUPS + 1):
                for u in range(4):
                    if g < GROUPS:
                        bc_first_tap(g, u)
                    if (g, u) != (0, 0) and (g < GROUPS or u == 0):
                        bc_silu_of(g if u else g - 1, (u - 1) % 4)
                    if g < TT and u == 1:
                        act.wait_ge(huT_done, g + 1)
                        act.activation(huT[g % 2], bank[7][:, :], ACT.Copy).then_inc(huT_ready, 1)
                if g == 0:
                    exps(0)
                if g >= 1:
                    g_blocks(g - 1)
                if g < TT:
                    act.wait_ge(moe_done, g + 1)
                    act.activation(gff[:, g, :], bank[6][:, 0:EMB], ACT.Silu).then_inc(gff_ready, 1)

            def first_tap(c, n):
                act.wait_ge(hid_done, n + 1)
                if not isinstance(n, int) or n > 0:
                    act.wait_ge(hs_ready, n)
                act.activation(cv[0], bank[0][:, :], ACT.Identity, scale=conv_w[:, bass.ds(c, 1), TAPS - 1],
                               bias=conv_b[:, bass.ds(c, 1)]).then_inc(tap_done, 1)

            def silu_gate(n, s):
                act.wait_ge(gate_done, n + 1)
                act.activation(sg[s % 2], bank[1][:, :], ACT.Silu, scale=UNSCALE).then_inc(sg_ready, 1)

            def silu_hidden(n):
                act.wait_ge(conv_done, n + 1)
                act.activation(hs, cv[0], ACT.Silu).then_inc(hs_ready, 1)

            def place(n, q):
                act.wait_ge(m_ready, n + 1)
                if isinstance(n, int) and n == 0:
                    act.wait_ge(pool_const, 5)
                else:
                    act.wait_ge(y_done, 2 * n - 1)
                for r in range(4):
                    last = act.activation(mb[32 * r:32 * r + 32, q % 2, :, :, 32 * r:32 * r + 32],
                                          mc[32 * r:32 * r + 32, :, :, :], ACT.Copy)
                last.then_inc(mb_ready, 1)

            def square(n, s):
                act.wait_ge(yg_ready, n + 1)
                if not isinstance(n, int) or n > 1:
                    act.wait_ge(ssq_done, n)
                act.activation(sq[s % 2], yg[s % 2], ACT.Square).then_inc(sq_ready, 1)

            act.wait_ge(bc_silu, 4 * GROUPS - 1)
            first_tap(0, 0)
            silu_hidden(0)

            def body(half, j, last):
                for s in range(4):
                    c = 4 * j + s
                    n = c + half * CT
                    over = last and s == 3
                    more = not (over and half == 1)
                    pair = 2 * j + (s // 2) + half * (CT // 2)
                    build_next = not (last and s >= 2 and half == 1)
                    if more:
                        first_tap(0 if over else c + 1, n + 1)
                    if s % 2 == 0:
                        place(pair, s // 2)
                    silu_gate(n, s)
                    if not (isinstance(n, int) and n == 0):
                        square(n - 1, s + 1)
                    if more:
                        silu_hidden(n + 1)
                    if s % 2 == 0 and build_next:
                        exps(pair + 1)

            for half in range(2):
                body(half, 0, False)
                with act.Fori(1, NJ - 1) as j:
                    body(half, j, False)
                body(half, NJ - 1, True)
            square(2 * CT - 1, 3)

            act.wait_ge(ss_done, 1)
            act.activation(rstd[:, :], bank[0][:, 0:TT], ACT.Sqrt, scale=1.0 / INTER, bias=eps_rms[:, :]).then_inc(act_step, 1)
            w_hi(0)
            act.wait_ge(dve_step, 4)
            act.activation(sd[:, :], mv[:, :, 1], ACT.Sqrt, bias=eps_ln[:, :]).then_inc(act_step, 1)
            w_hi(1)
            x_hi(1)
            act.wait_ge(attn_in, 16 * 8)
            act.mul(q_lo[:, :], mix[:, 1:2], 0.25 * UNSCALE)
            act.mul(bq4[:, :], bq[:, :], 0.25).then_inc(act_step, 1)
            act.wait_ge(act_step, 10)
            act.mul(bq_lo[:, :], bq4[:, :], mix[:, 1:2]).then_inc(act_step, 1)
            act.wait_ge(act_step, 11)
            with act.Fori(0, 2) as hf:
                for gt in range(2):
                    b = u = 2 * hf + gt
                    for i in range(4):
                        act.wait_ge(qkv_done, 5 * b + i + 1)
                        for n in range(2):
                            c = 2 * (i % 2) + n
                            src = bank[i % 3][:, n * SEQ:(n + 1) * SEQ]
                            if i < 2:
                                act.activation(q16[:, c, :], src, ACT.Identity, scale=0.25 * UNSCALE, bias=bq4[:, c:c + 1])
                                last = act.activation(qk32[i % 2][:, n, :], src, ACT.Identity, scale=q_lo[:, :], bias=bq_lo[:, c:c + 1])
                            else:
                                last = act.activation(k16[:, 0, c, :], src, ACT.Identity, scale=UNSCALE, bias=bk[:, c:c + 1])
                        last.then_inc(qk_read, 1)
                    for m in range(4):
                        act.wait_ge(gate_up_done, 8 * u + m + 1)
                        act.activation(sgu[m], bank[(4, 5, 3, 2)[m]][:, :], ACT.Silu, scale=UNSCALE).then_inc(sgu_ready, 1)
                    def heads_out(i):
                        act.wait_ge(pv_done, b * AH + 8 * i + 8)
                        act.activation(oT[:, 2 * i:2 * i + 2, :].rearrange("p n q -> p (n q)"), bank[3 + i][:, :], ACT.Copy,
                                       scale=1.0 / P_SCALE)\
                            .then_inc(oT_ready, 1)

                    for h in range(AH + 3):
                        if h >= 3:
                            act.wait_ge(pT_done, b * AH + h - 2)
                            act.activation(pT[(h - 3) % 2][:, 0, :, :].rearrange("p k q -> p (k q)"), turn_bank(h - 3), ACT.Copy,
                                           scale=P_SCALE)\
                                .then_inc(pTh_ready, 1)
                        if h < AH:
                            act.wait_ge(mx_ready, b * AH + h + 1)
                            if h >= 2:
                                act.wait_ge(pn_ready, b * AH + h - 1)
                            for q in range(2):
                                last = act.activation(pr[h % 2][:, q, :], bank[h % 2][:, q * SEQ:(q + 1) * SEQ], ACT.Exp,
                                                      bias=nmx[:, h, q:q + 1], accum_out=den[:, q, h:h + 1])
                            last.then_inc(p_ready, 1)
                        if h == 11:
                            heads_out(0)
                        if h in (1, 2, 3, 4):
                            m = h - 1
                            act.wait_ge(hm_ready, 4 * u + m + 1)
                            act.activation(ha[:, m, :], hm[:, m, :], ACT.Abs).then_inc(ha_ready, 1)
                    heads_out(1)
                act.wait_ge(kept_used, 2 * hf + 2)
                for i in range(2):
                    act.activation(g1[i], bank[6 + i][:, :], ACT.Silu).then_inc(g1_ready, 1)

        @block.vector
        def _(dve):
            steps = [0]

            def link(ins):
                ins.then_inc(chain, 1)
                steps[0] += 1
                dve.wait_ge(chain, steps[0])

            dve.memset(eps_ln[:, :], LN_EPS)
            link(dve.memset(eps_rms[:, :], RMS_EPS))

            def ln_stats():
                for t in range(TT):
                    link_last = dve.bn_stats(stats[:, t, :], x[:, t, :])
                link(link_last)
                for t in range(TT):
                    link_last = dve.bn_aggr(mv[:, t, :], stats[:, t, :])
                link_last.then_inc(dve_step, 1)

            def lo_part(slot, raw_slot, w):
                dve.wait_ge(wh_ready, w + 1)
                dve.scalar_tensor_tensor(wt16[:, slot, 1, :, :, :].rearrange("p a k c -> p (a k c)"),
                                         wring[:, raw_slot, :, :, :].rearrange("p a k c -> p (a k c)"), W_SCALE,
                                         wt16[:, slot, 0, :, :, :].rearrange("p a k c -> p (a k c)"),
                                         ALU.mult, ALU.subtract).then_inc(wl_ready, 1)

            def split(hi, lo, raw):
                link(dve.tensor_scalar(hi, raw, W_SCALE, None, ALU.mult))
                return dve.scalar_tensor_tensor(lo, raw, W_SCALE, hi, ALU.mult, ALU.subtract)

            def x_lo(n):
                for i, (half, k) in enumerate(((0, 0), (0, 1), (1, 0), (1, 1))):
                    dve.wait_ge(xh_ready, 4 * n + i + 1)
                    d = (slice(None), k, slice(half * HALF, (half + 1) * HALF))
                    dve.scalar_tensor_tensor(x16[1][d], bank[2 * k + half][:, :], X_SCALE, x16[0][d], ALU.mult, ALU.subtract)\
                        .then_inc(x16_ready, 1)

            def ff_lo(a):
                dve.wait_ge(ff_hi, a + 1)
                hi, lo = [wgu16[:, i, a, :, :, :, :].rearrange("p k m g c -> p (k m g c)") for i in range(2)]
                dve.scalar_tensor_tensor(lo, w_gu[:, a * 2048:(a + 1) * 2048], W_SCALE, hi, ALU.mult, ALU.subtract).then_inc(ff16, 1)

            def ln_apply():
                link(dve.reciprocal(rstd[:, :], sd[:, :]))
                for t in range(TT):
                    dve.tensor_scalar(xn[:, t, :], x[:, t, :], mv[:, t, 0:1], rstd[:, t:t + 1],
                                      ALU.subtract, ALU.mult).then_inc(ln_tile, 1)

            dve.wait_ge(x_in, 32)
            ln_stats()
            dve.wait_ge(act_step, 1)
            ln_apply()
            dve.wait_ge(const_in, 16 * 18)
            split(dtr16[:, 0, :, :], dtr16[:, 1, :, :], dtr).then_inc(early16, 1)
            link(dve.tensor_scalar(conv_w[:, :, :], conv_w[:, :, :], UNSCALE, None, ALU.mult))
            x_lo(0)
            dve.wait_ge(moe_in, 16 * 4)
            split(wu16[:, 0, :, :].rearrange("p k c -> p (k c)"), wu16[:, 1, :, :].rearrange("p k c -> p (k c)"), w_u)\
                .then_inc(early16, 1)
            lo_part(0, 0, 0)
            dve.wait_ge(dt_done, 1)
            dve.scalar_tensor_tensor(sp[0], bank[4][:, :].rearrange("p (t h) -> p t h", t=TT), UNSCALE,
                                     dt_bias[:, None, :].broadcast_to([P, TT, HEADS]), ALU.mult, ALU.add).then_inc(dve_step, 1)
            lo_part(1, 1, 1)
            dve.wait_ge(act_step, 3)
            dve.tensor_scalar(sp[2], sp[1], 1.0, None, ALU.add).then_inc(dve_step, 1)
            dve.wait_ge(dve_step, 3)
            link(dve.tensor_scalar(adt[:, :, :], sp[2], -1.0, 1e-30, ALU.add, ALU.max))
            link(dve.reciprocal(dts[:, :, :], adt[:, :, :]))
            link(dve.tensor_tensor(dts[:, :, :], dts[:, :, :], sp[1], ALU.mult))
            dve.wait_ge(act_step, 5)
            link(dve.tensor_tensor(dts[:, :, :], dts[:, :, :], decay[:, :, :], ALU.mult))
            link(dve.tensor_scalar(adt[:, :, :], sp[2], 1.0, None, ALU.is_equal))
            link(dve.tensor_tensor(adt[:, :, :], adt[:, :, :], sp[1], ALU.mult))
            link(dve.tensor_tensor(dts[:, :, :], dts[:, :, :], adt[:, :, :], ALU.add))
            link(dve.scalar_tensor_tensor(dts[:, :, :], sp[0], 0.0, dts[:, :, :], ALU.max, ALU.add))
            link(dve.tensor_scalar(a_row[:, :], a_row[:, :], -1.0, None, ALU.mult))
            dve.tensor_tensor(adt[:, :, :], dts[:, :, :], a_row[:, None, :].broadcast_to([P, TT, HEADS]),
                              ALU.mult).then_inc(adt_ready, 1)

            dve.wait_ge(sc_done, 1)
            link(dve.tensor_scalar(sc, bank[7][:, 0:TT * EXPERTS].rearrange("p (t s) -> p t s", t=TT), UNSCALE, None, ALU.mult))
            for t in range(TT):
                last = dve.max(top[:, t, :], sc[:, t, :])
            link(last)
            for t in range(TT):
                last = dve.max_index(topi[:, t, :], top[:, t, :], sc[:, t, :])
            link(last)
            dve.tensor_tensor(pe_, sc, top[:, :, 0:1].broadcast_to([P, TT, EXPERTS]), ALU.subtract)
            dve.wait_ge(moe_in, 16 * 4)
            link(dve.tensor_tensor(awt, attr, w_a[:, None, :].broadcast_to([P, EXPERTS, EXPERTS]), ALU.mult))
            link(dve.tensor_reduce(aw[:, :], awt, AX.X, ALU.add))
            link(dve.tensor_copy(topf[:, :, :], topi[:, :, :]))
            dve.tensor_copy(rsum[3][:, :], topf[:, :, 0]).then_inc(route_exp, 1)
            for i in range(2):
                last = dve.tensor_tensor(sel[i], expert_no[:, None, :].broadcast_to([P, TT, EXPERTS]),
                                         topf[:, :, i:i + 1].broadcast_to([P, TT, EXPERTS]), ALU.is_equal)
            link(last)
            link(dve.tensor_tensor(sel[0], sel[0], sel[1], ALU.add))
            dve.wait_ge(act_step, 7)
            link(dve.tensor_scalar(aw[:, :], aw[:, :], 1.0, None, ALU.add))
            link(dve.reciprocal(aw[:, :], aw[:, :]))
            link(dve.tensor_reduce(rsum[0][:, :], pe_, AX.X, ALU.add))
            link(dve.reciprocal(rsum[1][:, :], rsum[0][:, :]))
            link(dve.tensor_tensor(pe_, pe_, rsum[1][:, :, None].broadcast_to([P, TT, EXPERTS]), ALU.mult))
            link(dve.tensor_tensor(pe_, pe_, sel[0], ALU.mult))
            link(dve.tensor_reduce(rsum[0][:, :], pe_, AX.X, ALU.add))
            link(dve.tensor_scalar(rsum[0][:, :], rsum[0][:, :], 1e-8, None, ALU.add))
            link(dve.reciprocal(rsum[1][:, :], rsum[0][:, :]))
            link(dve.tensor_tensor(pe_, pe_, rsum[1][:, :, None].broadcast_to([P, TT, EXPERTS]), ALU.mult))
            link(dve.tensor_tensor(sel[1], pe_, aw[:, None, :].broadcast_to([P, TT, EXPERTS]), ALU.mult))
            link(dve.tensor_reduce(rsum[2][:, :], sel[1], AX.X, ALU.add))
            link(dve.tensor_scalar(rsum[2][:, :], rsum[2][:, :], 0.2, 0.9, ALU.mult, ALU.add))
            link(dve.tensor_scalar(rsum[2][:, :], rsum[2][:, :], UNSCALE, None, ALU.mult))
            link(dve.tensor_tensor(pe_, pe_, rsum[2][:, :, None].broadcast_to([P, TT, EXPERTS]), ALU.mult))
            def weigh_experts(t):
                dve.wait_ge(hu_done, t + 1)
                dve.tensor_tensor(hug[t % 2].rearrange("p (s r) -> p s r", s=EXPERTS),
                                  bank[6][:, :].rearrange("p (s r) -> p s r", s=EXPERTS),
                                  pe_[:, t, :, None].broadcast_to([P, EXPERTS, RANK]), ALU.mult).then_inc(hug_ready, 1)

            def conv(dst, src, w, last_sem):
                d = dst.rearrange("p (b t) -> p b t", b=2)
                s = src.rearrange("p (b t) -> p b t", b=2)
                for k in range(1, TAPS):
                    ins = dve.scalar_tensor_tensor(d[:, :, k:SEQ], s[:, :, 0:SEQ - k], w(TAPS - 1 - k),
                                                   d[:, :, k:SEQ], ALU.mult, ALU.add)
                    if k < TAPS - 1:
                        yield ins
                ins.then_inc(last_sem, 1)

            def attn_lo(i):
                dve.wait_ge(attn_hi, 2)
                if i < 4:
                    hi, lo = [wqk16[:, part, i // 2, i % 2, :] for part in range(2)]
                    raw = wqk[:, i // 2, i % 2, :]
                else:
                    hi, lo = [wv16[:, part, :, :] for part in range(2)]
                    raw = wv
                dve.scalar_tensor_tensor(lo, raw, W_SCALE, hi, ALU.mult, ALU.subtract).then_inc(attn16, 1)

            for g in range(GROUPS):
                for u in range(4):
                    if u == 3:
                        lo_part(g % 2, (g + 2) % 4, g + 2)
                    dve.wait_ge(bc_tap, 4 * g + u + 1)
                    tile = INTER // P + (u // 2) * GROUPS + g
                    for ins in conv(cv[u % 2], bank[u][:, :], lambda k: conv_w[:, tile, k:k + 1], bc_conv):
                        link(ins)
                    if u == 0:
                        weigh_experts(g)
                    if u == 3 and g >= 3:
                        attn_lo(g - 3)

            def transposed(n, s):
                dve.wait_ge(t_done, n + 1)
                dve.tensor_copy(hT[s % 2], bank[2][:, :].rearrange("p (t c) -> p t c", t=HT)).then_inc(hT_ready, 1)

            def hidden_conv(c, n, beside=None):
                dve.wait_ge(tap_done, n + 1)
                k = 0
                for ins in conv(cv[0], bank[0][:, :], lambda k: conv_w[:, bass.ds(c, 1), k], conv_done):
                    k += 1
                    ins.then_inc(conv_step, 1)
                    if k == 1 and beside:
                        beside()
                    dve.wait_ge(conv_step, 2 * n + k)

            def gated(n, s):
                dve.wait_ge(y_done, n + 1)
                dve.wait_ge(sg_ready, n + 1)
                dve.tensor_tensor(yg[s % 2], bank[3][:, :], sg[s % 2], ALU.mult).then_inc(yg_ready, 1)

            def m_sum(n):
                dve.wait_ge(e2d_ready, n + 1)
                dve.wait_ge(m_ready, n)
                dve.tensor_tensor(ms, e1, e2, ALU.add).then_inc(m_add, 1)

            def m_times_g(n, q, half):
                dve.wait_ge(m_add, n + 1)
                if isinstance(n, int) and n == 0:
                    dve.wait_ge(g_ready, GROUPS)
                g0 = 4 * (q % 2)
                dve.tensor_tensor(ms, ms, gc[:, half * HT:(half + 1) * HT, g0:g0 + 4, :], ALU.mult).then_inc(m_g, 1)

            hidden_conv(0, 0)
            m_sum(0)
            m_times_g(0, 0, 0)

            def keep_sums(half):
                dve.wait_ge(gff_ready, TT)
                dve.wait_ge(out_done, (half + 1) * CT)
                for i in range(2):
                    t0 = half * HT + 2 * i
                    dve.tensor_tensor(s0[:, t0:t0 + 2, :], bank[6 + i][:, :].rearrange("p (t e) -> p t e", t=2),
                                      gff[:, t0:t0 + 2, :], ALU.mult).then_inc(s0_ready, 1)

            def body(half, j, last):
                for s in range(4):
                    c = 4 * j + s
                    n = c + half * CT
                    over = last and s == 3
                    split_next = not (last and s >= 2 and half == 1)
                    if split_next and s % 2 == 1:
                        lo_part(s % 2, (s + 2) % 4, n + 2 + GROUPS)
                    transposed(n, s)
                    next_m = 2 * j + s // 2 + 1 + half * (CT // 2)
                    build_next = s % 2 == 1 and not (last and s == 3 and half == 1)
                    if not (over and half == 1):
                        hidden_conv(0 if over else c + 1, n + 1, (lambda: m_sum(next_m)) if build_next else None)
                    if build_next:
                        m_times_g(next_m, s // 2 + 1, half + 1 if over else half)
                    if split_next and s % 2 == 0:
                        lo_part(s % 2, (s + 2) % 4, n + 2 + GROUPS)
                    gated(n, s)
                    if half == 1 and isinstance(j, int) and c == 0:
                        keep_sums(0)

            for half in range(2):
                body(half, 0, False)
                with dve.Fori(1, NJ - 1) as j:
                    body(half, j, False)
                body(half, NJ - 1, True)
            keep_sums(1)

            dve.wait_ge(act_step, 8)
            link(dve.reciprocal(rstd[:, :], rstd[:, :]))
            dve.wait_ge(s0_ready, 4)
            for t in range(TT):
                last = dve.scalar_tensor_tensor(x[:, t, :], s0[:, t, :], rstd[:, t:t + 1], x[:, t, :], ALU.mult, ALU.add)
            link(last)
            ln_stats()
            dve.wait_ge(act_step, 9)
            ln_apply()
            x_lo(1)
            ff_lo(0)
            ff_lo(1)
            dve.memset(nmx, 0.0).then_inc(s1_ready, 1)
            dve.wait_ge(down_in, 16)
            pairs = [(0, 1), (0, 2), (1, 2), (0, 3), (1, 3), (2, 3)]
            keep = ((2.0, ALU.is_ge), (1.0, ALU.is_ge), (0.0, ALU.is_ge), (1.0, ALU.is_le))
            with dve.Fori(0, 2) as hf:
                for gt in range(2):
                    b = u = 2 * hf + gt
                    for i in range(4):
                        n = 2 * (i % 2)
                        dve.wait_ge(qk_read, 4 * b + i + 1)
                        if i >= 2:
                            dve.wait_ge(qk_ready, 4 * b + i - 1)
                            for m in range(2):
                                last = dve.tensor_scalar(qk32[i % 2][:, m, :], bank[i % 3][:, m * SEQ:(m + 1) * SEQ], UNSCALE,
                                                         bk[:, n + m:n + m + 1], ALU.mult, ALU.add)
                            last.then_inc(k32_ready, 1)
                            dve.wait_ge(k32_ready, 2 * b + i - 1)
                        if i < 2:
                            d = q16[:, n:n + 2, :]
                            ins = dve.scalar_tensor_tensor(d, d, mix[:, 0:1], qk32[i % 2], ALU.mult, ALU.add)
                        else:
                            ins = dve.tensor_tensor(k16[:, 1, n:n + 2, :], qk32[i % 2], k16[:, 0, n:n + 2, :], ALU.subtract)
                        ins.then_inc(qk_ready, 1)
                    def feed_forward(h):
                        for m, at_h in enumerate((0, 0, 2, 3)):
                            if h == at_h:
                                dve.wait_ge(gate_up_done, 8 * u + m + 5)
                                dve.scalar_tensor_tensor(hm[:, m, :], bank[4 + m % 2][:, :], UNSCALE, sgu[m], ALU.mult, ALU.mult)\
                                    .then_inc(hm_ready, 1)
                        for i in range(6):
                            if h == (4, 5, 6, 8, 10, 11)[i]:
                                dve.wait_ge(ha_ready, 4 * u + pairs[i][1] + 1)
                                dve.tensor_tensor(beats[i], ha[:, pairs[i][0], :], ha[:, pairs[i][1], :], ALU.is_ge).then_inc(cmp_done, 1)
                        for m, at_h in enumerate((13, 14, 15, 16)):
                            if h == at_h:
                                dve.wait_ge(wins_ready, 4 * u + m + 1)
                                dve.scalar_tensor_tensor(hk[:, m, :], win[m], keep[m][0], hm[:, m, :], keep[m][1], ALU.mult)\
                                    .then_inc(hk_ready, 1)

                    for h in range(AH + 3):
                        if 1 <= h <= AH:
                            dve.wait_ge(p_ready, b * AH + h)
                            dve.reciprocal(rden[:, :, h - 1], den[:, :, h - 1]).then_inc(rden_ready, 1)
                        if h < AH:
                            dve.wait_ge(s_done, b * AH + h + 1)
                            dve.tensor_reduce(nmx[:, h, :], bank[h % 2][:, :].rearrange("p (q k) -> p q k", q=2),
                                              AX.X, ALU.max, negate=True).then_inc(mx_ready, 1)
                        if h >= 3:
                            dve.wait_ge(pTh_ready, b * AH + h - 2)
                            hi, lo = [pT[(h - 3) % 2][:, i, :, :].rearrange("p k q -> p (k q)") for i in range(2)]
                            dve.scalar_tensor_tensor(lo, turn_bank(h - 3), P_SCALE, hi, ALU.mult, ALU.subtract).then_inc(pT_ready, 1)
                        if h == 0:
                            dve.wait_ge(qkv_done, 5 * b + 5)
                            dve.scalar_tensor_tensor(v32.rearrange("p k h d -> p k (h d)"), bank[1][:, :].rearrange("p (k e) -> p k e", k=2),
                                                     UNSCALE, bv[:, None, :].broadcast_to([P, 2, EMB]), ALU.mult, ALU.add).then_inc(v_step, 1)
                            dve.wait_ge(v_step, 2 * b + 1)
                            dve.tensor_copy(v16[:, :, :, 0, :], v32).then_inc(v_step, 1)
                            dve.wait_ge(v_step, 2 * b + 2)
                            dve.tensor_tensor(v16[:, :, :, 1, :], v32, v16[:, :, :, 0, :], ALU.subtract).then_inc(v_ready, 1)
                        feed_forward(h)
                    dve.wait_ge(wo_done, b + 1)
                    dve.tensor_tensor(s1[:, bass.ds(hf * HT + 2 * gt, 2), :], bank[3][:, :].rearrange("p (q e) -> p q e", q=2),
                                      bo[:, None, :].broadcast_to([P, 2, EMB]), ALU.add).then_inc(s1_ready, 1)
                for i in range(2):
                    dve.wait_ge(g1_ready, 2 * hf + i + 1)
                    dve.wait_ge(s1_ready, 2 * hf + 3)
                    s = s1[:, bass.ds(hf * HT + 2 * i, 2), :]
                    dve.tensor_tensor(s, s, g1[i].rearrange("p (t e) -> p t e", t=2), ALU.mult).then_inc(fin_step, 1)
                    dve.wait_ge(fin_step, 2 * hf + i + 1)
                    dve.tensor_tensor(s, s, x[:, bass.ds(hf * HT + 2 * i, 2), :], ALU.add).then_inc(y_ready, 1)

        @block.tensor
        def _(pe):
            def ln_transposes(n):
                for t in range(TT):
                    pe.wait_ge(ln_tile, n * TT + t + 1)
                    for k in range(KE):
                        last = pe.transpose(bank[2 * k + t // HT][:, (t % HT) * P:(t % HT + 1) * P],
                                            xn[:, t, k * P:(k + 1) * P], ident[:, :])
                    if t % HT == HT - 1:
                        last.then_inc(xT_done, 1)

            pe.wait_ge(const_in, 16 * 18)
            ln_transposes(0)
            def product(dst, left, right):
                for k in range(KE):
                    for i, (a, b) in enumerate(((0, 0), (0, 1), (1, 0))):
                        last = pe.matmul(dst, left(a, k), right(b, k), start=(k == 0 and i == 0), stop=(k == KE - 1 and i == 2))
                return last

            def x_cols(c0, n):
                return lambda i, k: x16[i][:, k, c0:c0 + n] if isinstance(c0, int) else x16[i][:, k, bass.ds(c0, n)]

            pe.wait_ge(x16_ready, 4)
            pe.wait_ge(early16, 1)
            for t in range(TT):
                last = product(bank[4][:, t * HEADS:(t + 1) * HEADS], x_cols(t * P, P), lambda i, k: dtr16[:, i, k, 0:HEADS])
            last.then_inc(dt_done, 1)
            for t in range(TT):
                last = product(bank[7][:, t * EXPERTS:(t + 1) * EXPERTS], x_cols(t * P, P),
                               lambda i, k: dtr16[:, i, k, HEADS:HEADS + EXPERTS])
            last.then_inc(sc_done, 1)

            def segments(n):
                pe.wait_ge(r1_ready, n + 1)
                if not isinstance(n, int) or n > 0:
                    pe.wait_ge(exp_done, n)
                r = [r1[:, part, :, :, :].rearrange("p t h i -> p (t h i)") for part in range(3)]
                for part in range(3):
                    pe.matmul(bank[4][:, :], later_b[:, :], r[part], start=(part == 0), stop=False)
                pe.matmul(bank[4][:, :].rearrange("p (a i) -> p a i", i=CS), ident_b[:, :],
                          future[:, None, :].broadcast_to([P, 16, CS]), start=False, stop=True)
                for part in range(3):
                    last = pe.matmul(bank[5][:, :], chunk[:, :], r[part], start=(part == 0), stop=(part == 2))
                last.then_inc(seg_done, 1)

            def expert_up(t):
                if t >= 1:
                    pe.wait_ge(gff_ready, t)
                product(bank[6][:, :], x_cols(t * P, P), lambda i, k: wu16[:, i, k, :]).then_inc(hu_done, 1)

            def expert_turn(t):
                pe.wait_ge(hug_ready, t + 1)
                for c in range(4):
                    last = pe.transpose(bank[7][:, c * P:(c + 1) * P], hug[t % 2][:, c * P:(c + 1) * P], ident[:, :])
                last.then_inc(huT_done, 1)

            def expert_down(t):
                pe.wait_ge(huT_ready, t + 1)
                for c in range(4):
                    last = pe.matmul(bank[6][:, 0:EMB], huT[t % 2][:, c * P:(c + 1) * P], w_v[:, c, :],
                                     start=(c == 0), stop=(c == 3))
                last.then_inc(moe_done, 1)

            def bc_project(g, u):
                pe.wait_ge(wl_ready, g + 1)
                if g >= 1:
                    pe.wait_ge(bc_conv, 4 * g + u - 3)
                product(bank[u][:, :], lambda i, k: wt16[:, g % 2, i, u // 2, k, :], x_cols((u % 2) * HALF, HALF)).then_inc(bcp_done, 1)

            def g_product(g):
                pe.wait_ge(bc_silu, 4 * g + 4)
                pe.wait_ge(g_ready, g)
                if g == 0:
                    pe.wait_ge(exp_done, 1)
                for t in range(TT):
                    last = pe.matmul(bank[4 + t // HT][:, (t % HT) * P:(t % HT + 1) * P], bt[g % 2][:, t * P:(t + 1) * P],
                                     ct[g % 2][:, t * P:(t + 1) * P], start=True, stop=True)
                last.then_inc(g_done, 1)

            def project(i, s, half, done):
                product(bank[i][:, :], lambda part, k: wt16[:, s % 2, part, i, k, :], x_cols(half * HALF, HALF)).then_inc(done, 1)

            for g in range(GROUPS + 1):
                if g == GROUPS:
                    pe.wait_ge(wl_ready, GROUPS + 1)
                    pe.wait_ge(bc_conv, 4 * GROUPS - 2)
                    project(0, 0, 0, hid_done)
                    project(1, 0, 0, gate_done)
                if g == 0:
                    for i in range(4):
                        bc_project(0, i)
                    pe.wait_ge(adt_ready, 1)
                    pe.matmul(bank[5][:, :], later[:, :], adt[:, :, :].rearrange("p t h -> p (t h)"), start=True, stop=True)\
                        .then_inc(suffix_done, 1)
                    pe.wait_ge(early16, 2)
                    expert_up(0)
                    expert_turn(0)
                elif g < GROUPS:
                    bc_project(g, 0)
                    expert_up(g)
                    bc_project(g, 1)
                    bc_project(g, 2)
                    expert_turn(g)
                    bc_project(g, 3)
                if g == 0:
                    pe.wait_ge(decay_ready, 1)
                    segments(0)
                if g >= 1:
                    g_product(g - 1)
                if g < TT:
                    expert_down(g)

            pe.wait_ge(g_ready, GROUPS)

            def zero_sums():
                for i in range(2):
                    pe.matmul(bank[6 + i][:, :].rearrange("p (a i) -> p a i", i=CS), ident_b[:, :],
                              zeros[:, None, :].broadcast_to([P, 16, CS]), start=True, stop=False, skip_group_check=True)

            def body(half, j, last_body):
                for s in range(4):
                    c = 4 * j + s
                    n = c + half * CT
                    over = last_body and s == 3
                    more = not (over and half == 1)
                    pair = 2 * j + s // 2 + half * (CT // 2)
                    if more:
                        pe.wait_ge(wl_ready, n + 2 + GROUPS)
                        pe.wait_ge(conv_done, n + 1)
                        project(0, s + 1, half + 1 if over else half, hid_done)
                    pe.wait_ge(hs_ready, n + 1)
                    for t in range(HT):
                        last = pe.transpose(bank[2][:, t * P:(t + 1) * P], hs[:, t * P:(t + 1) * P], ident[:, :])
                    last.then_inc(t_done, 1)
                    if s % 2 == 0 and not (last_body and s == 2 and half == 1):
                        segments(pair + 1)
                    if isinstance(j, int) and c == 0:
                        if half == 1:
                            project_out(CT - 1, n - 1, 3)
                    else:
                        if isinstance(j, int) and c == 1:
                            if half == 1:
                                pe.wait_ge(s0_ready, 2)
                            zero_sums()
                        project_out(c - 1, n - 1, s - 1)
                    pe.wait_ge(hT_ready, n + 1)
                    pe.wait_ge(mb_ready, pair + 1)
                    for t in range(HT):
                        for h in range(2):
                            last = pe.matmul(bank[3][HD * h:HD * h + HD, t * P:(t + 1) * P], hT[s % 2][:, t, HD * h:HD * h + HD],
                                             mb[:, s // 2, t, 2 * (s % 2) + h, :], start=True, stop=True, skip_group_check=True)
                    last.then_inc(y_done, 1)
                    if more:
                        pe.wait_ge(sg_ready, n + 1)
                        project(1, s + 1, half + 1 if over else half, gate_done)

            def project_out(c, n, s):
                pe.wait_ge(yg_ready, n + 1)
                w = w_out[:, bass.ds(c, 1), :].rearrange("p a e -> p (a e)")
                for t in range(HT):
                    last = pe.matmul(bank[6 + t // 2][:, (t % 2) * EMB:(t % 2 + 1) * EMB], yg[s % 2][:, t * P:(t + 1) * P],
                                     w, start=False, stop=False, skip_group_check=True)
                last.then_inc(out_done, 1)

            pe.wait_ge(pool_const, 9)
            for half in range(2):
                body(half, 0, False)
                with pe.Fori(1, NJ - 1) as j:
                    body(half, j, False)
                body(half, NJ - 1, True)
            project_out(CT - 1, 2 * CT - 1, 3)
            pe.wait_ge(ssq_done, 2 * CT + 1)
            for t in range(TT):
                last = pe.matmul(bank[0][:, t:t + 1], ssq[:, t // HT, (t % HT) * P:(t % HT + 1) * P], ones[:, 0:1],
                                 start=True, stop=True)
            last.then_inc(ss_done, 1)

            pe.wait_ge(act_step, 8)
            ln_transposes(1)
            pe.wait_ge(x16_ready, 6)
            pe.wait_ge(attn16, 5)
            with pe.Fori(0, 2) as hf:
                zero_sums()
                for gt in range(2):
                    b = u = 2 * hf + gt
                    x0 = hf * HALF + gt * SEQ

                    def gate(m):
                        product(bank[(4, 5, 3, 2)[m]][:, :], lambda i, k: wgu16[:, i, 0, k, m, gt, :], x_cols(hf * HALF, HALF))\
                            .then_inc(gate_up_done, 1)

                    def up(m):
                        if m < 2:
                            pe.wait_ge(sgu_ready, 4 * u + m + 1)
                        else:
                            pe.wait_ge(hm_ready, 4 * u + m - 1)
                        product(bank[4 + m % 2][:, :], lambda i, k: wgu16[:, i, 1, k, m, gt, :], x_cols(hf * HALF, HALF))\
                            .then_inc(gate_up_done, 1)

                    def down(m):
                        pe.wait_ge(hk_ready, 4 * u + m + 1)
                        for t in range(HT):
                            last = pe.matmul(bank[6 + t // 2][:, (t % 2) * EMB:(t % 2 + 1) * EMB], hk[:, m, t * P:(t + 1) * P],
                                             w_down[:, m, gt, :], start=False, stop=False, skip_group_check=True)
                        if m == 3:
                            last.then_inc(kept_used, 1)

                    def scores(h):
                        r, n = h % 4, h // 4
                        if h >= 2:
                            pe.wait_ge(p_ready, b * AH + h - 1)
                        for q in range(2):
                            for i in range(2):
                                last = pe.matmul(bank[h % 2][:, q * SEQ:(q + 1) * SEQ], q16[32 * r:32 * r + 32, n, q * P:(q + 1) * P],
                                                 k16[32 * r:32 * r + 32, i, n, :], start=(i == 0), stop=(i == 1),
                                                 tile_position=(32 * r, 0))
                        last.then_inc(s_done, 1)

                    def turn(h):
                        pe.wait_ge(pn_ready, b * AH + h + 1)
                        if h == 3:
                            pe.wait_ge(hm_ready, 4 * u + 4)
                        elif h >= 1:
                            pe.wait_ge(pT_ready, b * AH + (h if h < 3 else h - 1))
                        for k in range(2):
                            for q in range(2):
                                last = pe.transpose(turn_bank(h)[:, (2 * k + q) * P:(2 * k + q + 1) * P],
                                                    pn[h % 2][:, q, k * P:(k + 1) * P], ident[:, :])
                        last.then_inc(pT_done, 1)

                    def weigh(h):
                        r, n = h % 4, h // 4
                        if h == 8:
                            pe.wait_ge(hm_ready, 4 * u + 4)
                        pe.wait_ge(pT_ready, b * AH + h + 1)
                        for i in range(2):
                            for k in range(2):
                                last = pe.matmul(bank[3 + n // 2][32 * r:32 * r + 32, (n % 2) * SEQ:(n % 2 + 1) * SEQ],
                                                 v16[:, k, h, :, :].rearrange("p s d -> p (s d)"), pT[h % 2][:, i, k, :],
                                                 start=(i == 0 and k == 0), stop=(i == 1 and k == 1), skip_group_check=True)
                        last.then_inc(pv_done, 1)

                    for i in range(4):
                        if i == 1:
                            pe.wait_ge(x16_ready, 8)
                        if i == 3:
                            pe.wait_ge(qk_read, 4 * b + 1)
                        for n in range(2):
                            c0 = (2 * (i % 2) + n) * P
                            last = product(bank[i % 3][:, n * SEQ:(n + 1) * SEQ],
                                           lambda part, k: wqk16[:, part, i // 2, k, c0:c0 + P], x_cols(x0, SEQ))
                        last.then_inc(qkv_done, 1)
                    def project_heads(n):
                        if n % 2 == 0:
                            pe.wait_ge(oT_ready, 2 * b + n // 2 + 1)
                        for q in range(2):
                            last = pe.matmul(bank[3][:, q * EMB:(q + 1) * EMB], oT[:, n, q * P:(q + 1) * P], wo[:, n, :],
                                             start=(n == 0 and q == 0), stop=(n == 3), skip_group_check=True)
                        if n == 3:
                            last.then_inc(wo_done, 1)

                    pe.wait_ge(ff16, 1)
                    gate(0)
                    gate(1)
                    pe.wait_ge(s1_ready, b + 1)
                    gate(2)
                    pe.wait_ge(qk_ready, 4 * b + 4)
                    gate(3)
                    scores(0)
                    pe.wait_ge(qk_read, 4 * b + 2)
                    for i in range(2):
                        last = product(bank[1][:, i * EMB:(i + 1) * EMB], x_cols(x0 + i * P, P), lambda part, k: wv16[:, part, k, :])
                    last.then_inc(qkv_done, 1)
                    pe.wait_ge(ff16, 2)
                    up(0)
                    up(1)
                    pe.wait_ge(v_ready, b + 1)
                    for i in range(AH + 3):
                        if i + 1 < AH:
                            scores(i + 1)
                        if i < 2:
                            up(i + 2)
                        if i == 2:
                            pe.wait_ge(sgu_ready, 4 * u + 4)
                        if 2 <= i <= AH + 1:
                            turn(i - 2)
                        if i >= 3:
                            weigh(i - 3)
                        if i in (12, 13):
                            project_heads(i - 12)
                        if i >= 15:
                            down(i - 15)
                    project_heads(2)
                    project_heads(3)
                pe.wait_ge(g1_ready, 2 * hf + 2)


_F32_INS = {
    "x": (TOK, EMB), "w_in": (EMB, PROJ), "w_out": (INTER, EMB), "conv_w": (P, CONV_T, TAPS), "conv_b": (P, CONV_T),
    "norm_w": (P, CT), "dt_bias": (1, HEADS), "a_log": (1, HEADS), "d": (1, HEADS), "w_router": (EMB, EXPERTS),
    "w_a": (1, EXPERTS), "attr": (1, EXPERTS * EXPERTS), "w_u": (EMB, EXPERTS * RANK), "w_v": (EXPERTS * RANK, EMB),
    "wq": (EMB, 2 * EMB), "wk": (EMB, 2 * EMB), "wv": (EMB, EMB), "wo": (P, 4, EMB), "bq": (P, 4), "bk": (P, 4),
    "bv": (1, EMB), "bo": (1, EMB), "w_gate": (EMB, FF), "w_up": (EMB, FF), "w_down": (FF, EMB),
}

_CONST_INS = {"ident": (P, P), "later": (P, P), "diag": (P, CS), "expert_no": (P, EXPERTS), "mix": (P, 2)}
_BF16_INS = {"later_b": (P, P), "chunk": (P, P), "upto": (P, CS), "future": (P, CS), "ident_b": (P, P)}


def kernel(**inputs):
    import ml_dtypes
    import numpy as np
    import concourse.bacc as bacc
    from concourse.bass_utils import run_bass_kernel_spmd as run

    a = {k: np.asarray(v) for k, v in inputs.items()}
    m, f = "L0_attn_", "L0_ffn_"
    q, w = "L1_attn_", "L1_ffn_"

    def twice(w, axis):
        return np.repeat(np.expand_dims(w, axis + 1), 2, axis + 1)

    by_member = np.arange(FF).reshape(FF // 4, 4).T.reshape(-1)
    data = {
        "x": a[m + "input_states"].reshape(TOK, EMB),
        "w_in": a[m + "in_proj_w"].T,
        "w_out": a[m + "out_proj_w"].T,
        "conv_w": a[m + "conv_w"].reshape(CONV_T, P, TAPS).transpose(1, 0, 2),
        "conv_b": a[m + "conv_b"].reshape(CONV_T, P).T,
        "norm_w": a[m + "norm_w"].reshape(CT, P).T,
        "dt_bias": a[m + "dt_bias"].reshape(1, HEADS),
        "a_log": a[m + "A_log"].reshape(1, HEADS),
        "d": a[m + "D"].reshape(1, HEADS),
        "w_router": a[f + "Wr"].T,
        "w_a": a[f + "Wa"],
        "attr": a[f + "attr"].reshape(1, EXPERTS * EXPERTS),
        "w_u": a[f + "U"].transpose(1, 0, 2).reshape(EMB, EXPERTS * RANK),
        "w_v": a[f + "V"].reshape(EXPERTS * RANK, EMB),
        "wq": twice(a[q + "Wq"].T.reshape(EMB, AH, AD), 1), "wk": twice(a[q + "Wk"].T.reshape(EMB, AH, AD), 1),
        "wv": a[q + "Wv"].T, "wo": twice(a[q + "Wo"].T.reshape(4, 4, AD, EMB), 1).transpose(1, 2, 3, 0, 4),
        "bq": twice(a[q + "bq"].reshape(4, 4, AD), 1).transpose(1, 2, 3, 0),
        "bk": twice(a[q + "bk"].reshape(4, 4, AD), 1).transpose(1, 2, 3, 0),
        "bv": a[q + "bv"].reshape(1, EMB), "bo": a[q + "bo"].reshape(1, EMB),
        "w_gate": a[w + "w_gate"][:, by_member], "w_up": a[w + "w_up"][:, by_member],
        "w_down": a[w + "w_down"][by_member, :],
    }
    k, j = np.arange(P)[:, None], np.arange(P)[None, :]
    same, i = k // CS == j // CS, np.arange(CS)[None, :]
    data["ident"] = (k == j).astype(np.float32)
    data["later"] = (same & (k > j)).astype(np.float32)
    data["later_b"] = (same & (k > j)).astype(ml_dtypes.bfloat16)
    data["chunk"] = same.astype(ml_dtypes.bfloat16)
    data["upto"] = (k % CS <= i).astype(ml_dtypes.bfloat16)
    data["diag"] = (k % CS == i).astype(np.float32)
    data["expert_no"] = np.broadcast_to(np.arange(EXPERTS, dtype=np.float32), (P, EXPERTS))
    first = np.arange(P) % (2 * AD) < AD
    data["mix"] = np.stack([np.where(first, 1.0, -1.0), np.where(first, 0.0, 1.0)], 1).astype(np.float32)
    data["future"] = np.where(i < k % CS, -30000.0, 0.0).astype(ml_dtypes.bfloat16)
    data["ident_b"] = (k == j).astype(ml_dtypes.bfloat16)

    nc = bacc.Bacc("TRN2", target_bir_lowering=False, num_devices=1)
    arrays, aps = {}, {}
    for name, shape in {**_F32_INS, **_CONST_INS, **_BF16_INS}.items():
        arrays[name + "_dram"] = np.ascontiguousarray(data[name]).reshape(shape)
        dt = BF16 if name in _BF16_INS else F32
        aps[name] = nc.dram_tensor(name + "_dram", shape, dt, kind="ExternalInput").ap()
    out = nc.dram_tensor("out_dram", (TOK, EMB), F32, kind="ExternalOutput").ap()
    build(nc, aps, out)
    r = run(nc, [arrays], core_ids=[0])
    return r.results[0]["out_dram"].reshape(BATCH, SEQ, EMB)
```
